# Optimizing a Trainium2 kernel written in Bass

```python
import numpy as np
import jax
import jax.numpy as jnp

def _softmax(x, axis=-1):
    return jax.nn.softmax(x, axis=axis)

def _gelu(x):
    return jax.nn.gelu(x, approximate=True)

def _silu(x):
    return jax.nn.silu(x)

def _sigmoid(x):
    return jax.nn.sigmoid(x)

def _layernorm(x, axis=-1, eps=1e-05):
    m = jnp.mean(x, axis=axis, keepdims=True)
    v = jnp.var(x, axis=axis, keepdims=True)
    return (x - m) / jnp.sqrt(v + eps)

def _scatter_add(tgt, idx, src, axis=0):
    return tgt.at[idx].add(src)

def _segment_sum(src, seg, n):
    return jax.ops.segment_sum(src, seg, n)
kernel_name = 'mk_macaron_d4_jaxref_r8_d36834'

def setup_inputs(seed: int=0):
    np.random.seed(seed)
    _w = jnp.asarray

    def _L0_attn_setup():
        import jax, jax.numpy as jnp
        import numpy as np
        B, T, H, S, F, G = (2, 256, 512, 128, 1248, 6)
        GRAD_ORDER_MIN = 4
        THD = 2.5
        key = jax.random.key(seed)
        ks = jax.random.split(key, 9)
        sc = 0.02
        hidden_states = jax.random.normal(ks[0], (B, T, H), jnp.float32)
        up_w = jax.random.normal(ks[1], (S, H), jnp.float32) * sc
        gate_w = jax.random.normal(ks[2], (S, H), jnp.float32) / np.sqrt(H)
        local_point = jax.random.normal(ks[3], (S,), jnp.float32)
        local_approx_output = jax.random.normal(ks[4], (H, S), jnp.float32) * sc
        fuse_weight = jax.random.normal(ks[5], (H, S, G), jnp.float32) * sc
        discount_factor = jnp.asarray(np.cumsum(np.log(np.arange(1, G + 1, dtype=np.float64))), jnp.float32)
        ffn_gate_w = jax.random.normal(ks[6], (F, H), jnp.float32) * sc
        ffn_up_w = jax.random.normal(ks[7], (F, H), jnp.float32) * sc
        ffn_down_w = jax.random.normal(ks[8], (H, F), jnp.float32) * sc
        return {'hidden_states': hidden_states, 'up_w': up_w, 'gate_w': gate_w, 'local_point': local_point, 'local_approx_output': local_approx_output, 'fuse_weight': fuse_weight, 'discount_factor': discount_factor, 'ffn_gate_w': ffn_gate_w, 'ffn_up_w': ffn_up_w, 'ffn_down_w': ffn_down_w}
    _L0_attn_in = _L0_attn_setup()

    def _L0_ffn_setup():
        import jax, jax.numpy as jnp
        import numpy as np
        BS = 128
        FP8_MAX = 448.0

        def act_quant(x):
            T, K = x.shape
            xb = x.reshape(T, K // BS, BS)
            amax = jnp.max(jnp.abs(xb), axis=-1)
            scale = amax / FP8_MAX + 1e-12
            xq = (xb / scale[:, :, None]).reshape(T, K)
            return (xq, scale)

        def linear_dsv3(x, wq, w_scale):
            T, K = x.shape
            N = wq.shape[0]
            xq, xs = act_quant(x)
            xdq = (xq.reshape(T, K // BS, BS) * xs[:, :, None]).reshape(T, K)
            wdq = (wq.reshape(N // BS, BS, K // BS, BS) * w_scale[:, None, :, None]).reshape(N, K)
            return xdq @ wdq.T
        key = jax.random.key(seed)
        ks = jax.random.split(key, 4)
        DIM, INTER = (512, 1792)

        def make_qweight(k, n, m):
            w = jax.random.normal(k, (n, m), dtype=jnp.float32) * 0.02
            wb = w.reshape(n // BS, BS, m // BS, BS)
            amax = jnp.max(jnp.abs(wb), axis=(1, 3))
            scale = amax / FP8_MAX + 1e-12
            wq = (wb / scale[:, None, :, None]).reshape(n, m)
            return (wq, scale)
        x = jax.random.normal(ks[0], (2, 128, DIM), dtype=jnp.float32)
        w1, w1_scale = make_qweight(ks[1], INTER, DIM)
        w3, w3_scale = make_qweight(ks[2], INTER, DIM)
        w2, w2_scale = make_qweight(ks[3], DIM, INTER)
        return {'x': x, 'w1': w1, 'w1_scale': w1_scale, 'w3': w3, 'w3_scale': w3_scale, 'w2': w2, 'w2_scale': w2_scale}
    _L0_ffn_in = _L0_ffn_setup()

    def _L1_attn_setup():
        import jax, jax.numpy as jnp
        import numpy as np
        import math
        B, L, D, H = (32, 64, 512, 32)
        HD = D // H
        key = jax.random.key(seed)
        ks = jax.random.split(key, 9)
        s = 1.0 / math.sqrt(D)
        return {'x': jax.random.normal(ks[0], (B, L, D), jnp.float32), 'Wq': jax.random.normal(ks[1], (D, D), jnp.float32) * s, 'bq': jax.random.normal(ks[2], (D,), jnp.float32) * s, 'Wk': jax.random.normal(ks[3], (D, D), jnp.float32) * s, 'bk': jax.random.normal(ks[4], (D,), jnp.float32) * s, 'Wv': jax.random.normal(ks[5], (D, D), jnp.float32) * s, 'bv': jax.random.normal(ks[6], (D,), jnp.float32) * s, 'Wo': jax.random.normal(ks[7], (D, D), jnp.float32) * s, 'bo': jax.random.normal(ks[8], (D,), jnp.float32) * s}
    _L1_attn_in = _L1_attn_setup()

    def _L1_ffn_setup():
        import jax, jax.numpy as jnp
        import numpy as np
        import math
        E, DK, R = (8, 32, 16)
        SCALING = 16.0 / 16.0
        key = jax.random.key(seed)
        ks = jax.random.split(key, 7)
        Bt, S, Din, Dout = (4, 256, 512, 512)
        x = jax.random.normal(ks[0], (Bt, S, Din), jnp.float32)
        W = jax.random.normal(ks[1], (Dout, Din), jnp.float32) * 0.02
        b = jnp.zeros((Dout,), jnp.float32)
        Wq = jax.random.normal(ks[2], (E * DK, Din), jnp.float32) * 0.02
        Wk = jax.random.normal(ks[3], (E * DK, Din), jnp.float32) * 0.02
        A = jax.random.normal(ks[4], (E, R, Din), jnp.float32) * 0.02
        Bm = jax.random.normal(ks[5], (E, Dout, R), jnp.float32) * 0.02
        return {'x': x, 'W': W, 'b': b, 'Wq': Wq, 'Wk': Wk, 'A': A, 'Bm': Bm}
    _L1_ffn_in = _L1_ffn_setup()

    def _L2_attn_setup():
        import jax, jax.numpy as jnp
        import numpy as np
        import math
        FACTOR = 1
        key = jax.random.key(seed)
        x = jax.random.normal(key, (8, 64, 512), dtype=jnp.float32)
        return {'x': x}
    _L2_attn_in = _L2_attn_setup()

    def _L2_ffn_setup():
        import jax, jax.numpy as jnp
        import numpy as np

        @jax.custom_vjp
        def ste_sign(w):
            return jnp.sign(w)

        def _ste_fwd(w):
            return (jnp.sign(w), w)

        def _ste_bwd(w, g):
            mask = ((w > -1) & (w < 1)).astype(g.dtype)
            return (g * mask,)
        ste_sign.defvjp(_ste_fwd, _ste_bwd)
        key = jax.random.key(seed)
        k = jax.random.split(key, 6)
        B, S, H, O, E = (4, 256, 512, 512, 8)
        return {'x': jax.random.normal(k[0], (B, S, H), dtype=jnp.float32), 'weight': jax.random.normal(k[1], (O, H), dtype=jnp.float32) * 0.02, 'bias': jax.random.normal(k[2], (O,), dtype=jnp.float32) * 0.02, 'gate_w': jax.random.normal(k[3], (E, H), dtype=jnp.float32) * 0.02, 'in_channel_scale': jax.random.normal(k[4], (E, H), dtype=jnp.float32), 'out_channel_scale': jax.random.normal(k[5], (E, O), dtype=jnp.float32)}
    _L2_ffn_in = _L2_ffn_setup()

    def _L3_attn_setup():
        import math
        import jax, jax.numpy as jnp
        import numpy as np
        NUM_HEADS = 32
        NUM_KV_HEADS = 8
        HEAD_DIM = 128
        HIDDEN = 512
        ROPE_THETA = 500000.0
        ROPE_FACTOR = 8.0
        HIGH_FF = 4.0
        LOW_FF = 1.0
        ORIG_MAX_POS = 1024

        def _llama3_inv_freq():
            inv = 1.0 / ROPE_THETA ** (np.arange(0, HEAD_DIM, 2, dtype=np.float32) / HEAD_DIM)
            wavelen = 2.0 * np.pi / inv
            low_wl = ORIG_MAX_POS / LOW_FF
            high_wl = ORIG_MAX_POS / HIGH_FF
            inv_scaled = np.where(wavelen > low_wl, inv / ROPE_FACTOR, inv)
            smooth = (ORIG_MAX_POS / wavelen - LOW_FF) / (HIGH_FF - LOW_FF)
            smoothed = (1.0 - smooth) / ROPE_FACTOR * inv + smooth * inv
            is_medium = (wavelen <= low_wl) & (wavelen >= high_wl)
            return jnp.asarray(np.where(is_medium, smoothed, inv_scaled), dtype=jnp.float32)

        def _rotate_half(x):
            h = x.shape[-1] // 2
            return jnp.concatenate([-x[..., h:], x[..., :h]], axis=-1)
        key = jax.random.key(seed)
        ks = jax.random.split(key, 5)
        s = 0.02
        return {'x': jax.random.normal(ks[0], (1, 256, HIDDEN), dtype=jnp.float32), 'Wq': jax.random.normal(ks[1], (NUM_HEADS * HEAD_DIM, HIDDEN), dtype=jnp.float32) * s, 'Wk': jax.random.normal(ks[2], (NUM_KV_HEADS * HEAD_DIM, HIDDEN), dtype=jnp.float32) * s, 'Wv': jax.random.normal(ks[3], (NUM_KV_HEADS * HEAD_DIM, HIDDEN), dtype=jnp.float32) * s, 'Wo': jax.random.normal(ks[4], (HIDDEN, NUM_HEADS * HEAD_DIM), dtype=jnp.float32) * s}
    _L3_attn_in = _L3_attn_setup()

    def _L3_ffn_setup():
        import jax, jax.numpy as jnp
        import numpy as np
        B, T, D_IN, D_OUT = (8, 256, 512, 512)
        N_LORAS, RANK = (16, 32)
        SCALING = 1.0
        key = jax.random.key(seed)
        ks = jax.random.split(key, 8)
        std = 1.0 / D_IN ** 0.5
        x = jax.random.normal(ks[0], (B, T, D_IN), dtype=jnp.float32)
        idx = jax.random.randint(ks[1], (B,), 0, N_LORAS)
        gate = jax.nn.one_hot(idx, N_LORAS, dtype=jnp.float32)
        kernel = jax.random.normal(ks[2], (D_IN, D_OUT), dtype=jnp.float32) * std
        bias = jnp.zeros((D_OUT,), dtype=jnp.float32)
        lora_A = jax.random.normal(ks[3], (N_LORAS, RANK, D_IN), dtype=jnp.float32) * std
        lora_B = jax.random.normal(ks[4], (N_LORAS, D_OUT, RANK), dtype=jnp.float32) * 0.01
        lora_A_shared = jax.random.normal(ks[5], (RANK, D_IN), dtype=jnp.float32) * std
        lora_B_shared = jax.random.normal(ks[6], (D_OUT, RANK), dtype=jnp.float32) * 0.01
        return {'x': x, 'gate': gate, 'kernel': kernel, 'bias': bias, 'lora_A': lora_A, 'lora_B': lora_B, 'lora_A_shared': lora_A_shared, 'lora_B_shared': lora_B_shared}
    _L3_ffn_in = _L3_ffn_setup()
    _d = {'L0_attn_hidden_states': _L0_attn_in['hidden_states'], 'L0_attn_up_w': _L0_attn_in['up_w'], 'L0_attn_gate_w': _L0_attn_in['gate_w'], 'L0_attn_local_point': _L0_attn_in['local_point'], 'L0_attn_local_approx_output': _L0_attn_in['local_approx_output'], 'L0_attn_fuse_weight': _L0_attn_in['fuse_weight'], 'L0_attn_discount_factor': _L0_attn_in['discount_factor'], 'L0_attn_ffn_gate_w': _L0_attn_in['ffn_gate_w'], 'L0_attn_ffn_up_w': _L0_attn_in['ffn_up_w'], 'L0_attn_ffn_down_w': _L0_attn_in['ffn_down_w'], 'L0_ffn_w1': _L0_ffn_in['w1'], 'L0_ffn_w1_scale': _L0_ffn_in['w1_scale'], 'L0_ffn_w3': _L0_ffn_in['w3'], 'L0_ffn_w3_scale': _L0_ffn_in['w3_scale'], 'L0_ffn_w2': _L0_ffn_in['w2'], 'L0_ffn_w2_scale': _L0_ffn_in['w2_scale'], 'L1_attn_Wq': _L1_attn_in['Wq'], 'L1_attn_bq': _L1_attn_in['bq'], 'L1_attn_Wk': _L1_attn_in['Wk'], 'L1_attn_bk': _L1_attn_in['bk'], 'L1_attn_Wv': _L1_attn_in['Wv'], 'L1_attn_bv': _L1_attn_in['bv'], 'L1_attn_Wo': _L1_attn_in['Wo'], 'L1_attn_bo': _L1_attn_in['bo'], 'L1_ffn_W': _L1_ffn_in['W'], 'L1_ffn_b': _L1_ffn_in['b'], 'L1_ffn_Wq': _L1_ffn_in['Wq'], 'L1_ffn_Wk': _L1_ffn_in['Wk'], 'L1_ffn_A': _L1_ffn_in['A'], 'L1_ffn_Bm': _L1_ffn_in['Bm'], 'L2_ffn_weight': _L2_ffn_in['weight'], 'L2_ffn_bias': _L2_ffn_in['bias'], 'L2_ffn_gate_w': _L2_ffn_in['gate_w'], 'L2_ffn_in_channel_scale': _L2_ffn_in['in_channel_scale'], 'L2_ffn_out_channel_scale': _L2_ffn_in['out_channel_scale'], 'L3_attn_Wq': _L3_attn_in['Wq'], 'L3_attn_Wk': _L3_attn_in['Wk'], 'L3_attn_Wv': _L3_attn_in['Wv'], 'L3_attn_Wo': _L3_attn_in['Wo'], 'L3_ffn_gate': _L3_ffn_in['gate'], 'L3_ffn_kernel': _L3_ffn_in['kernel'], 'L3_ffn_bias': _L3_ffn_in['bias'], 'L3_ffn_lora_A': _L3_ffn_in['lora_A'], 'L3_ffn_lora_B': _L3_ffn_in['lora_B'], 'L3_ffn_lora_A_shared': _L3_ffn_in['lora_A_shared'], 'L3_ffn_lora_B_shared': _L3_ffn_in['lora_B_shared']}
    _x0 = _d['L0_attn_hidden_states']
    _d['L0_attn_hidden_states'] = jax.random.normal(jax.random.fold_in(jax.random.key(seed), 1), (1, 1024, 512), dtype=_x0.dtype)
    del _x0
    return _d

def reference(L0_attn_hidden_states, L0_attn_up_w, L0_attn_gate_w, L0_attn_local_point, L0_attn_local_approx_output, L0_attn_fuse_weight, L0_attn_discount_factor, L0_attn_ffn_gate_w, L0_attn_ffn_up_w, L0_attn_ffn_down_w, L0_ffn_w1, L0_ffn_w1_scale, L0_ffn_w3, L0_ffn_w3_scale, L0_ffn_w2, L0_ffn_w2_scale, L1_attn_Wq, L1_attn_bq, L1_attn_Wk, L1_attn_bk, L1_attn_Wv, L1_attn_bv, L1_attn_Wo, L1_attn_bo, L1_ffn_W, L1_ffn_b, L1_ffn_Wq, L1_ffn_Wk, L1_ffn_A, L1_ffn_Bm, L2_ffn_weight, L2_ffn_bias, L2_ffn_gate_w, L2_ffn_in_channel_scale, L2_ffn_out_channel_scale, L3_attn_Wq, L3_attn_Wk, L3_attn_Wv, L3_attn_Wo, L3_ffn_gate, L3_ffn_kernel, L3_ffn_bias, L3_ffn_lora_A, L3_ffn_lora_B, L3_ffn_lora_A_shared, L3_ffn_lora_B_shared):

    def _L0_attn_ref(hidden_states, up_w, gate_w, local_point, local_approx_output, fuse_weight, discount_factor, ffn_gate_w, ffn_up_w, ffn_down_w):
        import jax, jax.numpy as jnp
        import numpy as np
        B, T, H, S, F, G = (2, 256, 512, 128, 1248, 6)
        GRAD_ORDER_MIN = 4
        THD = 2.5
        approx_up = hidden_states @ up_w.T
        gate_pre = hidden_states @ gate_w.T
        delta = gate_pre - local_point
        neg_factor = jnp.where(delta > 0, 1.0, -1.0).astype(hidden_states.dtype)
        delta_abs = jnp.abs(delta)
        log_delta = jnp.log(delta_abs)
        keep = (delta_abs <= THD).astype(hidden_states.dtype)
        approx_out = approx_up @ local_approx_output.T
        for idx in range(G):
            m = idx + 1
            dterm = jnp.exp(log_delta * m - discount_factor[idx])
            if m % 2 == 1:
                dterm = dterm * neg_factor
            tmp = dterm * approx_up
            if m > GRAD_ORDER_MIN:
                tmp = tmp * keep
            approx_out = approx_out + tmp @ fuse_weight[:, :, idx].T
        ffn_out = jax.nn.silu(hidden_states @ ffn_gate_w.T) * (hidden_states @ ffn_up_w.T) @ ffn_down_w.T
        return approx_out + ffn_out

    def _L0_ffn_ref(x, w1, w1_scale, w3, w3_scale, w2, w2_scale):
        import jax, jax.numpy as jnp
        import numpy as np
        BS = 128
        FP8_MAX = 448.0

        def act_quant(x):
            T, K = x.shape
            xb = x.reshape(T, K // BS, BS)
            amax = jnp.max(jnp.abs(xb), axis=-1)
            scale = amax / FP8_MAX + 1e-12
            xq = (xb / scale[:, :, None]).reshape(T, K)
            return (xq, scale)

        def linear_dsv3(x, wq, w_scale):
            T, K = x.shape
            N = wq.shape[0]
            xq, xs = act_quant(x)
            xdq = (xq.reshape(T, K // BS, BS) * xs[:, :, None]).reshape(T, K)
            wdq = (wq.reshape(N // BS, BS, K // BS, BS) * w_scale[:, None, :, None]).reshape(N, K)
            return xdq @ wdq.T
        B, S, D = x.shape
        xf = x.reshape(-1, D)
        g = linear_dsv3(xf, w1, w1_scale)
        u = linear_dsv3(xf, w3, w3_scale)
        h = jax.nn.silu(g) * u
        y = linear_dsv3(h, w2, w2_scale)
        return y.reshape(B, S, D)

    def _L1_attn_ref(x, Wq, bq, Wk, bk, Wv, bv, Wo, bo):
        import jax, jax.numpy as jnp
        import numpy as np
        import math
        B, L, D, H = (32, 64, 512, 32)
        HD = D // H
        b, l, d = x.shape
        h, hd = (H, HD)
        q = (x @ Wq.T + bq).reshape(b, l, h, hd).transpose(0, 2, 1, 3)
        k = (x @ Wk.T + bk).reshape(b, l, h, hd).transpose(0, 2, 1, 3)
        v = (x @ Wv.T + bv).reshape(b, l, h, hd).transpose(0, 2, 1, 3)
        scores = jnp.einsum('bhqd,bhkd->bhqk', q, k) / math.sqrt(hd)
        causal = jnp.tril(jnp.ones((l, l), bool))
        scores = jnp.where(causal, scores, -jnp.inf)
        att = jax.nn.softmax(scores, axis=-1)
        out = jnp.einsum('bhqk,bhkd->bhqd', att, v)
        out = out.transpose(0, 2, 1, 3).reshape(b, l, d)
        return out @ Wo.T + bo

    def _L1_ffn_ref(x, W, b, Wq, Wk, A, Bm):
        import jax, jax.numpy as jnp
        import numpy as np
        import math
        E, DK, R = (8, 32, 16)
        SCALING = 16.0 / 16.0
        Bt, S, Din = x.shape
        result = jnp.einsum('bsi,oi->bso', x, W) + b
        q = jnp.einsum('bsi,ni->bsn', x, Wq).reshape(Bt, S, E, DK)
        k = jnp.einsum('bsi,ni->bsn', x, Wk).reshape(Bt, S, E, DK)
        scores = jnp.einsum('bsed,bsed->bse', q, k) / math.sqrt(DK)
        w = jax.nn.softmax(scores, axis=-1)
        h = jnp.einsum('bsi,eri->bser', x, A)
        combined = jnp.einsum('bse,bser,eor->bso', w, h, Bm) * SCALING
        return result + combined

    def _L2_attn_ref(x):
        import jax, jax.numpy as jnp
        import numpy as np
        import math
        FACTOR = 1
        B, C, L = x.shape
        xh = x[:, None]
        f = jnp.fft.rfft(xh, axis=-1)
        corr = jnp.fft.irfft(f * jnp.conj(f), n=L, axis=-1)
        top_k = int(FACTOR * math.log(L))
        weights, delay = jax.lax.top_k(corr, top_k)
        tmp_corr = jax.nn.softmax(weights, axis=-1)
        init_index = jnp.arange(L)
        idx = (init_index[None, None, None, None, :] + delay[..., None]) % L
        pattern = jnp.take_along_axis(xh[:, :, :, None, :], idx, axis=-1)
        delays_agg = jnp.sum(pattern * tmp_corr[..., None], axis=-2)
        return delays_agg[:, 0]

    def _L2_ffn_ref(x, weight, bias, gate_w, in_channel_scale, out_channel_scale):
        import jax, jax.numpy as jnp
        import numpy as np

        @jax.custom_vjp
        def ste_sign(w):
            return jnp.sign(w)

        def _ste_fwd(w):
            return (jnp.sign(w), w)

        def _ste_bwd(w, g):
            mask = ((w > -1) & (w < 1)).astype(g.dtype)
            return (g * mask,)
        ste_sign.defvjp(_ste_fwd, _ste_bwd)
        B, S, H = x.shape
        xf = x.reshape(-1, H)
        router_logits = xf @ gate_w.T
        routing = jax.nn.softmax(router_logits.astype(jnp.float32), axis=1).astype(x.dtype)
        in_scale = routing @ in_channel_scale
        out_scale = routing @ out_channel_scale
        wb = ste_sign(weight)
        out = xf * in_scale @ wb.T * out_scale + bias
        return out.reshape(B, S, -1)

    def _L3_attn_ref(x, Wq, Wk, Wv, Wo):
        import math
        import jax, jax.numpy as jnp
        import numpy as np
        NUM_HEADS = 32
        NUM_KV_HEADS = 8
        HEAD_DIM = 128
        HIDDEN = 512
        ROPE_THETA = 500000.0
        ROPE_FACTOR = 8.0
        HIGH_FF = 4.0
        LOW_FF = 1.0
        ORIG_MAX_POS = 1024

        def _llama3_inv_freq():
            inv = 1.0 / ROPE_THETA ** (np.arange(0, HEAD_DIM, 2, dtype=np.float32) / HEAD_DIM)
            wavelen = 2.0 * np.pi / inv
            low_wl = ORIG_MAX_POS / LOW_FF
            high_wl = ORIG_MAX_POS / HIGH_FF
            inv_scaled = np.where(wavelen > low_wl, inv / ROPE_FACTOR, inv)
            smooth = (ORIG_MAX_POS / wavelen - LOW_FF) / (HIGH_FF - LOW_FF)
            smoothed = (1.0 - smooth) / ROPE_FACTOR * inv + smooth * inv
            is_medium = (wavelen <= low_wl) & (wavelen >= high_wl)
            return jnp.asarray(np.where(is_medium, smoothed, inv_scaled), dtype=jnp.float32)

        def _rotate_half(x):
            h = x.shape[-1] // 2
            return jnp.concatenate([-x[..., h:], x[..., :h]], axis=-1)
        B, T, _ = x.shape
        G = NUM_HEADS // NUM_KV_HEADS
        q = jnp.einsum('bth,oh->bto', x, Wq).reshape(B, T, NUM_HEADS, HEAD_DIM).transpose(0, 2, 1, 3)
        k = jnp.einsum('bth,oh->bto', x, Wk).reshape(B, T, NUM_KV_HEADS, HEAD_DIM).transpose(0, 2, 1, 3)
        v = jnp.einsum('bth,oh->bto', x, Wv).reshape(B, T, NUM_KV_HEADS, HEAD_DIM).transpose(0, 2, 1, 3)
        inv_freq = _llama3_inv_freq()
        pos = jnp.arange(T, dtype=jnp.float32)
        freqs = pos[:, None] * inv_freq[None, :]
        emb = jnp.concatenate([freqs, freqs], axis=-1)
        cos, sin = (jnp.cos(emb), jnp.sin(emb))
        q = q * cos + _rotate_half(q) * sin
        k = k * cos + _rotate_half(k) * sin
        qg = q.reshape(B, NUM_KV_HEADS, G, T, HEAD_DIM)
        scale = 1.0 / math.sqrt(HEAD_DIM)
        scores = jnp.einsum('bkgtd,bksd->bkgts', qg, k) * scale
        causal = jnp.tril(jnp.ones((T, T), dtype=bool))
        scores = jnp.where(causal, scores, -jnp.inf)
        attn = jax.nn.softmax(scores, axis=-1)
        out = jnp.einsum('bkgts,bksd->bkgtd', attn, v)
        out = out.reshape(B, NUM_HEADS, T, HEAD_DIM).transpose(0, 2, 1, 3).reshape(B, T, NUM_HEADS * HEAD_DIM)
        return jnp.einsum('bto,ho->bth', out, Wo)

    def _L3_ffn_ref(x, gate, kernel, bias, lora_A, lora_B, lora_A_shared, lora_B_shared):
        import jax, jax.numpy as jnp
        import numpy as np
        B, T, D_IN, D_OUT = (8, 256, 512, 512)
        N_LORAS, RANK = (16, 32)
        SCALING = 1.0
        base_out = jnp.matmul(x, kernel) + bias
        b = gate.shape[0]
        x_flat = x.reshape(b, -1, x.shape[-1])
        A_eff = jnp.einsum('bn,nri->bri', gate, lora_A)
        B_eff = jnp.einsum('bn,nor->bor', gate, lora_B)
        Ax = jnp.einsum('bri,bti->btr', A_eff, x_flat)
        delta_flat = jnp.einsum('bor,btr->bto', B_eff, Ax)
        Ax_s = jnp.einsum('ri,bti->btr', lora_A_shared, x_flat)
        delta_flat = delta_flat + jnp.einsum('or,btr->bto', lora_B_shared, Ax_s)
        delta = delta_flat.reshape(x.shape[:-1] + (kernel.shape[-1],))
        return base_out + (SCALING * delta).astype(base_out.dtype)
    x = L0_attn_hidden_states
    x = x + 0.5 * _L0_ffn_ref(_layernorm(x, axis=-1), L0_ffn_w1, L0_ffn_w1_scale, L0_ffn_w3, L0_ffn_w3_scale, L0_ffn_w2, L0_ffn_w2_scale)
    x = x + _L0_attn_ref(_layernorm(x, axis=-1), L0_attn_up_w, L0_attn_gate_w, L0_attn_local_point, L0_attn_local_approx_output, L0_attn_fuse_weight, L0_attn_discount_factor, L0_attn_ffn_gate_w, L0_attn_ffn_up_w, L0_attn_ffn_down_w)
    x = x + 0.5 * _L0_ffn_ref(_layernorm(x, axis=-1), L0_ffn_w1, L0_ffn_w1_scale, L0_ffn_w3, L0_ffn_w3_scale, L0_ffn_w2, L0_ffn_w2_scale)
    x = x + 0.5 * _L1_ffn_ref(_layernorm(x, axis=-1), L1_ffn_W, L1_ffn_b, L1_ffn_Wq, L1_ffn_Wk, L1_ffn_A, L1_ffn_Bm)
    x = x + _L1_attn_ref(_layernorm(x, axis=-1), L1_attn_Wq, L1_attn_bq, L1_attn_Wk, L1_attn_bk, L1_attn_Wv, L1_attn_bv, L1_attn_Wo, L1_attn_bo)
    x = x + 0.5 * _L1_ffn_ref(_layernorm(x, axis=-1), L1_ffn_W, L1_ffn_b, L1_ffn_Wq, L1_ffn_Wk, L1_ffn_A, L1_ffn_Bm)
    x = x + 0.5 * _L2_ffn_ref(_layernorm(x, axis=-1), L2_ffn_weight, L2_ffn_bias, L2_ffn_gate_w, L2_ffn_in_channel_scale, L2_ffn_out_channel_scale)
    x = x + _L2_attn_ref(_layernorm(x, axis=-1))
    x = x + 0.5 * _L2_ffn_ref(_layernorm(x, axis=-1), L2_ffn_weight, L2_ffn_bias, L2_ffn_gate_w, L2_ffn_in_channel_scale, L2_ffn_out_channel_scale)
    x = x + 0.5 * _L3_ffn_ref(_layernorm(x, axis=-1), L3_ffn_gate, L3_ffn_kernel, L3_ffn_bias, L3_ffn_lora_A, L3_ffn_lora_B, L3_ffn_lora_A_shared, L3_ffn_lora_B_shared)
    x = x + _L3_attn_ref(_layernorm(x, axis=-1), L3_attn_Wq, L3_attn_Wk, L3_attn_Wv, L3_attn_Wo)
    x = x + 0.5 * _L3_ffn_ref(_layernorm(x, axis=-1), L3_ffn_gate, L3_ffn_kernel, L3_ffn_bias, L3_ffn_lora_A, L3_ffn_lora_B, L3_ffn_lora_A_shared, L3_ffn_lora_B_shared)
    return x

_drawn_inputs = setup_inputs


def setup_inputs(seed=0):
    import zlib

    import numpy as np

    out = dict(_drawn_inputs(seed))
    spreads = {'L1_ffn_b': (0.0, 0.8), 'L3_ffn_bias': (0.0, 2.0)}
    factors = {'L0_ffn_w1_scale': 6.533,
     'L0_ffn_w3_scale': 6.364,
     'L0_ffn_w2_scale': 7.783,
     'L1_attn_bq': 64.0,
     'L1_attn_bk': 200.0,
     'L1_ffn_Wq': 8.0,
     'L1_ffn_Wk': 8.0,
     'L1_ffn_A': 4.684,
     'L1_ffn_Bm': 4.673,
     'L2_ffn_bias': 200.0,
     'L3_attn_Wq': 8.0,
     'L3_attn_Wk': 8.0,
     'L3_attn_Wv': 2.98,
     'L3_attn_Wo': 3.028,
     'L3_ffn_gate': 4.111,
     'L3_ffn_lora_A': 4.365,
     'L3_ffn_lora_B': 4.399,
     'L3_ffn_lora_A_shared': 21.521,
     'L3_ffn_lora_B_shared': 21.953,
     'L0_attn_gate_w': 3.384,
     'L0_attn_local_point': 3.312,
     'L0_attn_local_approx_output': 8.0,
     'L0_attn_ffn_gate_w': 8.0,
     'L0_attn_ffn_up_w': 8.0,
     'L0_attn_ffn_down_w': 8.0,
     'L1_attn_Wq': 8.0,
     'L1_attn_Wk': 8.0,
     'L1_attn_Wv': 8.0,
     'L1_attn_bv': 8.0,
     'L1_attn_Wo': 8.0,
     'L1_attn_bo': 64.0,
     'L1_ffn_W': 3.198,
     'L2_ffn_gate_w': 2.695,
     'L3_ffn_kernel': 5.183}
    for name, (base, spread) in spreads.items():
        noise = np.random.default_rng([zlib.crc32(name.encode()), seed]).standard_normal(out[name].shape)
        drawn = base * np.exp(spread * noise) if base else spread * noise
        out[name] = jnp.asarray(drawn.astype(out[name].dtype))
    for name, factor in factors.items():
        out[name] = (out[name] * factor).astype(out[name].dtype)
    return out
```

```python
import numpy as np
import concourse.bass as bass
from concourse import mybir

F32 = mybir.dt.float32
F32R = mybir.dt.float32r
ALU = mybir.AluOpType
ACT = mybir.ActivationFunctionType
AX = mybir.AxisListType.X

P = 128
T = 1024
D = 512
TT = T // P
KT = D // P
HT = TT // 2
HALF = T // 2
CHUNK = 3 * D
PA = 2 * D
EPS = 1e-5

FFN0, GATE0, FFN1, ATT1, FFN2, ATT2, FFN3, ATT3 = "FFN0 GATE0 FFN1 ATT1 FFN2 ATT2 FFN3 ATT3".split()
ORDER = [FFN0, GATE0, FFN0, FFN1, ATT1, FFN1, FFN2, ATT2, FFN2, FFN3, ATT3, FFN3]

F0_STEPS = 1792 // P
G0_STEPS = -(-1248 // P)
ORDERS = 6
THD = 2.5
EXP1, DK1, RANK1 = 8, 32, 16
H1, HD1 = 32, 16
E2 = 8
TOPK = int(np.log(D))
H3, KV3, HD3 = 32, 8, 128
NL3, R3, B3 = 16, 32, 8
GROUPS = {ATT1: 4, ATT3: 8}
NEG = -1e30
BIG, NONE = 1e30, -3e38

CHUNKS = {FFN0: F0_STEPS, GATE0: G0_STEPS + 3, FFN1: 4, ATT1: 2, FFN2: 2, ATT2: 5, FFN3: 2, ATT3: 4}
EFF_CHUNKS = 3


def chunk_bases():
    base, at = {}, 0
    for kind in (FFN0, GATE0, FFN1, ATT1, FFN2, ATT2, FFN3, ATT3):
        base[kind] = at
        at += CHUNKS[kind] * (GROUPS.get(kind, 1)) + (EFF_CHUNKS if kind == FFN3 else 0)
    return base, at


DRAM_BASE, N_DRAM_CHUNKS = chunk_bases()


class Call:
    pass


def plan(layers):
    calls, chunks = [], []
    xb = steps = t_runs = lns = 0
    for n, kind in enumerate(layers):
        halves = [None] if kind in GROUPS else [0, 1]
        for half in halves:
            c = Call()
            c.kind, c.half, c.first = kind, half, half in (0, None)
            c.xb = xb
            c.sb = steps
            c.cb = len(chunks)
            c.n = sum(1 for q in calls if q.kind == kind)
            base = DRAM_BASE[kind]
            if kind in GROUPS:
                c.lns = [lns, lns + 1]
                lns += 2
                c.ts = [t_runs, t_runs + 1]
                t_runs += 2
                chunks += [(base + g * CHUNKS[kind] + i, False, False) for g in range(GROUPS[kind]) for qt in range(2)
                           for i in range(CHUNKS[kind])]
                xb += TT * GROUPS[kind]
            else:
                c.lns = [lns]
                lns += 1
                if kind == FFN3:
                    if half == 0:
                        chunks += [(base + i, False, False) for i in range(EFF_CHUNKS)]
                    base += EFF_CHUNKS
                c.mb = len(chunks)
                chunks += [(base + i, kind == FFN0, kind == FFN2) for i in range(CHUNKS[kind])]
                c.ts = [t_runs + i for i in range(2 if kind in (FFN2, ATT2) else 1)]
                t_runs += len(c.ts)
                xb += HT
                steps += {FFN0: F0_STEPS, GATE0: G0_STEPS}.get(kind, 0)
            calls.append(c)
    return calls, chunks, xb


class Chain:

    def __init__(self, eng, sem):
        self.eng, self.sem, self.value = eng, sem, 0

    def sig(self, ins):
        ins.then_inc(self.sem, 1)
        self.value = self.value + 1

    def wait(self):
        self.eng.wait_ge(self.sem, self.value)

    def link(self, ins):
        self.sig(ins)
        self.wait()

    def enter(self, j, per_turn):
        self.start, self.per_turn = self.value, per_turn
        self.value = j * per_turn + self.start
        self.turn = self.value

    def leave(self, turns, used):
        assert used == self.per_turn, (used, self.per_turn)
        self.value = self.start + turns * self.per_turn


def build(nc, inp, x_in, out, layers=ORDER):
    calls, chunks, x_total = plan(layers)
    kinds = set(layers)
    sems = {}

    def sem(name):
        if name not in sems:
            sems[name] = nc.alloc_semaphore(name)
        return sems[name]

    top = [16512]

    def keep(name, shape, dtype=F32):
        size = int(np.prod(shape[1:])) * 4
        t = nc.alloc_sbuf_tensor_at(name, shape, dtype, offset=top[0])
        top[0] += -(-size // 32) * 32
        return t

    x = keep("x", [P, TT, D])
    xt_hi = keep("xt_hi", [P, KT, T], F32R)
    xt_lo = keep("xt_lo", [P, KT, T], F32R)
    xn = keep("xn", [P, HT, D])
    raw = keep("raw", [P, 2, CHUNK])
    w_hi = [keep(f"w_hi{s}", [P, CHUNK], F32R) for s in range(2)]
    w_lo = [keep(f"w_lo{s}", [P, CHUNK], F32R) for s in range(2)]
    ident = keep("ident", [P, P])
    stats = keep("stats", [P, HT, 6])
    mv = keep("mv", [P, HT, 2])
    var_eps = keep("var_eps", [P, HT])
    rstd = keep("rstd", [P, HT])
    ident_r = keep("ident_r", [P, P], F32R)
    mask = keep("mask", [P, P])
    mask_r = keep("mask_r", [P, P], F32R)
    minus_half = keep("minus_half", [P, HT])
    ARENA = top[0]
    SBUF_END = 229344

    class Arena:

        def __init__(self, tag):
            self.tag, self.at = tag, ARENA

        def __call__(self, name, shape, dtype=F32):
            size = int(np.prod(shape[1:])) * 4
            t = nc.alloc_sbuf_tensor_at(f"{self.tag}_{name}", shape, dtype, offset=self.at)
            self.at += -(-size // 32) * 32
            assert self.at <= SBUF_END, (self.tag, name, self.at - SBUF_END)
            return t

    a = Arena("g")
    s_buf = a("s_buf", [P, 2, D])
    h_buf = a("h_buf", [P, 2, D])
    h_hi = [a(f"h_hi{p}", [P, D], F32R) for p in range(2)]
    h_lo = [a(f"h_lo{p}", [P, D], F32R) for p in range(2)]
    scales = a("scales", [P, F0_STEPS, 3 * KT])
    lpoint = a("lpoint", [P, 1])
    coef = a("coef", [P, ORDERS])
    delta = a("delta", [P, D])
    near = a("near", [P, D])
    term = a("term", [P, ORDERS + 1, D])
    term_hi = [a(f"term_hi{m}", [P, D], F32R) for m in range(ORDERS + 1)]
    term_lo = [a(f"term_lo{m}", [P, D], F32R) for m in range(ORDERS + 1)]

    a = Arena("f1")
    bias1 = a("bias", [P, D])
    q_sb = a("q_sb", [P, HT, EXP1 * DK1])
    h1 = a("h1", [P, HT * EXP1, RANK1])
    prod = a("prod", [P, HT * EXP1, DK1])
    score1 = a("score1", [P, HT, EXP1])
    top1 = a("top1", [P, HT])
    soft1 = a("soft1", [P, HT, EXP1])
    wh = a("wh", [P, HT * EXP1, RANK1])
    wht_hi = a("wht_hi", [P, HALF], F32R)
    wht_lo = a("wht_lo", [P, HALF], F32R)

    a = Arena("f2")
    bias2 = a("bias", [P, D])
    small2 = a("small", [P, KT * E2])
    small2_hi = a("small_hi", [P, KT * E2], F32R)
    small2_lo = a("small_lo", [P, KT * E2], F32R)
    chan = a("chan", [P, 2 * D])
    chan_hi = a("chan_hi", [P, 2 * D], F32R)
    chan_lo = a("chan_lo", [P, 2 * D], F32R)
    logit = a("logit", [P, HT, E2])
    top2 = a("top2", [P, HT])
    route = a("route", [P, HT, E2])
    rt_hi = a("rt_hi", [P, HALF], F32R)
    rt_lo = a("rt_lo", [P, HALF], F32R)
    out_sc = a("out_sc", [P, HT, D])
    scaled_y = a("scaled_y", [P, HT, D])

    a = Arena("a2")
    spec = a("spec", [P, 4, HALF])
    sq = a("sq", [P, 4, HALF])
    power_hi = a("power_hi", [P, 2, HALF], F32R)
    power_lo = a("power_lo", [P, 2, HALF], F32R)
    power_sum = a("power_sum", [P, 2, HALF])
    nyq_hi = a("nyq_hi", [P, HALF], F32R)
    nyq_lo = a("nyq_lo", [P, HALF], F32R)
    corr = a("corr", [P, HT, D + 8])
    marked = a("marked", [P, HT, D + 8])
    ex2 = a("ex2", [P, HT, D])
    top8 = a("top8", [P, HT, 8])
    nmax2 = a("nmax2", [P, HT])
    sum2 = a("sum2", [P, HT])
    cross = a("cross", [P, 4, HALF])
    mix = a("mix", [P, 4, HALF])
    mix_hi = a("mix_hi", [P, 4, HALF], F32R)
    mix_lo = a("mix_lo", [P, 4, HALF], F32R)

    a = Arena("f3")
    bias3 = a("bias", [P, D])
    gate_rep = a("gate_rep", [P, 4 * B3])
    same_rank = a("same_rank", [P, R3])
    own_block = a("own_block", [P, HALF])
    gmat = a("gmat", [P, 4 * B3, R3])
    gmat_hi = a("gmat_hi", [P, 4 * B3 * R3], F32R)
    gmat_lo = a("gmat_lo", [P, 4 * B3 * R3], F32R)
    aeff_hi = a("aeff_hi", [P, KT, B3 * R3], F32R)
    aeff_lo = a("aeff_lo", [P, KT, B3 * R3], F32R)
    beff_hi = a("beff_hi", [P, 2, D], F32R)
    beff_lo = a("beff_lo", [P, 2, D], F32R)
    h3 = a("h3", [P, HALF])
    h3_hi = a("h3_hi", [P, HALF], F32R)
    h3_lo = a("h3_lo", [P, HALF], F32R)
    hs_hi = a("hs_hi", [R3, HALF], F32R)
    hs_lo = a("hs_lo", [R3, HALF], F32R)

    att = {}
    for kind, tag in ((ATT1, "a1"), (ATT3, "a3")):
        a, m = Arena(tag), Call()
        att[kind] = m
        m.tag, m.kind, m.ch = tag, kind, CHUNKS[kind]
        m.heads = {ATT1: H1, ATT3: H3}[kind] // GROUPS[kind]
        m.groups = GROUPS[kind]
        m.prob = [a(f"prob{i}", [P, HT, T]) for i in range(2)]
        m.pt_hi = [a(f"pt_hi{i}", [P, HALF], F32R) for i in range(2)]
        m.pt_lo = [a(f"pt_lo{i}", [P, HALF], F32R) for i in range(2)]
        m.nmax = a("nmax", [P, 8])
        m.rsum = a("rsum", [P, 8])
        m.rinv = a("rinv", [P, 8])
        m.v_hi = a("v_hi", [P, TT, P], F32R)
        m.v_lo = a("v_lo", [P, TT, P], F32R)
        if kind == ATT1:
            m.qkv = a("qkv", [P, 2, 3, m.heads, HD1])
            m.bias_qkv = a("bias_qkv", [P, m.groups, 3 * m.heads * HD1])
            m.bias_o = a("bias_o", [P, D])
            m.q_parts = [a(f"q_parts{i}", [P, m.heads, 2, 2, HD1], F32R) for i in range(2)]
            m.k_parts = [a(f"k_parts{i}", [P, m.heads, 2, 2, HD1], F32R) for i in range(2)]
            m.q = a("q", [P, m.heads // 2, HALF], F32R)
            m.k = a("k", [P, m.heads // 2, T], F32R)
            m.v_pad = [[a(f"v_pad_{q}{i}", [P, TT, P], F32R) for q in ("hi", "lo")] for i in range(2)]
            m.zero = a("zero", [P, TT, HD1])
            m.o_hi = a("o_hi", [P, 1, HALF], F32R)
            m.o_lo = a("o_lo", [P, 1, HALF], F32R)
        else:
            m.cos = a("cos", [P, TT, HD3 // 2])
            m.sin = a("sin", [P, TT, HD3 // 2])
            m.by_cos = a("by_cos", [P, 2 * (m.heads + 1), HD3 // 2])
            m.by_sin = a("by_sin", [P, 2 * (m.heads + 1), HD3 // 2])
            m.rot = [a(f"rot{i}", [P, m.heads + 1, HD3]) for i in range(2)]
            m.q_hi = a("q_hi", [P, m.heads, HALF], F32R)
            m.q_lo = a("q_lo", [P, m.heads, HALF], F32R)
            m.k_hi = a("k_hi", [P, T], F32R)
            m.k_lo = a("k_lo", [P, T], F32R)
            m.o_hi = a("o_hi", [P, m.heads, HALF], F32R)
            m.o_lo = a("o_lo", [P, m.heads, HALF], F32R)

    Y = nc.alloc_psum_tensor("Y", [P, 4, D], F32)
    W = nc.alloc_psum_tensor("W", [P, 4, D], F32)

    def mm3(o, a_hi, a_lo, b_hi, b_lo, start, stop):
        nc.tensor.matmul(o, a_hi, b_hi, start=start, stop=False)
        nc.tensor.matmul(o, a_lo, b_hi, start=False, stop=False)
        return nc.tensor.matmul(o, a_hi, b_lo, start=False, stop=stop)

    def gated(c):
        if c.kind == FFN0:
            return F0_STEPS, c.cb, 0
        return G0_STEPS, c.cb + 1, 2

    aux = {
        FFN1: [(bias1[:, :], inp["ffn1_b"].broadcast_to((P, D)))],
        FFN2: [(bias2[:, :], inp["ffn2_b"].broadcast_to((P, D))), (small2[:, :], inp["router"]),
               (chan[0:E2, :], inp["channel"])],
        FFN3: [(bias3[:, :], inp["ffn3_b"].broadcast_to((P, D))), (gate_rep[:, :], inp["gate_rep"]),
               (same_rank[:, :], inp["same_rank"]), (own_block[:, :], inp["own_block"])],
    }
    aux[ATT1] = [(att[ATT1].bias_qkv[:, :, :].rearrange("p g c -> p (g c)"), inp["att1_qkv_b"].broadcast_to((P, 3 * D))),
                 (att[ATT1].bias_o[:, :], inp["att1_o_b"].broadcast_to((P, D)))]
    aux[ATT3] = [(att[ATT3].cos[:, :, :], inp["rope_cos"]), (att[ATT3].sin[:, :, :], inp["rope_sin"])]
    aux_total = 0
    for q in calls:
        if q.first:
            aux_total += 16 * len(aux.get(q.kind, []))
        q.aux = aux_total

    class Phase:

        def __init__(self, c, g, qt):
            m = self.m = att[c.kind]
            self.c, self.g, self.qt = c, g, qt
            self.nkb = (qt + 1) * HT
            per = 2 * m.heads * HT
            self.tiles = g * TT + qt * HT
            self.rows = g * per + qt * m.heads * HT
            self.blocks = g * (3 * m.heads * HT) + qt * m.heads * HT
            self.units = g * (2 * m.heads) + qt * m.heads
            self.chunk = g * (2 * m.ch) + (c.cb + qt * m.ch)
            self.chunk0 = c.cb + qt * m.ch
            self.no = g * 2 + qt
            self.x = g * TT + (c.xb + qt * HT)

        def sem(self, name):
            return sem(f"{self.m.tag}_{name}")

        def share(self, n, q):
            return range(q * self.nkb // HT, (q + 1) * self.nkb // HT)

        def cols(self, j):
            return max(0, j - self.qt * HT) * P

    def tok(half, t):
        return half * HALF + t * P

    with nc.Block() as block:

        @block.sync
        def _(sp):
            def load(c, dram, slot):
                if not isinstance(c, int) or c >= 2:
                    sp.wait_ge(sem("w_lo_b"), c - 1)
                sp.dma_start(raw[:, slot, :], inp["weights"][dram]).then_inc(sem(f"raw{slot}"), 16)

            sp.dma_start(x[:, :, :], x_in.rearrange("(t p) d -> p t d", p=P)).then_inc(sem("x_loaded"), 16)
            sp.dma_start(ident[:, :], inp["ident"]).then_inc(sem("const"), 16)
            sp.dma_start(mask[:, :], inp["mask"]).then_inc(sem("const"), 16)
            if kinds & {FFN0, GATE0}:
                sp.dma_start(scales[:, :, :], inp["scales"].rearrange("(a s) k -> a s k", a=1).broadcast_to((P, F0_STEPS, 12))).then_inc(sem("const"), 16)
                sp.dma_start(lpoint[:, :], inp["local_point"]).then_inc(sem("const"), 16)
                sp.dma_start(coef[:, :], inp["discount"].broadcast_to((P, ORDERS))).then_inc(sem("const"), 16)
            at_aux = {q.cb + 1: q for q in calls if q.first and aux.get(q.kind)}

            def load_aux(n):
                if n in at_aux:
                    q = at_aux.pop(n)
                    if q.xb:
                        sp.wait_ge(sem("x_ready"), q.xb)
                    for dst, src in aux[q.kind]:
                        sp.dma_start(dst, src).then_inc(sem("aux"), 16)

            n = 0
            grouped = {q.cb: q for q in calls if q.kind in GROUPS}
            while n < len(chunks):
                m = n
                if n in grouped:
                    q = grouped[n]
                    per, first = 2 * CHUNKS[q.kind], chunks[n][0]
                    if q.xb:
                        sp.wait_ge(sem("x_ready"), q.xb)
                    for dst, src in aux[q.kind]:
                        sp.dma_start(dst, src).then_inc(sem("aux"), 16)
                    at_aux.pop(n + 1)
                    with sp.Fori(0, GROUPS[q.kind]) as g:
                        for a in range(per):
                            load(g * per + (n + a), bass.ds(g * CHUNKS[q.kind] + (first + a % CHUNKS[q.kind]), 1), (n + a) % 2)
                    n += per * GROUPS[q.kind]
                    continue
                load_aux(n)
                while m + 1 < len(chunks) and chunks[m + 1][0] == chunks[m][0] + 1 and m + 1 not in at_aux and m + 1 not in grouped:
                    m += 1
                count = m + 1 - n
                while count and (n < 2 or count % 2):
                    load(n, chunks[n][0], n % 2)
                    n, count = n + 1, count - 1
                if count >= 4:
                    with sp.Fori(0, count // 2) as j:
                        for a in range(2):
                            load(j * 2 + (n + a), bass.ds(j * 2 + (chunks[n][0] + a), 1), (n + a) % 2)
                else:
                    for a in range(count):
                        load(n + a, chunks[n + a][0], (n + a) % 2)
                n += count
            sp.wait_ge(sem("x_ready"), x_total)
            sp.dma_start(out.rearrange("(t p) d -> p t d", p=P), x[:, :, :]).then_inc(sem("stored"), 16)
            sp.wait_ge(sem("stored"), 16)

        @block.gpsimd
        def _(pool):
            nc.gpsimd.memset(minus_half[:, :], -0.5).then_inc(sem("pool_const"), 1)

            def scale(c, i):
                slot = (i % 2 + cs) % 2
                return slot

            def apply_scale(c, slot, step):
                pool.wait_ge(sem(f"raw{slot}"), raw_count(c))
                v = raw[:, slot, :].rearrange("p (b f) -> p b f", f=P)
                sc = scales[:, step, :].rearrange("p (k one) -> p k one", one=1)
                nc.gpsimd.tensor_tensor(v, v, sc.broadcast_to((P, 12, P)), ALU.mult).then_inc(sem("scaled"), 1)

            def raw_count(c):
                return 16 * (c[0] // 2 + 1) + 16 * c[1] if isinstance(c, tuple) else 16 * (c // 2 + 1)

            def split_lo(c, slot, sign=False):
                for part, lo, hi in (("a", 0, PA), ("b", PA, CHUNK)):
                    pool.wait_ge(sem(f"w_hi_{part}"), c + 1)
                    if sign:
                        pool.wait_ge(sem(f"w_lo_{part}"), c)
                        pool.sem_inc(sem(f"w_lo_{part}"), 1)
                    else:
                        nc.gpsimd.tensor_tensor(w_lo[slot][:, lo:hi], raw[:, slot, lo:hi], w_hi[slot][:, lo:hi].bitcast(F32),
                                                ALU.subtract).then_inc(sem(f"w_lo_{part}"), 1)

            def pow_of(ln):
                pool.wait_ge(sem("var_ready"), ln + 1)
                nc.gpsimd.tensor_tensor(rstd[:, :], var_eps[:, :], minus_half[:, :], ALU.pow).then_inc(sem("rstd"), 1)

            pool.wait_ge(sem("pool_const"), 1)
            if chunks[0][1]:
                pool.wait_ge(sem("const"), 16 * 5)
                apply_scale(0, 0, 0)
            at_chunk = {}
            for q in calls:
                if q.kind not in GROUPS:
                    at_chunk.setdefault(q.cb + 1, []).extend(q.lns)
            scaled_step = lambda c: chunks[c][0] - DRAM_BASE[FFN0]

            def one(c):
                for ln in at_chunk.get(c, []):
                    pow_of(ln)
                if c + 1 < len(chunks) and chunks[c + 1][1]:
                    apply_scale(c + 1, (c + 1) % 2, scaled_step(c + 1))
                split_lo(c, c % 2, chunks[c][2])

            def run_chunks(n, stop):
                while n < stop:
                    def plain(c):
                        if c + 1 >= stop or c in at_chunk or chunks[c][2]:
                            return None
                        nxt = chunks[c + 1]
                        return (nxt[1], nxt[0] - c if nxt[1] else None)
                    one(n)
                    n += 1
                    if n >= stop or plain(n) is None:
                        continue
                    m = n
                    while plain(m + 1) is not None and plain(m + 1) == plain(n):
                        m += 1
                    pairs = (m + 1 - n) // 2
                    if pairs < 2:
                        continue
                    with pool.Fori(0, pairs) as j:
                        for a in range(2):
                            c = n + a
                            if chunks[c + 1][1]:
                                slot = (c + 1) % 2
                                pool.wait_ge(sem(f"raw{slot}"), j * 16 + 16 * ((c + 1) // 2 + 1))
                                v = raw[:, slot, :].rearrange("p (b f) -> p b f", f=P)
                                sc = scales[:, bass.ds(j * 2 + scaled_step(c + 1), 1), :].rearrange("p one k -> p k one")
                                nc.gpsimd.tensor_tensor(v, v, sc.broadcast_to((P, 12, P)), ALU.mult).then_inc(sem("scaled"), 1)
                            split_lo(j * 2 + c, c % 2)
                    n += 2 * pairs

            def attention(c):
                m = att[c.kind]
                if not calls.index(c):
                    split_lo(c.cb, c.cb % 2)
                else:
                    split_lo(c.cb, c.cb % 2)
                for ln in c.lns:
                    pow_of(ln)
                if c.kind == ATT1:
                    for pads in m.v_pad:
                        for v in pads:
                            nc.gpsimd.memset(v[:, :, :].bitcast(F32), 0.0).then_inc(sem("pool_pad"), 1)
                    nc.gpsimd.memset(m.zero[:, :, :], 0.0).then_inc(sem("pool_pad"), 1)
                    pool.wait_ge(sem("pool_pad"), 5)

                def phase(g, qt):
                    ph = Phase(c, g, qt)

                    def pad(u):
                        if u >= 2:
                            pool.wait_ge(ph.sem("av"), ph.units + (u - 1))
                        old, new = ((u - 2) % m.heads) * HD1, u * HD1
                        for v, src in zip(m.v_pad[u % 2], (m.v_hi, m.v_lo)):
                            nc.gpsimd.tensor_tensor(v[:, :, old:old + HD1], m.zero[:, :, :], m.zero[:, :, :], ALU.add)
                            ins = nc.gpsimd.tensor_copy(v[:, 0:ph.nkb, new:new + HD1], src[:, 0:ph.nkb, new:new + HD1].bitcast(F32))
                        ins.then_inc(ph.sem("pad"), 1)

                    for i in range(1, m.ch):
                        if i < 2 or c.kind == ATT1:
                            split_lo(ph.chunk + i, (ph.chunk0 + i) % 2)
                    if c.kind == ATT3:
                        split_lo(ph.chunk + 1, (ph.chunk0 + 1) % 2) if m.ch < 2 else None
                        for t in range(HT):
                            pool.wait_ge(ph.sem("by_sin"), ph.tiles + (t + 1))
                            nc.gpsimd.tensor_tensor(m.rot[t % 2][:, :, :].rearrange("p h d -> p (h d)"),
                                                    m.by_cos[:, :, :].rearrange("p h d -> p (h d)"),
                                                    m.by_sin[:, :, :].rearrange("p h d -> p (h d)"), ALU.add).then_inc(ph.sem("rot"), 1)
                        for i in range(2, m.ch):
                            split_lo(ph.chunk + i, (ph.chunk0 + i) % 2)
                    else:
                        pool.wait_ge(ph.sem("v_lo"), ph.tiles + HT)
                        pad(0)
                    if c.kind == ATT1:
                        for u in range(1, m.heads):
                            pad(u)

                with pool.Fori(0, m.groups) as g:
                    phase(g, 0)
                    split_lo(g * (2 * m.ch) + (c.cb + m.ch), (c.cb + m.ch) % 2)
                    phase(g, 1)
                    with_next(g, c, m)

            def with_next(g, c, m):
                split_lo(g * (2 * m.ch) + (c.cb + 2 * m.ch), (c.cb + 2 * m.ch) % 2)

            skip = 0
            for n, c in enumerate(calls):
                stop = calls[n + 1].cb if n + 1 < len(calls) else len(chunks)
                if c.kind in GROUPS:
                    attention(c)
                    skip = 1
                else:
                    run_chunks(c.cb + skip, stop)
                    skip = 0

        @block.scalar
        def _(act):
            n_scaled = [0]

            def split_hi(c, part, loop=None):
                if c >= len(chunks):
                    return
                slot = c % 2
                _, scaled, sign = chunks[c]
                off = 0 if loop is None else loop
                if scaled:
                    k = sum(1 for q in chunks[:c + 1] if q[1])
                    act.wait_ge(sem("scaled"), off * 2 + k)
                else:
                    act.wait_ge(sem(f"raw{slot}"), off * 16 + 16 * (c // 2 + 1))
                if c >= 2:
                    act.wait_ge(sem(f"w_free_{part}"), off * 2 + (c - 1))
                lo, hi = (0, PA) if part == "a" else (PA, CHUNK)
                nc.scalar.activation(w_hi[slot][:, lo:hi], raw[:, slot, lo:hi], ACT.Sign if sign else ACT.Copy)\
                    .then_inc(sem(f"w_hi_{part}"), 1)

            def turn(n, half):
                for t in range(HT):
                    act.wait_ge(sem("turned"), n * HT + t + 1)
                    nc.scalar.activation(xt_hi[:, :, tok(half, t):tok(half, t) + P],
                                         W[:, t % 2, :].rearrange("p (k q) -> p k q", k=KT), ACT.Copy).then_inc(sem("xt_hi"), 1)

            def gate0_terms(c, ms):
                for m in ms:
                    act.wait_ge(*((sem("term"), ORDERS * c.n + m) if m else (sem("up_copied"), c.n + 1)))
                    kw = {} if m == 0 else dict(scale=coef[:, m - 1:m])
                    nc.scalar.activation(term_hi[m][:, :], term[:, m, :], ACT.Copy if m == 0 else ACT.Identity, **kw)\
                        .then_inc(sem("term_hi"), 1)

            def gated_call(c):
                steps, cb, _ = gated(c)
                if c.kind == GATE0:
                    split_hi(cb, "a")
                    act.wait_ge(sem("w_free_a"), cb)
                    nc.scalar.activation(term[:, 0, :], W[:, 0, :], ACT.Copy).then_inc(sem("up_copied"), 1)
                    gate0_terms(c, [0])
                    split_hi(cb, "b")

                def step(i, j=None):
                    off = 0 if j is None else j
                    split_hi(cb + i + 1, "a", j)
                    p = i % 2
                    act.wait_ge(sem("w_free_a"), off * 2 + (cb + i + 1))
                    nc.scalar.activation(s_buf[:, p, :], W[:, 2 * p, :], ACT.Silu).then_inc(sem("silu"), 1)
                    act.wait_ge(sem("h"), off * 2 + (c.sb + i + 1))
                    nc.scalar.activation(h_hi[p][:, :], h_buf[:, p, :], ACT.Copy).then_inc(sem("h_hi"), 1)
                    split_hi(cb + i + 1, "b", j)

                step(0)
                if c.kind == GATE0:
                    gate0_terms(c, [1, 2])
                step(1)
                if c.kind == GATE0:
                    gate0_terms(c, [3, 4, 5, 6])
                with act.Fori(0, (steps - 4) // 2) as j:
                    step(2, j)
                    step(3, j)
                step(steps - 2)
                step(steps - 1)
                if c.kind == GATE0:
                    for q in (1, 2):
                        for part in "ab":
                            split_hi(cb + steps + q, part)

            def split(c):
                split_hi(c, "a")
                split_hi(c, "b")

            def ffn1_call(c):
                cb = c.cb
                split(cb + 1)
                split(cb + 2)
                act.wait_ge(sem("w_free_a"), cb + 2)
                nc.scalar.activation(q_sb[:, :, :], W[:, :, 0:EXP1 * DK1], ACT.Copy).then_inc(sem("q_copied"), 1)
                nc.scalar.activation(h1[:, :, :], Y[:, 0, :].rearrange("p (e r) -> p e r", r=RANK1), ACT.Copy)\
                    .then_inc(sem("h1_copied"), 1)
                split(cb + 3)
                act.wait_ge(sem("score1"), c.n + 1)
                nc.scalar.activation(soft1[:, :, :], score1[:, :, :], ACT.Exp, scale=DK1 ** -0.5).then_inc(sem("exp1"), 1)
                act.wait_ge(sem("wh_turned"), c.n + 1)
                nc.scalar.activation(wht_hi[:, :], W[:, 0, :], ACT.Copy).then_inc(sem("wht_hi"), 1)
                split(cb + 4)

            def ffn2_call(c):
                if c.first:
                    act.wait_ge(sem("aux"), c.aux)
                    nc.scalar.activation(small2_hi[:, :], small2[:, :], ACT.Copy)
                    nc.scalar.activation(chan_hi[0:E2, :], chan[0:E2, :], ACT.Copy).then_inc(sem("chan_hi"), 1)
                split(c.cb + 1)
                act.wait_ge(sem("logit"), c.n + 1)
                nc.scalar.activation(route[:, :, :], logit[:, :, :], ACT.Exp).then_inc(sem("exp2"), 1)
                act.wait_ge(sem("route_turned"), c.n + 1)
                nc.scalar.activation(rt_hi[0:E2, :], W[0:E2, 1, :], ACT.Copy).then_inc(sem("rt_hi"), 1)
                turn(c.ts[1], c.half)
                act.wait_ge(sem("out_scale"), c.n + 1)
                nc.scalar.activation(out_sc[:, :, :], W[:, :, :], ACT.Copy).then_inc(sem("out_sc"), 1)
                split(c.cb + 2)

            def att2_call(c):
                cb = c.cb
                split(cb + 1)
                split(cb + 2)
                act.wait_ge(sem("spectrum"), 2 * c.n + 1)
                nc.scalar.activation(spec[:, :, :], Y[:, :, :], ACT.Copy).then_inc(sem("spec"), 1)
                nc.scalar.activation(sq[:, :, :], Y[:, :, :], ACT.Square).then_inc(sem("sq"), 1)
                act.wait_ge(sem("power"), c.n + 1)
                nc.scalar.activation(power_hi[:, :, :], power_sum[:, :, :], ACT.Copy)
                nc.scalar.activation(nyq_hi[0:1, :], sq[0:1, 2, :], ACT.Copy).then_inc(sem("power_hi"), 1)
                split(cb + 3)
                act.wait_ge(sem("correlated"), c.n + 1)
                for t in range(HT):
                    nc.scalar.activation(corr[:, t, 0:D], W[:, t, :], ACT.Copy).then_inc(sem("corr"), 1)
                for t in range(HT):
                    act.wait_ge(sem("nmax2"), c.n * HT + t + 1)
                    nc.scalar.activation(ex2[:, t, :], W[:, t, :], ACT.Exp, bias=nmax2[:, t:t + 1]).then_inc(sem("ex2"), 1)
                turn(c.ts[1], c.half)
                split(cb + 4)
                act.wait_ge(sem("mix"), c.n + 1)
                nc.scalar.activation(mix_hi[:, :, :], mix[:, :, :], ACT.Copy).then_inc(sem("mix_hi"), 1)
                split(cb + 5)

            def ffn3_call(c):
                if c.first:
                    split(c.cb + 1)
                    act.wait_ge(sem("gmat"), c.n // 2 + 1)
                    nc.scalar.activation(gmat_hi[:, :], gmat[:, :, :].rearrange("p b r -> p (b r)"), ACT.Copy).then_inc(sem("gmat_hi"), 1)
                    split(c.cb + 2)
                    act.wait_ge(sem("eff"), c.n + 1)
                    nc.scalar.activation(aeff_hi[:, :, :], W[:, :, 0:B3 * R3], ACT.Copy).then_inc(sem("eff_hi"), 1)
                    split(c.cb + 3)
                    act.wait_ge(sem("eff"), c.n + 2)
                    nc.scalar.activation(beff_hi[:, :, :], Y[:, 0:2, :], ACT.Copy).then_inc(sem("eff_hi"), 1)
                split(c.mb + 1)
                act.wait_ge(sem("h3"), c.n + 1)
                nc.scalar.activation(h3_hi[:, :], h3[:, :], ACT.Copy)
                nc.scalar.activation(hs_hi[:, :], W[0:R3, 1, :], ACT.Copy).then_inc(sem("h3_hi"), 1)
                split(c.mb + 2)

            def attention(c):
                m = att[c.kind]

                def phase(g, qt):
                    ph = Phase(c, g, qt)

                    def hi(i, part=None):
                        slot = (ph.chunk0 + i) % 2
                        for part in "ab":
                            act.wait_ge(sem(f"raw{slot}"), g * (16 * m.ch) + 16 * ((ph.chunk0 + i) // 2 + 1))
                            act.wait_ge(sem(f"w_free_{part}"), ph.chunk + (i - 1))
                            lo, hi_ = (0, PA) if part == "a" else (PA, CHUNK)
                            nc.scalar.activation(w_hi[slot][:, lo:hi_], raw[:, slot, lo:hi_], ACT.Copy).then_inc(sem(f"w_hi_{part}"), 1)

                    def project1(t):
                        s, tt = t % 2, qt * HT + t
                        act.wait_ge(ph.sem("qkv"), ph.tiles + (t + 1))
                        for i, dst in ((0, m.q_parts[s][:, :, :, 0, :]), (1, m.k_parts[s][:, :, 0, :, :])):
                            src = m.qkv[:, s, i, :, :].rearrange("p h (one d) -> p h one d", one=1)
                            nc.scalar.activation(dst, src.broadcast_to((P, m.heads, 2, HD1)), ACT.Copy)
                        nc.scalar.activation(m.v_hi[:, tt, :], m.qkv[:, s, 2, :, :].rearrange("p h d -> p (h d)"), ACT.Copy)\
                            .then_inc(ph.sem("parts_hi"), 1)

                    def turned1(t):
                        act.wait_ge(ph.sem("qk_turned"), ph.tiles + (t + 1))
                        nc.scalar.activation(m.q[:, :, t * P:(t + 1) * P], Y[:, 0, :].rearrange("p (h q) -> p h q", q=P), ACT.Copy,
                                             scale=HD1 ** -0.5).then_inc(ph.sem("q_out"), 1)

                    def project3(t):
                        s, tt = t % 2, qt * HT + t
                        act.wait_ge(ph.sem("by_sin"), ph.tiles + (t + 1))
                        nc.scalar.activation(m.v_hi[:, tt, :], W[:, 2 * s + 1, P:2 * P], ACT.Copy).then_inc(ph.sem("v_hi"), 1)

                    def turned3(t):
                        tt = qt * HT + t
                        act.wait_ge(ph.sem("qk_turned"), ph.tiles + (t + 1))
                        nc.scalar.activation(m.q_hi[:, :, t * P:(t + 1) * P], Y[:, 0, :].rearrange("p (h q) -> p h q", q=P), ACT.Copy)
                        nc.scalar.activation(m.k_hi[:, tt * P:(tt + 1) * P], Y[:, 1, 0:P], ACT.Copy, scale=HD3 ** -0.5)\
                            .then_inc(ph.sem("qk_hi"), 1)

                    def exponent(u, q):
                        row = u * HT + q
                        n = (qt * HT + q + 1) * P
                        act.wait_ge(ph.sem("nmax"), ph.rows + (row + 1))
                        s = row % 2
                        sc = W[:, 2 * s:2 * s + 2, :].rearrange("p b c -> p (b c)")
                        nc.scalar.activation(m.prob[u % 2][:, q, 0:n], sc[:, 0:n], ACT.Exp, bias=m.nmax[:, row % 8:row % 8 + 1],
                                             accum_out=m.rsum[:, row % 8:row % 8 + 1]).then_inc(ph.sem("exp"), 1)

                    def upper(u, j):
                        b = u * ph.nkb + j
                        act.wait_ge(ph.sem("p_turned"), ph.blocks + (b + 1))
                        nc.scalar.activation(m.pt_hi[b % 2][:, ph.cols(j):HALF], Y[:, b % 2, ph.cols(j):HALF], ACT.Copy).then_inc(ph.sem("pt_hi"), 1)

                    def out_hi(u):
                        act.wait_ge(ph.sem("av"), ph.units + (u + 1))
                        nc.scalar.activation(m.o_hi[:, u if c.kind == ATT3 else 0, :], Y[:, 2 + u % 2 if c.kind == ATT3 else 2, :], ACT.Copy)\
                            .then_inc(ph.sem("o_hi"), 1)

                    hi(1)
                    proj, turned = (project1, turned1) if c.kind == ATT1 else (project3, turned3)
                    proj(0)
                    for t in range(HT):
                        if t + 1 < HT:
                            proj(t + 1)
                        turned(t)
                    if c.kind == ATT3:
                        hi(2)
                        hi(3)
                    for q in range(HT):
                        exponent(0, q)
                    for u in range(m.heads):
                        for q in range(HT):
                            if u + 1 < m.heads:
                                exponent(u + 1, q)
                            for j in ph.share(u, q):
                                upper(u, j)
                                if c.kind == ATT3 and u and j == 0:
                                    out_hi(u - 1)
                    out_hi(m.heads - 1)
                    hi(m.ch)

                with act.Fori(0, m.groups) as g:
                    phase(g, 0)
                    phase(g, 1)

            if GATE0 in kinds:
                act.wait_ge(sem("const"), 16 * 5)
                nc.scalar.activation(coef[:, :], coef[:, :], ACT.Exp, scale=-1.0).then_inc(sem("coef"), 1)
                act.wait_ge(sem("coef"), 1)
            split_hi(0, "a")
            split_hi(0, "b")
            act.wait_ge(sem("const"), 32)
            nc.scalar.activation(ident_r[:, :], ident[:, :], ACT.Copy)
            nc.scalar.activation(mask_r[:, :], mask[:, :], ACT.Copy).then_inc(sem("const_r"), 1)
            for c in calls:
                if c.kind in GROUPS:
                    turn(c.ts[0], 0)
                    turn(c.ts[1], 1)
                    attention(c)
                    continue
                turn(c.ts[0], c.half)
                dict(FFN0=gated_call, GATE0=gated_call, FFN1=ffn1_call, FFN2=ffn2_call, ATT2=att2_call, FFN3=ffn3_call)[c.kind](c)

        @block.vector
        def _(dve):
            chain = Chain(dve, sem("dve"))
            xc = [0]

            def layer_norm(ln, half):
                for t in range(HT):
                    ins = nc.vector.bn_stats(stats[:, t, :], x[:, half * HT + t, :])
                chain.link(ins)
                for t in range(HT):
                    ins = nc.vector.bn_aggr(mv[:, t, :], stats[:, t, :])
                chain.link(ins)
                nc.vector.tensor_scalar(var_eps[:, :], mv[:, :, 1], EPS, None, ALU.add).then_inc(sem("var_ready"), 1)
                dve.wait_ge(sem("rstd"), ln + 1)

            def turn_in(n, ln, half):
                layer_norm(ln, half)
                for t in range(HT):
                    nc.vector.tensor_scalar(xn[:, t, :], x[:, half * HT + t, :], mv[:, t, 0:1], rstd[:, t:t + 1],
                                            ALU.subtract, ALU.mult).then_inc(sem("turn_in"), 1)

            def turn(n, half):
                for t in range(HT):
                    dve.wait_ge(sem("xt_hi"), n * HT + t + 1)
                    sl = slice(tok(half, t), tok(half, t) + P)
                    nc.vector.tensor_tensor(xt_lo[:, :, sl], W[:, t % 2, :].rearrange("p (k q) -> p k q", k=KT),
                                            xt_hi[:, :, sl].bitcast(F32), ALU.subtract).then_inc(sem("xt_lo"), 1)

            def residual(half, coef_, name, count):
                dve.wait_ge(sem(name), count)
                for t in range(HT):
                    nc.vector.scalar_tensor_tensor(x[:, half * HT + t, :], Y[:, t, :], coef_, x[:, half * HT + t, :],
                                                   ALU.mult, ALU.add).then_inc(sem("x_ready"), 1)
                    xc[0] += 1

            def term_lo_of(c, ms):
                for m in ms:
                    dve.wait_ge(sem("term_hi"), (ORDERS + 1) * c.n + m + 1)
                    if m == 0:
                        ins = nc.vector.tensor_tensor(term_lo[0][:, :], term[:, 0, :], term_hi[0][:, :].bitcast(F32), ALU.subtract)
                    else:
                        ins = nc.vector.scalar_tensor_tensor(term_lo[m][:, :], term[:, m, :], coef[:, m - 1:m],
                                                             term_hi[m][:, :].bitcast(F32), ALU.mult, ALU.subtract)
                    ins.then_inc(sem("term_lo"), 1)

            def gated_call(c):
                steps, cb, after = gated(c)

                def step(i, j=None):
                    off = 0 if j is None else j
                    p = i % 2
                    dve.wait_ge(sem("silu"), off * 2 + (c.sb + i + 1))
                    nc.vector.tensor_tensor(h_buf[:, p, :], W[:, 2 * p + 1, :], s_buf[:, p, :], ALU.mult).then_inc(sem("h"), 1)
                    dve.wait_ge(sem("h_hi"), off * 2 + (c.sb + i + 1))
                    nc.vector.tensor_tensor(h_lo[p][:, :], h_buf[:, p, :], h_hi[p][:, :].bitcast(F32), ALU.subtract)\
                        .then_inc(sem("h_lo"), 1)

                def power(m):
                    ins = nc.vector.tensor_tensor(term[:, m, :], term[:, m - 1, :], delta[:, :], ALU.mult)
                    if m == 5:
                        chain.link(ins)
                        ins = nc.vector.tensor_tensor(term[:, m, :], term[:, m, :], near[:, :], ALU.mult)
                    ins.then_inc(sem("term"), 1)
                    dve.wait_ge(sem("term"), ORDERS * c.n + m)

                if c.kind == GATE0:
                    if c.n == 0:
                        dve.wait_ge(sem("const"), 16 * 5)
                        dve.wait_ge(sem("coef"), 1)
                    dve.wait_ge(sem("w_free_a"), cb)
                    chain.link(nc.vector.tensor_scalar(delta[:, :], W[:, 1, :], lpoint[:, 0:1], None, ALU.subtract))
                    dve.wait_ge(sem("up_copied"), c.n + 1)
                    chain.link(nc.vector.tensor_scalar(near[:, :], delta[:, :], -THD, None, ALU.is_ge))
                    nc.vector.scalar_tensor_tensor(near[:, :], delta[:, :], THD, near[:, :], ALU.is_le, ALU.mult)\
                        .then_inc(sem("gate_read"), 1)
                    dve.wait_ge(sem("gate_read"), c.n + 1)
                    term_lo_of(c, (0,))
                    step(0)
                    for m in (1, 2):
                        power(m)
                    term_lo_of(c, (1, 2))
                    step(1)
                    for m in (3, 4, 5, 6):
                        power(m)
                    term_lo_of(c, (3, 4, 5, 6))
                else:
                    step(0)
                    step(1)
                with dve.Fori(0, (steps - 4) // 2) as j:
                    step(2, j)
                    step(3, j)
                step(steps - 2)
                step(steps - 1)
                residual(c.half, 0.5 if c.kind == FFN0 else 1.0, "w_free_b", cb + steps + after)

            def add_bias(c, bias):
                dve.wait_ge(sem("aux"), c.aux)
                xs = x[:, c.half * HT:(c.half + 1) * HT, :]
                b = bias[:, :].rearrange("p (one d) -> p one d", one=1).broadcast_to((P, HT, D))
                dve.wait_ge(sem("turn_in"), (c.ts[0] + 1) * HT)
                chain.link(nc.vector.scalar_tensor_tensor(xs, b, 0.5, xs, ALU.mult, ALU.add))

            def over(ap, n):
                return ap.rearrange("p (m one) -> p m one", one=1).broadcast_to((ap.shape[0], ap.shape[1], n))

            def ffn1_call(c):
                add_bias(c, bias1)
                dve.wait_ge(sem("q_copied"), c.n + 1)
                chain.link(nc.vector.tensor_tensor(prod[:, :, :].rearrange("p (t e) d -> p t (e d)", t=HT), W[:, :, EXP1 * DK1:D],
                                                   q_sb[:, :, :], ALU.mult))
                s2 = score1[:, :, :].rearrange("p t e -> p (t e)")
                chain.link(nc.vector.tensor_reduce(s2, prod[:, :, :], AX, ALU.add))
                chain.link(nc.vector.tensor_reduce(top1[:, :], score1[:, :, :], AX, ALU.max))
                nc.vector.tensor_tensor(score1[:, :, :], score1[:, :, :], over(top1[:, :], EXP1), ALU.subtract).then_inc(sem("score1"), 1)
                dve.wait_ge(sem("exp1"), c.n + 1)
                chain.link(nc.vector.tensor_reduce(top1[:, :], soft1[:, :, :], AX, ALU.add))
                chain.link(nc.vector.reciprocal(top1[:, :], top1[:, :]))
                chain.link(nc.vector.tensor_tensor(soft1[:, :, :], soft1[:, :, :], over(top1[:, :], EXP1), ALU.mult))
                dve.wait_ge(sem("h1_copied"), c.n + 1)
                nc.vector.tensor_tensor(wh[:, :, :], h1[:, :, :], over(soft1[:, :, :].rearrange("p t e -> p (t e)"), RANK1), ALU.mult)\
                    .then_inc(sem("wh"), 1)
                dve.wait_ge(sem("wht_hi"), c.n + 1)
                nc.vector.tensor_tensor(wht_lo[:, :], W[:, 0, :], wht_hi[:, :].bitcast(F32), ALU.subtract).then_inc(sem("wht_lo"), 1)
                residual(c.half, 0.5, "w_free_a", c.cb + 4)

            def ffn2_call(c):
                add_bias(c, bias2)
                if c.first:
                    dve.wait_ge(sem("chan_hi"), c.n // 2 + 1)
                    nc.vector.tensor_tensor(small2_lo[:, :], small2[:, :], small2_hi[:, :].bitcast(F32), ALU.subtract)
                    nc.vector.tensor_tensor(chan_lo[0:E2, :], chan[0:E2, :], chan_hi[0:E2, :].bitcast(F32), ALU.subtract)\
                        .then_inc(sem("chan_lo"), 1)
                dve.wait_ge(sem("logits"), c.n + 1)
                lg = W[:, 0, 0:HT * E2].rearrange("p (t e) -> p t e", e=E2)
                chain.link(nc.vector.tensor_reduce(top2[:, :], lg, AX, ALU.max))
                nc.vector.tensor_tensor(logit[:, :, :], lg, over(top2[:, :], E2), ALU.subtract).then_inc(sem("logit"), 1)
                dve.wait_ge(sem("exp2"), c.n + 1)
                chain.link(nc.vector.tensor_reduce(top2[:, :], route[:, :, :], AX, ALU.add))
                chain.link(nc.vector.reciprocal(top2[:, :], top2[:, :]))
                nc.vector.tensor_tensor(route[:, :, :], route[:, :, :], over(top2[:, :], E2), ALU.mult).then_inc(sem("route"), 1)
                dve.wait_ge(sem("rt_hi"), c.n + 1)
                nc.vector.tensor_tensor(rt_lo[0:E2, :], W[0:E2, 1, :], rt_hi[0:E2, :].bitcast(F32), ALU.subtract).then_inc(sem("rt_lo"), 1)
                for t in range(HT):
                    dve.wait_ge(sem("in_scale"), c.n * HT + t + 1)
                    nc.vector.tensor_tensor(xn[:, t, :], W[:, t, :], xn[:, t, :], ALU.mult).then_inc(sem("turn_in"), 1)
                turn(c.ts[1], c.half)
                dve.wait_ge(sem("out_sc"), c.n + 1)
                dve.wait_ge(sem("w_free_a"), c.cb + 2)
                for t in range(HT):
                    ins = nc.vector.tensor_tensor(scaled_y[:, t, :], Y[:, t, :], out_sc[:, t, :], ALU.mult)
                chain.link(ins)
                for t in range(HT):
                    xs = x[:, c.half * HT + t, :]
                    nc.vector.scalar_tensor_tensor(xs, scaled_y[:, t, :], 0.5, xs, ALU.mult, ALU.add).then_inc(sem("x_ready"), 1)
                    xc[0] += 1

            def att2_call(c):
                dve.wait_ge(sem("turn_in"), (c.ts[0] + 1) * HT)
                nc.vector.memset(corr[:, :, D:D + 2], NONE)
                dve.wait_ge(sem("sq"), c.n + 1)
                chain.link(nc.vector.tensor_tensor(power_sum[:, :, :], sq[:, 0:2, :], sq[:, 2:4, :], ALU.add))
                nc.vector.tensor_copy(power_sum[0:1, 0, :], sq[0:1, 0, :]).then_inc(sem("power"), 1)
                dve.wait_ge(sem("power_hi"), c.n + 1)
                dve.wait_ge(sem("power"), c.n + 1)
                nc.vector.tensor_tensor(power_lo[:, :, :], power_sum[:, :, :], power_hi[:, :, :].bitcast(F32), ALU.subtract)
                nc.vector.tensor_tensor(nyq_lo[0:1, :], sq[0:1, 2, :], nyq_hi[0:1, :].bitcast(F32), ALU.subtract).then_inc(sem("power_lo"), 1)
                for t in range(HT):
                    dve.wait_ge(sem("corr"), c.n * HT + t + 1)
                    chain.link(nc.vector.max(top8[:, t, :], corr[:, t, 0:D]))
                    nc.vector.tensor_scalar(nmax2[:, t:t + 1], top8[:, t, 0:1], -1.0, None, ALU.mult).then_inc(sem("nmax2"), 1)
                    chain.link(nc.vector.memset(top8[:, t, TOPK:8], NONE))
                    chain.sig(nc.vector.match_replace(marked[:, t, 0:D + 2], top8[:, t, :], corr[:, t, 0:D + 2], BIG))
                chain.wait()
                for t in range(HT):
                    dve.wait_ge(sem("ex2"), c.n * HT + t + 1)
                    ins = nc.vector.scalar_tensor_tensor(ex2[:, t, :], marked[:, t, 0:D], BIG, ex2[:, t, :], ALU.is_equal, ALU.mult,
                                                         accum_out=sum2[:, t:t + 1])
                    chain.sig(ins)
                chain.wait()
                chain.link(nc.vector.reciprocal(sum2[:, :], sum2[:, :]))
                for t in range(HT):
                    nc.vector.tensor_scalar(xn[:, t, :], ex2[:, t, :], sum2[:, t:t + 1], None, ALU.mult).then_inc(sem("turn_in"), 1)
                turn(c.ts[1], c.half)
                dve.wait_ge(sem("spectrum"), 2 * c.n + 2)
                nc.vector.tensor_tensor(sq[:, :, :], Y[:, :, :], spec[:, :, :], ALU.mult)
                nc.vector.tensor_tensor(cross[:, 0:2, :], Y[:, 0:2, :], spec[:, 2:4, :], ALU.mult)
                chain.link(nc.vector.tensor_tensor(cross[:, 2:4, :], Y[:, 2:4, :], spec[:, 0:2, :], ALU.mult))
                nc.vector.tensor_tensor(mix[:, 0:2, :], sq[:, 0:2, :], sq[:, 2:4, :], ALU.add)
                chain.link(nc.vector.tensor_tensor(mix[:, 2:4, :], cross[:, 2:4, :], cross[:, 0:2, :], ALU.subtract))
                nc.vector.tensor_copy(mix[0:1, 0, :], sq[0:1, 0, :])
                nc.vector.tensor_copy(mix[0:1, 2, :], sq[0:1, 2, :]).then_inc(sem("mix"), 1)
                dve.wait_ge(sem("mix_hi"), c.n + 1)
                nc.vector.tensor_tensor(mix_lo[:, :, :], mix[:, :, :], mix_hi[:, :, :].bitcast(F32), ALU.subtract).then_inc(sem("mix_lo"), 1)
                residual(c.half, 1.0, "w_free_b", c.cb + 5)

            def ffn3_call(c):
                add_bias(c, bias3)
                if c.first:
                    g = over(gate_rep[:, :], R3)
                    r = same_rank[:, :].rearrange("p (one r) -> p one r", one=1).broadcast_to((P, 4 * B3, R3))
                    nc.vector.tensor_tensor(gmat[:, :, :], g, r, ALU.mult).then_inc(sem("gmat"), 1)
                    dve.wait_ge(sem("gmat_hi"), c.n // 2 + 1)
                    nc.vector.tensor_tensor(gmat_lo[:, :], gmat[:, :, :].rearrange("p b r -> p (b r)"), gmat_hi[:, :].bitcast(F32),
                                            ALU.subtract).then_inc(sem("gmat_lo"), 1)
                    dve.wait_ge(sem("eff_hi"), c.n + 1)
                    nc.vector.tensor_tensor(aeff_lo[:, :, :], W[:, :, 0:B3 * R3], aeff_hi[:, :, :].bitcast(F32), ALU.subtract)\
                        .then_inc(sem("eff_lo"), 1)
                    dve.wait_ge(sem("eff_hi"), c.n + 2)
                    nc.vector.tensor_tensor(beff_lo[:, :, :], Y[:, 0:2, :], beff_hi[:, :, :].bitcast(F32), ALU.subtract)\
                        .then_inc(sem("eff_lo"), 1)
                dve.wait_ge(sem("down3"), c.n + 1)
                nc.vector.tensor_tensor(h3[:, :], W[:, 0, :], own_block[:, :], ALU.mult).then_inc(sem("h3"), 1)
                dve.wait_ge(sem("h3_hi"), c.n + 1)
                nc.vector.tensor_tensor(h3_lo[:, :], h3[:, :], h3_hi[:, :].bitcast(F32), ALU.subtract)
                nc.vector.tensor_tensor(hs_lo[:, :], W[0:R3, 1, :], hs_hi[:, :].bitcast(F32), ALU.subtract).then_inc(sem("h3_lo"), 1)
                residual(c.half, 0.5, "w_free_b", c.mb + 2)

            def attention(c):
                m = att[c.kind]
                if c.kind == ATT1:
                    dve.wait_ge(sem("aux"), c.aux)
                    b = m.bias_o[:, :].rearrange("p (one d) -> p one d", one=1).broadcast_to((P, TT, D))
                    dve.wait_ge(sem("turn_in"), (c.ts[1] + 1) * HT)
                    chain.link(nc.vector.tensor_tensor(x[:, :, :], x[:, :, :], b, ALU.add))
                else:
                    dve.wait_ge(sem("aux"), c.aux)

                def phase(g, qt):
                    ph = Phase(c, g, qt)

                    def bank(s):
                        return W[:, 2 * s:2 * s + 2, :].rearrange("p b c -> p (b c)")

                    def project1(t):
                        s, tt = t % 2, qt * HT + t
                        n = 3 * m.heads * HD1
                        dve.wait_ge(ph.sem("proj"), ph.tiles + (t + 1))
                        qkv = m.qkv[:, s, :, :, :].rearrange("p i h d -> p (i h d)")
                        b = m.bias_qkv[:, bass.ds(g, 1), :].rearrange("p one c -> p (one c)")
                        nc.vector.tensor_tensor(qkv, W[:, 2 * s, 0:n], b, ALU.add).then_inc(ph.sem("qkv"), 1)
                        dve.wait_ge(ph.sem("parts_hi"), ph.tiles + (t + 1))
                        for i, hi, dst in ((0, m.q_parts[s][:, :, :, 0, :], m.q_parts[s][:, :, :, 1, :]),
                                           (1, m.k_parts[s][:, :, 0, :, :], m.k_parts[s][:, :, 1, :, :])):
                            src = m.qkv[:, s, i, :, :].rearrange("p h (one d) -> p h one d", one=1)
                            nc.vector.tensor_tensor(dst, src.broadcast_to((P, m.heads, 2, HD1)), hi.bitcast(F32), ALU.subtract)
                        nc.vector.tensor_tensor(m.v_lo[:, tt, :], m.qkv[:, s, 2, :, :].rearrange("p h d -> p (h d)"),
                                                m.v_hi[:, tt, :].bitcast(F32), ALU.subtract).then_inc(ph.sem("v_lo"), 1)

                    def turned1(t):
                        tt = qt * HT + t
                        dve.wait_ge(ph.sem("qk_turned"), ph.tiles + (t + 1))
                        nc.vector.tensor_copy(m.k[:, :, tt * P:(tt + 1) * P], Y[:, 1, :].rearrange("p (h q) -> p h q", q=P))\
                            .then_inc(ph.sem("k_out"), 1)

                    def project3(t):
                        s, tt = t % 2, qt * HT + t
                        H = m.heads + 1
                        dve.wait_ge(ph.sem("proj"), ph.tiles + (t + 1))
                        if t:
                            dve.wait_ge(ph.sem("rot"), ph.tiles + t)
                        cos = m.cos[:, tt, :].rearrange("p (one d) -> p one d", one=1)
                        sin = m.sin[:, tt, :].rearrange("p (one d) -> p one d", one=1).broadcast_to((P, H, HD3 // 2))
                        qk = bank(s)[:, 0:H * HD3]
                        pair = qk.rearrange("p (h two d) -> p h two d", h=H, two=2)
                        out2 = m.by_sin[:, :, :].rearrange("p (h two) d -> p h two d", two=2)
                        nc.vector.tensor_tensor(m.by_cos[:, :, :], qk.rearrange("p (h d) -> p h d", d=HD3 // 2),
                                                cos.broadcast_to((P, 2 * H, HD3 // 2)), ALU.mult)
                        nc.vector.scalar_tensor_tensor(out2[:, :, 0, :], pair[:, :, 1, :], -1.0, sin, ALU.mult, ALU.mult)
                        nc.vector.tensor_tensor(out2[:, :, 1, :], pair[:, :, 0, :], sin, ALU.mult).then_inc(ph.sem("by_sin"), 1)
                        dve.wait_ge(ph.sem("v_hi"), ph.tiles + (t + 1))
                        nc.vector.tensor_tensor(m.v_lo[:, tt, :], W[:, 2 * s + 1, P:2 * P], m.v_hi[:, tt, :].bitcast(F32), ALU.subtract)\
                            .then_inc(ph.sem("v_lo"), 1)

                    def turned3(t):
                        tt = qt * HT + t
                        dve.wait_ge(ph.sem("qk_hi"), ph.tiles + (t + 1))
                        q, kk = slice(t * P, (t + 1) * P), slice(tt * P, (tt + 1) * P)
                        nc.vector.tensor_tensor(m.q_lo[:, :, q], Y[:, 0, :].rearrange("p (h q) -> p h q", q=P),
                                                m.q_hi[:, :, q].bitcast(F32), ALU.subtract)
                        nc.vector.scalar_tensor_tensor(m.k_lo[:, kk], Y[:, 1, 0:P], HD3 ** -0.5, m.k_hi[:, kk].bitcast(F32),
                                                       ALU.mult, ALU.subtract).then_inc(ph.sem("k_out"), 1)

                    def maximum(u, q):
                        row = u * HT + q
                        dve.wait_ge(ph.sem("scores"), ph.rows + (row + 1))
                        nc.vector.tensor_reduce(m.nmax[:, row % 8:row % 8 + 1], bank(row % 2)[:, 0:(qt * HT + q + 1) * P], AX, ALU.max,
                                                negate=True).then_inc(ph.sem("nmax"), 1)

                    def inverse(row):
                        dve.wait_ge(ph.sem("exp"), ph.rows + (row + 1))
                        nc.vector.reciprocal(m.rinv[:, row % 8:row % 8 + 1], m.rsum[:, row % 8:row % 8 + 1]).then_inc(ph.sem("rinv"), 1)
                        dve.wait_ge(ph.sem("rinv"), ph.rows + (row + 1))
                        v = m.prob[row // HT % 2][:, row % HT, 0:(qt * HT + row % HT + 1) * P]
                        nc.vector.tensor_scalar(v, v, m.rinv[:, row % 8:row % 8 + 1], None, ALU.mult).then_inc(ph.sem("norm"), 1)

                    def lower(u, j):
                        b = u * ph.nkb + j
                        dve.wait_ge(ph.sem("pt_hi"), ph.blocks + (b + 1))
                        q = slice(ph.cols(j), HALF)
                        nc.vector.tensor_tensor(m.pt_lo[b % 2][:, q], Y[:, b % 2, q], m.pt_hi[b % 2][:, q].bitcast(F32), ALU.subtract)\
                            .then_inc(ph.sem("pt_lo"), 1)

                    def out_lo(u):
                        i, n = (u, ph.units + (u + 1)) if c.kind == ATT3 else (0, ph.no + 1)
                        dve.wait_ge(ph.sem("o_hi"), n)
                        nc.vector.tensor_tensor(m.o_lo[:, i, :], Y[:, 2 + i % 2, :], m.o_hi[:, i, :].bitcast(F32), ALU.subtract)\
                            .then_inc(ph.sem("o_lo"), 1)

                    proj, turned = (project1, turned1) if c.kind == ATT1 else (project3, turned3)
                    proj(0)
                    for t in range(HT):
                        if t + 1 < HT:
                            proj(t + 1)
                        turned(t)
                    done = 0
                    for q in range(HT):
                        maximum(0, q)
                        if q:
                            inverse(q - 1)
                    inverse(HT - 1)
                    for u in range(m.heads):
                        for q in range(HT):
                            row = (u + 1) * HT + q
                            if u + 1 < m.heads:
                                maximum(u + 1, q)
                                if q:
                                    inverse(row - 1)
                            if u + 1 < m.heads and q == HT - 1:
                                inverse(row)
                            for j in ph.share(u, q):
                                lower(u, j)
                                if c.kind == ATT3 and u and j == 0:
                                    out_lo(u - 1)
                    out_lo(m.heads - 1)
                    for t in range(HT):
                        dve.wait_ge(ph.sem("wo"), ph.no * HT + (t + 1))
                        xs = x[:, qt * HT + t, :]
                        nc.vector.tensor_tensor(xs, Y[:, 2 + t % 2, :], xs, ALU.add).then_inc(sem("x_ready"), 1)

                with dve.Fori(0, m.groups) as g:
                    dve.wait_ge(sem("x_ready"), g * TT + c.xb)
                    phase(g, 0)
                    phase(g, 1)
                xc[0] += TT * m.groups

            dve.wait_ge(sem("x_loaded"), 16)
            for c in calls:
                if xc[0]:
                    dve.wait_ge(sem("x_ready"), xc[0])
                if c.kind in GROUPS:
                    for h in range(2):
                        turn_in(c.ts[h], c.lns[h], h)
                        turn(c.ts[h], h)
                    attention(c)
                    continue
                turn_in(c.ts[0], c.lns[0], c.half)
                turn(c.ts[0], c.half)
                dict(FFN0=gated_call, GATE0=gated_call, FFN1=ffn1_call, FFN2=ffn2_call, ATT2=att2_call, FFN3=ffn3_call)[c.kind](c)

        @block.tensor
        def _(pe):
            def turn(n, src=xn):
                for t in range(HT):
                    pe.wait_ge(sem("turn_in"), n * HT + t + 1)
                    if n * HT + t >= 2:
                        pe.wait_ge(sem("xt_lo"), n * HT + t - 1)
                    for k in range(KT):
                        ins = nc.tensor.transpose(W[:, t % 2, k * P:(k + 1) * P], src[:, t, k * P:(k + 1) * P], ident[:, :])
                    ins.then_inc(sem("turned"), 1)
                pe.wait_ge(sem("xt_lo"), (n + 1) * HT)

            def xt(half, k, lo=0, hi=HALF):
                return (xt_hi[:, k, half * HALF + lo:half * HALF + hi], xt_lo[:, k, half * HALF + lo:half * HALF + hi])

            def gated_call(c):
                steps, cb, after = gated(c)

                def up(i, j=None):
                    off = 0 if j is None else j
                    s, p = (cb + i) % 2, i % 2
                    pe.wait_ge(sem("w_lo_a"), off * 2 + (cb + i + 1))
                    if c.sb + i >= 2:
                        pe.wait_ge(sem("h"), off * 2 + (c.sb + i - 1))
                    if c.kind == GATE0 and i == 0:
                        pe.wait_ge(sem("gate_read"), c.n + 1)
                    for g in range(2):
                        for k in range(KT):
                            w = slice((g * KT + k) * P, (g * KT + k + 1) * P)
                            ins = mm3(W[:, 2 * p + g, :], w_hi[s][:, w], w_lo[s][:, w], *xt(c.half, k), k == 0, k == KT - 1)
                    ins.then_inc(sem("w_free_a"), 1)

                def down(i, j=None):
                    off = 0 if j is None else j
                    s, p = (cb + i) % 2, i % 2
                    pe.wait_ge(sem("w_lo_b"), off * 2 + (cb + i + 1))
                    pe.wait_ge(sem("h_lo"), off * 2 + (c.sb + i + 1))
                    last = i == steps - 1 and not after and j is None
                    for t in range(HT):
                        q = slice(t * P, (t + 1) * P)
                        ins = mm3(Y[:, t, :], h_hi[p][:, q], h_lo[p][:, q], w_hi[s][:, PA:CHUNK], w_lo[s][:, PA:CHUNK],
                                  i == 0 and c.kind == FFN0, last)
                    ins.then_inc(sem("w_free_b"), 1)

                def terms(chunk, lo, m, start, stop, signal):
                    s = chunk % 2
                    pe.wait_ge(sem("term_lo"), (ORDERS + 1) * c.n + m + 1)
                    for t in range(HT):
                        q = slice(t * P, (t + 1) * P)
                        ins = mm3(Y[:, t, :], term_hi[m][:, q], term_lo[m][:, q], w_hi[s][:, lo:lo + D], w_lo[s][:, lo:lo + D],
                                  start, stop)
                    if signal:
                        ins.then_inc(sem(signal), 1)

                if c.kind == GATE0:
                    s = (cb - 1) % 2
                    pe.wait_ge(sem("w_lo_a"), cb)
                    for g in range(2):
                        for k in range(KT):
                            w = slice((g * KT + k) * P, (g * KT + k + 1) * P)
                            ins = mm3(W[:, g, :], w_hi[s][:, w], w_lo[s][:, w], *xt(c.half, k), k == 0, k == KT - 1)
                    ins.then_inc(sem("w_free_a"), 1)
                up(0)
                if c.kind == GATE0:
                    pe.wait_ge(sem("w_lo_b"), cb)
                    terms(cb - 1, PA, 0, True, False, "w_free_b")
                up(1)
                down(0)
                with pe.Fori(0, (steps - 2) // 2) as j:
                    for a in range(2):
                        up(2 + a, j)
                        down(1 + a, j)
                down(steps - 1)
                if c.kind == GATE0:
                    for q in range(2):
                        chunk = cb + steps + q
                        pe.wait_ge(sem("w_lo_a"), chunk + 1)
                        terms(chunk, 0, 3 * q + 1, False, False, None)
                        terms(chunk, D, 3 * q + 2, False, False, "w_free_a")
                        pe.wait_ge(sem("w_lo_b"), chunk + 1)
                        terms(chunk, PA, 3 * q + 3, False, q == 1, "w_free_b")

            def parts(chunk, lo, hi, rows=P):
                s = chunk % 2
                return w_hi[s][0:rows, lo:hi], w_lo[s][0:rows, lo:hi]

            def ready(chunk, part):
                pe.wait_ge(sem(f"w_lo_{part}"), chunk + 1)

            def blk(t):
                return t * P, (t + 1) * P

            def ffn1_call(c):
                cb = c.cb
                for chunk, part, ks in ((cb, "a", (0, 1)), (cb, "b", (2,)), (cb + 1, "a", (3,))):
                    ready(chunk, part)
                    for t in range(HT):
                        for k in ks:
                            lo = PA if part == "b" else (k % 3) * D
                            ins = mm3(W[:, t, :], *xt(c.half, k, *blk(t)), *parts(chunk, lo, lo + D), k == 0, k == 3)
                    if chunk == cb:
                        ins.then_inc(sem(f"w_free_{part}"), 1)
                for t in range(HT):
                    for k in range(KT):
                        ins = mm3(Y[:, 0, t * P:(t + 1) * P], *xt(c.half, k, *blk(t)), *parts(cb + 1, D + k * P, D + (k + 1) * P),
                                  k == 0, k == KT - 1)
                ins.then_inc(sem("w_free_a"), 1)
                for chunk, part, ks in ((cb + 1, "b", (0,)), (cb + 2, "a", (1, 2)), (cb + 2, "b", (3,))):
                    ready(chunk, part)
                    for t in (1, 2, 3, 0):
                        if chunk == cb + 1 and t == 0:
                            pe.wait_ge(sem("h1_copied"), c.n + 1)
                        for k in ks:
                            lo = PA if part == "b" else (k - 1) * D
                            ins = mm3(Y[:, t, :], *xt(c.half, k, *blk(t)), *parts(chunk, lo, lo + D), k == 0, False)
                    ins.then_inc(sem(f"w_free_{part}"), 1)
                pe.wait_ge(sem("wh"), c.n + 1)
                for t in range(HT):
                    ins = nc.tensor.transpose(W[:, 0, t * P:(t + 1) * P],
                                              wh[:, t * EXP1:(t + 1) * EXP1, :].rearrange("p e r -> p (e r)"), ident[:, :])
                ins.then_inc(sem("wh_turned"), 1)
                ready(cb + 3, "a")
                pe.wait_ge(sem("wht_lo"), c.n + 1)
                for t in range(HT):
                    lo, hi = blk(t)
                    ins = mm3(Y[:, t, :], wht_hi[:, lo:hi], wht_lo[:, lo:hi], *parts(cb + 3, 0, D), False, True)
                ins.then_inc(sem("w_free_a"), 1)
                pe.wait_ge(sem("w_free_b"), cb + 3)
                pe.sem_inc(sem("w_free_b"), 1)

            def ffn2_call(c):
                pe.wait_ge(sem("chan_lo"), c.n // 2 + 1)
                for t in range(HT):
                    for k in range(KT):
                        w = slice(k * E2, (k + 1) * E2)
                        ins = mm3(W[:, 0, t * E2:(t + 1) * E2], *xt(c.half, k, *blk(t)), small2_hi[:, w], small2_lo[:, w],
                                  k == 0, k == KT - 1)
                ins.then_inc(sem("logits"), 1)
                pe.wait_ge(sem("route"), c.n + 1)
                for t in range(HT):
                    ins = nc.tensor.transpose(W[0:E2, 1, t * P:(t + 1) * P], route[:, t, :], ident[:, :])
                ins.then_inc(sem("route_turned"), 1)
                pe.wait_ge(sem("rt_lo"), c.n + 1)
                for t in range(HT):
                    lo, hi = blk(t)
                    mm3(W[:, t, :], rt_hi[0:E2, lo:hi], rt_lo[0:E2, lo:hi], chan_hi[0:E2, 0:D], chan_lo[0:E2, 0:D], True, True)\
                        .then_inc(sem("in_scale"), 1)
                turn(c.ts[1])
                for t in range(HT):
                    lo, hi = blk(t)
                    ins = mm3(W[:, t, :], rt_hi[0:E2, lo:hi], rt_lo[0:E2, lo:hi], chan_hi[0:E2, D:], chan_lo[0:E2, D:], True, True)
                ins.then_inc(sem("out_scale"), 1)
                for chunk, part, ks in ((c.cb, "a", (0, 1)), (c.cb, "b", (2,)), (c.cb + 1, "a", (3,))):
                    ready(chunk, part)
                    for t in range(HT):
                        for k in ks:
                            lo = PA if part == "b" else (k % 3) * D
                            x_hi, x_lo = xt(c.half, k, *blk(t))
                            w = w_hi[chunk % 2][:, lo:lo + D]
                            nc.tensor.matmul(Y[:, t, :], x_hi, w, start=k == 0, stop=False)
                            ins = nc.tensor.matmul(Y[:, t, :], x_lo, w, start=False, stop=k == 3)
                    ins.then_inc(sem(f"w_free_{part}"), 1)
                pe.wait_ge(sem("w_free_b"), c.cb + 1)
                pe.sem_inc(sem("w_free_b"), 1)

            def att2_call(c):
                cb = c.cb

                def transform(pieces, last):
                    for k, (chunk, part, lo, signal) in enumerate(pieces):
                        ready(chunk, part)
                        for f in range(4):
                            ins = mm3(Y[:, f, :], *parts(chunk, lo + f * P, lo + (f + 1) * P), *xt(c.half, k), k == 0, k == 3)
                        if signal:
                            ins.then_inc(sem(signal), 1)
                    return ins

                transform([(cb, "a", 0, None), (cb, "a", D, "w_free_a"), (cb, "b", PA, "w_free_b"), (cb + 1, "a", 0, "spectrum")], None)
                pe.wait_ge(sem("power_lo"), c.n + 1)
                for part, lo, f in (("a", D, 0), ("b", PA, 1)):
                    ready(cb + 1, part)
                    for t in range(HT):
                        q = slice(*blk(t))
                        ins = mm3(W[:, t, :], power_hi[:, f, q], power_lo[:, f, q], *parts(cb + 1, lo, lo + D), f == 0, False)
                    ins.then_inc(sem(f"w_free_{part}"), 1)
                ready(cb + 2, "a")
                for t in range(HT):
                    q = slice(*blk(t))
                    ins = mm3(W[:, t, :], nyq_hi[0:1, q], nyq_lo[0:1, q], *parts(cb + 2, 0, D, 1), False, True)
                ins.then_inc(sem("correlated"), 1)
                turn(c.ts[1])
                transform([(cb + 2, "a", D, "w_free_a"), (cb + 2, "b", PA, "w_free_b"), (cb + 3, "a", 0, None),
                           (cb + 3, "a", D, "w_free_a")], None)
                pe.wait_ge(sem("w_free_a"), cb + 4)
                pe.sem_inc(sem("spectrum"), 1)
                pe.wait_ge(sem("mix_lo"), c.n + 1)
                for f, (chunk, part, lo, signal) in enumerate([(cb + 3, "b", PA, 1), (cb + 4, "a", 0, 0), (cb + 4, "a", D, 1), (cb + 4, "b", PA, 1)]):
                    ready(chunk, part)
                    for t in range(HT):
                        q = slice(*blk(t))
                        ins = mm3(Y[:, t, :], mix_hi[:, f, q], mix_lo[:, f, q], *parts(chunk, lo, lo + D), f == 0, f == 3)
                    if signal:
                        ins.then_inc(sem(f"w_free_{part}"), 1)

            def ffn3_call(c):
                if c.first:
                    cb = c.cb
                    where = lambda k: ((cb, "a", 0), (cb, "a", D), (cb, "b", PA), (cb + 1, "a", 0), (cb + 1, "a", D), (cb + 1, "b", PA),
                                       (cb + 2, "a", 0), (cb + 2, "a", D))[k]
                    pe.wait_ge(sem("gmat_lo"), c.n // 2 + 1)
                    G = B3 * R3
                    for k in range(4):
                        chunk, part, lo = where(k)
                        ready(chunk, part)
                        for j in range(KT):
                            ins = mm3(W[:, j, 0:G], *parts(chunk, lo + j * P, lo + (j + 1) * P), gmat_hi[:, k * G:(k + 1) * G],
                                      gmat_lo[:, k * G:(k + 1) * G], k == 0, k == 3)
                        if k in (1, 2):
                            ins.then_inc(sem(f"w_free_{part}"), 1)
                    ins.then_inc(sem("eff"), 1)
                    for k in range(4):
                        chunk, part, lo = where(4 + k)
                        ready(chunk, part)
                        for g in range(2):
                            q = slice(k * G + g * P, k * G + (g + 1) * P)
                            ins = mm3(Y[:, g, :], gmat_hi[:, q], gmat_lo[:, q], *parts(chunk, lo, lo + D), k == 0, k == 3)
                        if k < 2:
                            ins.then_inc(sem(f"w_free_{part}"), 1)
                    ins.then_inc(sem("eff"), 1)
                    pe.wait_ge(sem("eff"), c.n + 2)
                    pe.sem_inc(sem("w_free_a"), 1)
                    pe.sem_inc(sem("w_free_b"), 1)
                    pe.wait_ge(sem("eff_lo"), c.n + 2)
                mb = c.mb
                ready(mb + 1, "a")
                hb = slice(c.half * P, (c.half + 1) * P)
                for k in range(KT):
                    mm3(W[:, 0, :], aeff_hi[:, k, hb], aeff_lo[:, k, hb], *xt(c.half, k), k == 0, k == 3)
                for k in range(KT):
                    lo = D + k * R3
                    ins = mm3(W[0:R3, 1, :], *parts(mb + 1, lo, lo + R3), *xt(c.half, k), k == 0, k == 3)
                ins.then_inc(sem("down3"), 1)
                for chunk, part, ks in ((mb, "a", (0, 1)), (mb, "b", (2,)), (mb + 1, "a", (3,))):
                    ready(chunk, part)
                    for t in range(HT):
                        for k in ks:
                            lo = PA if part == "b" else (k % 3) * D
                            ins = mm3(Y[:, t, :], *xt(c.half, k, *blk(t)), *parts(chunk, lo, lo + D), k == 0, False)
                    ins.then_inc(sem(f"w_free_{part}"), 1)
                ready(mb + 1, "b")
                pe.wait_ge(sem("h3_lo"), c.n + 1)
                for t in range(HT):
                    q = slice(*blk(t))
                    mm3(Y[:, t, :], h3_hi[:, q], h3_lo[:, q], beff_hi[:, c.half, :], beff_lo[:, c.half, :], False, False)
                    ins = mm3(Y[:, t, :], hs_hi[:, q], hs_lo[:, q], *parts(mb + 1, PA, CHUNK, R3), False, True)
                ins.then_inc(sem("w_free_b"), 1)

            def attention(c):
                m = att[c.kind]

                def phase(g, qt):
                    ph = Phase(c, g, qt)

                    def ready_(i):
                        for part in "ab":
                            pe.wait_ge(sem(f"w_lo_{part}"), ph.chunk + (i + 1))

                    def project(t):
                        s, tt = t % 2, qt * HT + t
                        if t >= 2:
                            pe.wait_ge(ph.sem("v_lo"), ph.tiles + (t - 1))
                        half, q = tt // HT, blk(tt % HT)
                        for k in range(KT):
                            if c.kind == ATT1:
                                w = parts(ph.chunk0, k * 384, (k + 1) * 384)
                                ins = mm3(W[:, 2 * s, 0:384], *xt(half, k, *q), *w, k == 0, k == KT - 1)
                            else:
                                lo = (k % 2) * 768
                                w = parts(ph.chunk0 + k // 2, lo, lo + D)
                                mm3(W[:, 2 * s, :], *xt(half, k, *q), *w, k == 0, k == KT - 1)
                                w = parts(ph.chunk0 + k // 2, lo + D, lo + 768)
                                ins = mm3(W[:, 2 * s + 1, 0:256], *xt(half, k, *q), *w, k == 0, k == KT - 1)
                        ins.then_inc(ph.sem("proj"), 1)

                    def turned(t):
                        if t:
                            pe.wait_ge(ph.sem("k_out"), ph.tiles + t)
                        if c.kind == ATT1:
                            if t:
                                pe.wait_ge(ph.sem("q_out"), ph.tiles + t)
                            pe.wait_ge(ph.sem("v_lo"), ph.tiles + (t + 1))
                            for b, src in ((0, m.q_parts[t % 2]), (1, m.k_parts[t % 2])):
                                v = src[:, :, :, :, :].rearrange("p h a b d -> p (h a b d)").bitcast(F32)
                                for i in range(4):
                                    ins = nc.tensor.transpose(Y[:, b, i * P:(i + 1) * P], v[:, i * P:(i + 1) * P], ident[:, :])
                        else:
                            pe.wait_ge(ph.sem("rot"), ph.tiles + (t + 1))
                            for h in range(m.heads + 1):
                                ins = nc.tensor.transpose(Y[:, h // 4, (h % 4) * P:(h % 4 + 1) * P], m.rot[t % 2][:, h, :], ident[:, :])
                        ins.then_inc(ph.sem("qk_turned"), 1)

                    def scores(u, q):
                        row, i = u * HT + q, qt * HT + q
                        if row >= 2:
                            pe.wait_ge(ph.sem("exp"), ph.rows + (row - 1))
                        s = row % 2
                        for b in range(i // 4 + 1):
                            lo, hi = b * D, min((i + 1) * P, (b + 1) * D)
                            out_ = W[:, 2 * s + b, 0:hi - lo]
                            diag = hi == (i + 1) * P
                            if c.kind == ATT1:
                                r = slice(64 * (u % 2), 64 * (u % 2) + 64)
                                nc.tensor.matmul(out_, m.q[r, u // 2, q * P:(q + 1) * P], m.k[r, u // 2, lo:hi], start=True, stop=not diag)
                            else:
                                qq = slice(q * P, (q + 1) * P)
                                mm3(out_, m.q_hi[:, u, qq], m.q_lo[:, u, qq], m.k_hi[:, lo:hi], m.k_lo[:, lo:hi], True, not diag)
                        nc.tensor.matmul(W[:, 2 * s + b, i * P - lo:hi - lo], ident_r[:, :], mask_r[:, :], start=False, stop=True)\
                            .then_inc(ph.sem("scores"), 1)

                    def turn_p(u, j):
                        b = u * ph.nkb + j
                        if j == 0:
                            pe.wait_ge(ph.sem("norm"), ph.rows + (u + 1) * HT)
                        if b >= 2:
                            pe.wait_ge(ph.sem("pt_lo"), ph.blocks + (b - 1))
                        for q in range(ph.cols(j) // P, HT):
                            ins = nc.tensor.transpose(Y[:, b % 2, q * P:(q + 1) * P], m.prob[u % 2][:, q, j * P:(j + 1) * P], ident[:, :])
                        ins.then_inc(ph.sem("p_turned"), 1)

                    def values(u, j):
                        b, lo = u * ph.nkb + j, ph.cols(j)
                        pe.wait_ge(ph.sem("pt_lo"), ph.blocks + (b + 1))
                        if c.kind == ATT1:
                            if j == 0:
                                pe.wait_ge(ph.sem("pad"), ph.units + (u + 1))
                            (v_hi, v_lo), out_ = m.v_pad[u % 2], Y[:, 2, lo:HALF]
                            start, stop = u == 0 and j == 0, u == m.heads - 1 and j == ph.nkb - 1
                        else:
                            if j == 0 and u >= 2:
                                pe.wait_ge(ph.sem("o_lo"), ph.units + (u - 1))
                            v_hi, v_lo, out_ = m.v_hi, m.v_lo, Y[:, 2 + u % 2, lo:HALF]
                            start, stop = j == 0, j == ph.nkb - 1
                        ins = mm3(out_, v_hi[:, j, :], v_lo[:, j, :], m.pt_hi[b % 2][:, lo:HALF], m.pt_lo[b % 2][:, lo:HALF], start, stop)
                        if j == ph.nkb - 1:
                            ins.then_inc(ph.sem("av"), 1)

                    ready_(0)
                    if c.kind == ATT3:
                        ready_(1)
                    project(0)
                    for t in range(HT):
                        if t + 1 < HT:
                            project(t + 1)
                        turned(t)
                    pe.wait_ge(ph.sem("proj"), ph.tiles + HT)
                    for i in range(2 if c.kind == ATT3 else 1):
                        for part in "ab":
                            pe.sem_inc(sem(f"w_free_{part}"), 1)
                    pe.wait_ge(ph.sem("k_out"), ph.tiles + HT)
                    if c.kind == ATT1:
                        pe.wait_ge(ph.sem("q_out"), ph.tiles + HT)
                    pe.wait_ge(ph.sem("v_lo"), ph.tiles + HT)
                    pe.wait_ge(sem("x_ready"), ph.x)
                    for q in range(HT):
                        scores(0, q)
                    last = None
                    for u in range(m.heads):
                        for q in range(HT):
                            if u + 1 < m.heads:
                                scores(u + 1, q)
                            for j in ph.share(u, q):
                                turn_p(u, j)
                                if last:
                                    values(*last)
                                last = (u, j)
                    values(*last)
                    pe.wait_ge(ph.sem("o_lo"), ph.units + m.heads if c.kind == ATT3 else ph.no + 1)
                    first = 2 if c.kind == ATT3 else 1
                    for i in range(first, m.ch):
                        ready_(i)
                    for t in range(HT):
                        if t >= 2:
                            pe.wait_ge(sem("x_ready"), ph.x + (t - 1))
                        n = m.heads if c.kind == ATT3 else 1
                        for h in range(n):
                            w = parts(ph.chunk0 + first + h // 3, (h % 3) * D, (h % 3 + 1) * D)
                            ins = mm3(Y[:, 2 + t % 2, :], m.o_hi[:, h, t * P:(t + 1) * P], m.o_lo[:, h, t * P:(t + 1) * P], *w, h == 0, h == n - 1)
                        ins.then_inc(ph.sem("wo"), 1)
                    pe.wait_ge(ph.sem("wo"), ph.no * HT + HT)
                    for i in range(first, m.ch):
                        for part in "ab":
                            pe.sem_inc(sem(f"w_free_{part}"), 1)

                with pe.Fori(0, m.groups) as g:
                    phase(g, 0)
                    phase(g, 1)

            pe.wait_ge(sem("const_r"), 1)
            pe.wait_ge(sem("const"), 16 * 5 if kinds & {FFN0, GATE0} else 32)
            for c in calls:
                if c.kind in GROUPS:
                    turn(c.ts[0])
                    turn(c.ts[1])
                    attention(c)
                    continue
                turn(c.ts[0])
                if c.xb:
                    pe.wait_ge(sem("x_ready"), c.xb)
                dict(FFN0=gated_call, GATE0=gated_call, FFN1=ffn1_call, FFN2=ffn2_call, ATT2=att2_call, FFN3=ffn3_call)[c.kind](c)


def _tiles(w):
    n = w.shape[0] // P
    return w.reshape(n, P, KT, P).transpose(0, 3, 2, 1)


def _pad_rows(w, n):
    return np.concatenate([w, np.zeros((n - w.shape[0],) + w.shape[1:], w.dtype)], 0)


def rope_tables():
    inv = 1.0 / 500000.0 ** (np.arange(0, HD3, 2, dtype=np.float32) / HD3)
    wavelen = 2.0 * np.pi / inv
    smooth = (1024 / wavelen - 1.0) / (4.0 - 1.0)
    medium = (wavelen <= 1024) & (wavelen >= 256)
    freq = np.where(medium, (1.0 - smooth) / 8.0 * inv + smooth * inv, np.where(wavelen > 1024, inv / 8.0, inv)).astype(np.float32)
    angle = np.arange(T, dtype=np.float32)[:, None] * freq[None, :]
    return np.cos(angle.astype(np.float64)).astype(np.float32), np.sin(angle.astype(np.float64)).astype(np.float32)


def layout(i):
    f = lambda name: np.asarray(i[name])
    out = []
    w1, w3 = _tiles(f("L0_ffn_w1")), _tiles(f("L0_ffn_w3"))
    w2 = f("L0_ffn_w2").T.reshape(F0_STEPS, P, D)
    out.append(np.concatenate([w1.reshape(F0_STEPS, P, D), w3.reshape(F0_STEPS, P, D), w2], 2))
    up, gate = _tiles(f("L0_attn_up_w"))[0].reshape(P, D), _tiles(f("L0_attn_gate_w"))[0].reshape(P, D)
    out.append(np.concatenate([up, gate, f("L0_attn_local_approx_output").T], 1)[None])
    n = G0_STEPS * P
    fg, fu = (_tiles(_pad_rows(f(f"L0_attn_ffn_{q}_w"), n)).reshape(G0_STEPS, P, D) for q in ("gate", "up"))
    fd = _pad_rows(f("L0_attn_ffn_down_w").T, n).reshape(G0_STEPS, P, D)
    out.append(np.concatenate([fg, fu, fd], 2))
    fuse = f("L0_attn_fuse_weight").transpose(1, 2, 0).reshape(P, 2, CHUNK).transpose(1, 0, 2)
    out.append(fuse)
    zeros = np.zeros((P, D), np.float32)
    kt = lambda w: [w.T[k * P:(k + 1) * P] for k in range(KT)]

    def pack(units):
        units = [np.pad(u, ((0, P - u.shape[0]), (0, D - u.shape[1]))) for u in units]
        units += [zeros] * (-len(units) % 3)
        return np.stack([np.concatenate(units[n:n + 3], 1) for n in range(0, len(units), 3)])

    qk = kt(np.concatenate([f("L1_ffn_Wq"), f("L1_ffn_Wk")], 0))
    down = np.concatenate(kt(f("L1_ffn_A").reshape(EXP1 * RANK1, D)), 1)
    out.append(pack(qk + [down] + kt(f("L1_ffn_W")) + [f("L1_ffn_Bm").transpose(0, 2, 1).reshape(EXP1 * RANK1, D)]))
    for g in range(GROUPS[ATT1]):
        rows_ = slice(g * P, (g + 1) * P)
        out.append(np.concatenate(kt(np.concatenate([f(f"L1_attn_W{q}")[rows_] for q in "qkv"], 0)), 1)[None])
        out.append(pack([f("L1_attn_Wo").T[rows_]]))
    out.append(pack(kt(f("L2_ffn_weight"))))
    lag, freq = np.arange(D), np.arange(D // 2)
    angle = lambda k: 2 * np.pi * (np.outer(lag, k) % D) / D
    fwd = np.concatenate([np.cos(angle(freq)), np.sin(angle(freq))], 1)
    top = np.cos(angle(np.array([D // 2])))[:, 0]
    fwd[:, D // 2] = top
    twice = np.where(freq == 0, 1.0, 2.0)[:, None] / D
    inv_cos, inv_sin = twice * np.cos(angle(freq)).T, -twice * np.sin(angle(freq)).T
    inv_sin[0] = top / D
    rows = lambda m: [m[k * P:(k + 1) * P].astype(np.float32) for k in range(m.shape[0] // P)]
    out.append(pack(rows(fwd) + rows(inv_cos) + [(top / D)[None].astype(np.float32)] + rows(fwd) + rows(inv_cos) + rows(inv_sin)))
    lora_a = f("L3_ffn_lora_A").reshape(NL3 * R3, D)
    lora_b = f("L3_ffn_lora_B").transpose(0, 2, 1).reshape(NL3 * R3, D)
    tiles = lambda w: [w[k * P:(k + 1) * P] for k in range(w.shape[0] // P)]
    out.append(pack(tiles(lora_a) + tiles(lora_b)))
    shared = np.concatenate(kt(f("L3_ffn_lora_A_shared")), 1)
    out.append(pack(tiles(f("L3_ffn_kernel")) + [shared, f("L3_ffn_lora_B_shared").T]))
    for g in range(KV3):
        n = H3 // KV3 * HD3
        qkv = kt(np.concatenate([f("L3_attn_Wq")[g * n:(g + 1) * n]] + [f(f"L3_attn_W{q}")[g * HD3:(g + 1) * HD3] for q in "kv"], 0))
        out += [np.concatenate(qkv[0:2], 1)[None], np.concatenate(qkv[2:4], 1)[None]]
        out.append(pack(tiles(f("L3_attn_Wo").T[g * n:(g + 1) * n])))
    rest = N_DRAM_CHUNKS - sum(o.shape[0] for o in out)
    arrays = {"ident": np.eye(P, dtype=np.float32)}
    s1, s3, s2 = f("L0_ffn_w1_scale"), f("L0_ffn_w3_scale"), f("L0_ffn_w2_scale").T
    arrays["scales"] = np.concatenate([s1, s3, s2], 1)
    arrays["local_point"] = f("L0_attn_local_point").reshape(P, 1)
    arrays["discount"] = f("L0_attn_discount_factor").reshape(1, ORDERS)
    arrays["ffn1_b"], arrays["ffn2_b"], arrays["ffn3_b"] = (f(f"L{n}_ffn_{q}").reshape(1, D) for n, q in ((1, "b"), (2, "bias"), (3, "bias")))
    arrays["router"] = np.concatenate(kt(f("L2_ffn_gate_w")), 1)
    arrays["channel"] = np.concatenate([f("L2_ffn_in_channel_scale"), f("L2_ffn_out_channel_scale")], 1)
    g = f("L3_ffn_gate").T.reshape(4, 4, 1, B3)
    arrays["gate_rep"] = np.broadcast_to(g, (4, 4, R3, B3)).transpose(1, 2, 0, 3).reshape(P, 4 * B3)
    arrays["same_rank"] = np.tile(np.eye(R3, dtype=np.float32), (4, 1))
    arrays["own_block"] = np.kron(np.eye(4, dtype=np.float32), np.ones((R3, P), np.float32))
    arrays["mask"] = np.triu(np.full((P, P), NEG, np.float32), 1)
    qkv_b = np.stack([f(f"L1_attn_b{q}").reshape(GROUPS[ATT1], P) for q in "qkv"], 1)
    arrays["att1_qkv_b"], arrays["att1_o_b"] = qkv_b.reshape(1, 3 * D), f("L1_attn_bo").reshape(1, D)
    cos, sin = rope_tables()
    arrays["rope_cos"], arrays["rope_sin"] = (q.reshape(TT, P, HD3 // 2).transpose(1, 0, 2) for q in (cos, sin))
    if rest:
        out.append(np.zeros((rest, P, CHUNK), np.float32))
    arrays["weights"] = np.concatenate(out, 0)
    assert arrays["weights"].shape[0] == N_DRAM_CHUNKS
    return {k: np.ascontiguousarray(v) for k, v in arrays.items()}


def kernel(**inputs):
    import concourse.bacc as bacc
    from concourse.bass_utils import run_bass_kernel_spmd

    nc = bacc.Bacc("TRN2", target_bir_lowering=False, num_devices=1)
    hidden = np.ascontiguousarray(np.asarray(inputs["L0_attn_hidden_states"]).reshape(T, D))
    arrays = {f"in_{name}": a for name, a in layout(inputs).items()}
    arrays["in_x"] = hidden
    aps = {name: nc.dram_tensor(name, a.shape, mybir.dt.from_np(a.dtype), kind="ExternalInput").ap() for name, a in arrays.items()}
    out = nc.dram_tensor("out", (T, D), F32, kind="ExternalOutput").ap()
    x_in = aps.pop("in_x")
    build(nc, {name[3:]: ap for name, ap in aps.items()}, x_in, out)
    got = run_bass_kernel_spmd(nc, [arrays], core_ids=[0])
    return got.results[0]["out"].reshape(1, T, D)
```

```python
import numpy as np
import concourse.bass as bass
from concourse import mybir

F32 = mybir.dt.float32
F32R = mybir.dt.float32r
ALU = mybir.AluOpType
ACT = mybir.ActivationFunctionType
AX = mybir.AxisListType.X

P = 128
T = 1024
D = 512
TT = T // P
KT = D // P
HT = TT // 2
HALF = T // 2
CHUNK = 3 * D
PA = 2 * D
EPS = 1e-5

FFN0, GATE0, FFN1, ATT1, FFN2, ATT2, FFN3, ATT3 = "FFN0 GATE0 FFN1 ATT1 FFN2 ATT2 FFN3 ATT3".split()
ORDER = [FFN0, GATE0, FFN0, FFN1, ATT1, FFN1, FFN2, ATT2, FFN2, FFN3, ATT3, FFN3]

F0_STEPS = 1792 // P
G0_STEPS = -(-1248 // P)
ORDERS = 6
THD = 2.5
EXP1, DK1, RANK1 = 8, 32, 16
H1, HD1 = 32, 16
E2 = 8
TOPK = int(np.log(D))
H3, KV3, HD3 = 32, 8, 128
NL3, R3, B3 = 16, 32, 8
GROUPS = {ATT1: 4, ATT3: 8}
AHEAD = HT + 2
PT_SLOTS = 3
AV = 3
NEG = -1e30
BIG, NONE = 1e30, -3e38

CHUNKS = {FFN0: F0_STEPS, GATE0: G0_STEPS + 3, FFN1: 4, ATT1: 2, FFN2: 2, ATT2: 5, FFN3: 2, ATT3: 4}
EFF_CHUNKS = 3


def chunk_bases():
    base, at = {}, 0
    for kind in (FFN0, GATE0, FFN1, ATT1, FFN2, ATT2, FFN3, ATT3):
        base[kind] = at
        at += CHUNKS[kind] * (GROUPS.get(kind, 1)) + (EFF_CHUNKS if kind == FFN3 else 0)
    return base, at


DRAM_BASE, N_DRAM_CHUNKS = chunk_bases()


class Call:
    pass


def kind_is_halved(c):
    return c.kind not in GROUPS


def plan(layers):
    calls, chunks = [], []
    xb = steps = t_runs = lns = 0
    for n, kind in enumerate(layers):
        halves = [None] if kind in GROUPS else [0, 1]
        for half in halves:
            c = Call()
            c.kind, c.half, c.first = kind, half, half in (0, None)
            c.xb = xb
            c.sb = steps
            c.cb = len(chunks)
            c.n = sum(1 for q in calls if q.kind == kind)
            base = DRAM_BASE[kind]
            if kind in GROUPS:
                c.lns = [lns, lns + 1]
                lns += 2
                c.ts = [t_runs, t_runs + 1]
                t_runs += 2
                chunks += [(base + g * CHUNKS[kind] + i, False, False) for g in range(GROUPS[kind])
                           for i in range(CHUNKS[kind])]
                xb += TT * GROUPS[kind]
            else:
                c.lns = [lns]
                lns += 1
                if kind == FFN3:
                    if half == 0:
                        chunks += [(base + i, False, False) for i in range(EFF_CHUNKS)]
                    base += EFF_CHUNKS
                c.mb = len(chunks)
                chunks += [(base + i, kind == FFN0, kind == FFN2) for i in range(CHUNKS[kind])]
                c.ts = [t_runs + i for i in range(2 if kind in (FFN2, ATT2) else 1)]
                t_runs += len(c.ts)
                xb += HT
                steps += {FFN0: F0_STEPS, GATE0: G0_STEPS}.get(kind, 0)
            calls.append(c)
    for c, after in zip(calls, calls[1:] + [None]):
        c.next = after
        c.prepares = after is not None and kind_is_halved(c)
    return calls, chunks, xb


class Chain:

    def __init__(self, eng, sem):
        self.eng, self.sem, self.value = eng, sem, 0

    def sig(self, ins):
        ins.then_inc(self.sem, 1)
        self.value = self.value + 1

    def wait(self):
        self.eng.wait_ge(self.sem, self.value)

    def link(self, ins):
        self.sig(ins)
        self.wait()

    def enter(self, j, per_turn):
        self.start, self.per_turn = self.value, per_turn
        self.value = j * per_turn + self.start
        self.turn = self.value

    def leave(self, turns, used):
        assert used == self.per_turn, (used, self.per_turn)
        self.value = self.start + turns * self.per_turn


def build(nc, inp, x_in, out, layers=ORDER):
    calls, chunks, x_total = plan(layers)
    kinds = set(layers)
    sems = {}

    def sem(name):
        if name not in sems:
            sems[name] = nc.alloc_semaphore(name)
        return sems[name]

    top = [16512]

    def keep(name, shape, dtype=F32):
        size = int(np.prod(shape[1:])) * 4
        t = nc.alloc_sbuf_tensor_at(name, shape, dtype, offset=top[0])
        top[0] += -(-size // 32) * 32
        return t

    x = keep("x", [P, TT, D])
    xt_hi = keep("xt_hi", [P, KT, T], F32R)
    xt_lo = keep("xt_lo", [P, KT, T], F32R)
    XN_AT = top[0]
    xn = keep("xn", [P, HT, D])
    raw = keep("raw", [P, 2, CHUNK])
    w_hi = [keep(f"w_hi{s}", [P, CHUNK], F32R) for s in range(2)]
    w_lo = [keep(f"w_lo{s}", [P, CHUNK], F32R) for s in range(2)]
    ident = keep("ident", [P, P])
    stats = keep("stats", [P, HT, 6])
    mv = keep("mv", [P, HT, 2])
    var_eps = keep("var_eps", [P, HT])
    rstd = keep("rstd", [P, HT])
    ident_r = keep("ident_r", [P, P], F32R)
    mask = keep("mask", [P, P])
    mask_r = keep("mask_r", [P, P], F32R)
    minus_half = keep("minus_half", [P, HT])
    ARENA = top[0]
    SBUF_END = 229344

    class Arena:

        def __init__(self, tag):
            self.tag, self.at = tag, ARENA

        def __call__(self, name, shape, dtype=F32):
            size = int(np.prod(shape[1:])) * 4
            t = nc.alloc_sbuf_tensor_at(f"{self.tag}_{name}", shape, dtype, offset=self.at)
            self.at += -(-size // 32) * 32
            assert self.at <= SBUF_END, (self.tag, name, self.at - SBUF_END)
            return t

    a = Arena("g")
    s_buf = a("s_buf", [P, 2, D])
    h_buf = a("h_buf", [P, 2, D])
    h_hi = [a(f"h_hi{p}", [P, D], F32R) for p in range(2)]
    h_lo = [a(f"h_lo{p}", [P, D], F32R) for p in range(2)]
    scales = a("scales", [P, F0_STEPS, 3 * KT])
    lpoint = a("lpoint", [P, 1])
    coef = a("coef", [P, ORDERS])
    delta = a("delta", [P, D])
    near = a("near", [P, D])
    term = a("term", [P, ORDERS + 1, D])
    term_hi = [a(f"term_hi{m}", [P, D], F32R) for m in range(ORDERS + 1)]
    term_lo = [a(f"term_lo{m}", [P, D], F32R) for m in range(ORDERS + 1)]

    a = Arena("f1")
    bias1 = a("bias", [P, D])
    q_sb = a("q_sb", [P, HT, EXP1 * DK1])
    h1 = a("h1", [P, HT * EXP1, RANK1])
    prod = a("prod", [P, HT * EXP1, DK1])
    score1 = a("score1", [P, HT, EXP1])
    top1 = a("top1", [P, HT])
    soft1 = a("soft1", [P, HT, EXP1])
    wh = a("wh", [P, HT * EXP1, RANK1])
    wht_hi = a("wht_hi", [P, HALF], F32R)
    wht_lo = a("wht_lo", [P, HALF], F32R)

    a = Arena("f2")
    bias2 = a("bias", [P, D])
    small2 = a("small", [P, KT * E2])
    small2_hi = a("small_hi", [P, KT * E2], F32R)
    small2_lo = a("small_lo", [P, KT * E2], F32R)
    chan = a("chan", [P, 2 * D])
    chan_hi = a("chan_hi", [P, 2 * D], F32R)
    chan_lo = a("chan_lo", [P, 2 * D], F32R)
    logit = a("logit", [P, HT, E2])
    top2 = a("top2", [P, HT])
    route = a("route", [P, HT, E2])
    rt_hi = a("rt_hi", [P, HALF], F32R)
    rt_lo = a("rt_lo", [P, HALF], F32R)
    out_sc = a("out_sc", [P, HT, D])
    scaled_y = a("scaled_y", [P, HT, D])

    a = Arena("a2")
    spec = a("spec", [P, 4, HALF])
    sq = a("sq", [P, 4, HALF])
    power_hi = a("power_hi", [P, 2, HALF], F32R)
    power_lo = a("power_lo", [P, 2, HALF], F32R)
    power_sum = a("power_sum", [P, 2, HALF])
    nyq_hi = a("nyq_hi", [P, HALF], F32R)
    nyq_lo = a("nyq_lo", [P, HALF], F32R)
    corr = a("corr", [P, HT, D + 8])
    marked = a("marked", [P, HT, D + 8])
    ex2 = a("ex2", [P, HT, D])
    top8 = a("top8", [P, HT, 8])
    nmax2 = a("nmax2", [P, HT])
    sum2 = a("sum2", [P, HT])
    cross = a("cross", [P, 4, HALF])
    mix = a("mix", [P, 4, HALF])
    mix_hi = a("mix_hi", [P, 4, HALF], F32R)
    mix_lo = a("mix_lo", [P, 4, HALF], F32R)

    a = Arena("f3")
    bias3 = a("bias", [P, D])
    gate_rep = a("gate_rep", [P, 4 * B3])
    same_rank = a("same_rank", [P, R3])
    own_block = a("own_block", [P, HALF])
    gmat = a("gmat", [P, 4 * B3, R3])
    gmat_hi = a("gmat_hi", [P, 4 * B3 * R3], F32R)
    gmat_lo = a("gmat_lo", [P, 4 * B3 * R3], F32R)
    aeff_hi = a("aeff_hi", [P, KT, B3 * R3], F32R)
    aeff_lo = a("aeff_lo", [P, KT, B3 * R3], F32R)
    beff_hi = a("beff_hi", [P, 2, D], F32R)
    beff_lo = a("beff_lo", [P, 2, D], F32R)
    h3 = a("h3", [P, HALF])
    h3_hi = a("h3_hi", [P, HALF], F32R)
    h3_lo = a("h3_lo", [P, HALF], F32R)
    hs_hi = a("hs_hi", [R3, HALF], F32R)
    hs_lo = a("hs_lo", [R3, HALF], F32R)

    att = {}
    for kind, tag in ((ATT1, "a1"), (ATT3, "a3")):
        a, m = Arena(tag), Call()
        att[kind] = m
        m.tag, m.kind, m.ch = tag, kind, CHUNKS[kind]
        m.heads = {ATT1: H1, ATT3: H3}[kind] // GROUPS[kind]
        m.groups = GROUPS[kind]
        m.prob_at = [sum(HT + i + 1 for i in range(q)) * P for q in range(HT)]
        m.prob = [a(f"prob{i}", [P, m.prob_at[-1] + T]) for i in range(2)]
        if kind == ATT1:
            m.w_hi, m.w_lo = w_hi, w_lo
        else:
            m.w_hi = w_hi + [a(f"w_hi{s}", [P, CHUNK], F32R) for s in (2, 3)]
            m.w_lo = w_lo + [a(f"w_lo{s}", [P, CHUNK], F32R) for s in (2, 3)]
        m.pt_hi = [a(f"pt_hi{i}", [P, HALF], F32R) for i in range(PT_SLOTS)]
        m.pt_lo = [a(f"pt_lo{i}", [P, HALF], F32R) for i in range(PT_SLOTS)]
        m.nmax = a("nmax", [P, 8])
        m.rsum = a("rsum", [P, 8])
        m.rinv = a("rinv", [P, 8])
        m.v_hi = a("v_hi", [P, TT, P], F32R)
        m.v_lo = a("v_lo", [P, TT, P], F32R)
        if kind == ATT1:
            m.qkv = a("qkv", [P, 2, 3, m.heads, HD1])
            m.bias_qkv = a("bias_qkv", [P, m.groups, 3 * m.heads * HD1])
            m.bias_o = a("bias_o", [P, D])
            m.q_parts = [a(f"q_parts{i}", [P, m.heads, 2, 2, HD1], F32R) for i in range(2)]
            m.k_parts = [a(f"k_parts{i}", [P, m.heads, 2, 2, HD1], F32R) for i in range(2)]
            m.q = a("q", [P, m.heads // 2, HALF], F32R)
            m.k = a("k", [P, m.heads // 2, T], F32R)
            m.v_pad = [[a(f"v_pad_{q}{i}", [P, TT, P], F32R) for q in ("hi", "lo")] for i in range(2)]
            m.zero = a("zero", [P, TT, HD1])
            m.o_hi = a("o_hi", [P, 1, HALF], F32R)
            m.o_lo = a("o_lo", [P, 1, HALF], F32R)
        else:
            m.cos = a("cos", [P, TT, HD3 // 2])
            m.sin = a("sin", [P, TT, HD3 // 2])
            m.by_sin = a("by_sin", [P, 2 * (m.heads + 1), HD3 // 2])
            m.o_raw = m.by_sin[:, :, :].rearrange("p h d -> p (h d)")[:, 0:HALF]
            m.rot = [a(f"rot{i}", [P, m.heads + 1, HD3]) for i in range(2)]
            m.q_hi = a("q_hi", [P, m.heads, HALF], F32R)
            m.q_lo = a("q_lo", [P, m.heads, HALF], F32R)
            m.k_hi = a("k_hi", [P, T], F32R)
            m.k_lo = a("k_lo", [P, T], F32R)
            m.o_hi = nc.alloc_sbuf_tensor_at("a3_o_hi", [P, m.heads, HALF], F32R, offset=XN_AT)
            m.o_lo = a("o_lo", [P, m.heads, HALF], F32R)

    Y = nc.alloc_psum_tensor("Y", [P, 4, D], F32)
    W = nc.alloc_psum_tensor("W", [P, 4, D], F32)

    def mm3(o, a_hi, a_lo, b_hi, b_lo, start, stop):
        nc.tensor.matmul(o, a_hi, b_hi, start=start, stop=False)
        nc.tensor.matmul(o, a_lo, b_hi, start=False, stop=False)
        return nc.tensor.matmul(o, a_hi, b_lo, start=False, stop=stop)

    def gated(c):
        if c.kind == FFN0:
            return F0_STEPS, c.cb, 0
        return G0_STEPS, c.cb + 1, 2

    aux = {
        FFN1: [(bias1[:, :], inp["ffn1_b"].broadcast_to((P, D)))],
        FFN2: [(bias2[:, :], inp["ffn2_b"].broadcast_to((P, D))), (small2[:, :], inp["router"]),
               (chan[0:E2, :], inp["channel"])],
        FFN3: [(bias3[:, :], inp["ffn3_b"].broadcast_to((P, D))), (gate_rep[:, :], inp["gate_rep"]),
               (same_rank[:, :], inp["same_rank"]), (own_block[:, :], inp["own_block"])],
    }
    aux[ATT1] = [(att[ATT1].bias_qkv[:, :, :].rearrange("p g c -> p (g c)"), inp["att1_qkv_b"].broadcast_to((P, 3 * D))),
                 (att[ATT1].bias_o[:, :], inp["att1_o_b"].broadcast_to((P, D)))]
    aux[ATT3] = [(att[ATT3].cos[:, :, :], inp["rope_cos"]), (att[ATT3].sin[:, :, :], inp["rope_sin"])]
    aux_total = 0
    for q in calls:
        if q.first:
            aux_total += 16 * len(aux.get(q.kind, []))
        q.aux = aux_total

    class Phase:

        def __init__(self, c, g, qt):
            m = self.m = att[c.kind]
            self.c, self.g, self.qt = c, g, qt
            self.nkb = (qt + 1) * HT
            per = 2 * m.heads * HT
            self.tiles = g * TT + qt * HT
            self.rows = g * per + qt * m.heads * HT
            self.blocks = g * (3 * m.heads * HT) + qt * m.heads * HT
            self.units = g * (2 * m.heads) + qt * m.heads
            self.chunk = g * m.ch + c.cb
            self.no = g * 2 + qt
            self.x = g * TT + (c.xb + qt * HT)

        def sem(self, name):
            return sem(f"{self.m.tag}_{name}")

        def steps(self):
            for u in range(self.m.heads):
                for q in range(HT):
                    row = lambda n: divmod(n, HT) if n < self.m.heads * HT else None
                    keys = [(u, j) for j in range(q * self.nkb // HT, (q + 1) * self.nkb // HT)]
                    yield u, q, keys, row(u * HT + q + AHEAD), row(u * HT + q + AHEAD - 1)

        def w_slot(self, i):
            return (self.c.cb + i) % 2 + (2 if 2 <= i < self.m.ch else 0)

        def row(self, u, q, lo=0, hi=None):
            hi = (self.qt * HT + q + 1) * P if hi is None else hi
            return self.m.prob[u % 2][:, self.m.prob_at[q] + lo:self.m.prob_at[q] + hi]

        def cols(self, j):
            return max(0, j - self.qt * HT) * P

    def tok(half, t):
        return half * HALF + t * P

    with nc.Block() as block:

        @block.sync
        def _(sp):
            def load(c, dram, slot):
                if not isinstance(c, int) or c >= 2:
                    sp.wait_ge(sem("w_lo_b"), c - 1)
                sp.dma_start(raw[:, slot, :], inp["weights"][dram]).then_inc(sem(f"raw{slot}"), 16)

            x_tiles = x_in.rearrange("(t p) d -> p t d", p=P)
            sp.dma_start(x[:, 0:HT, :], x_tiles[:, 0:HT, :]).then_inc(sem("x_loaded_0"), 16)
            sp.dma_start(ident[:, :], inp["ident"]).then_inc(sem("const"), 16)
            sp.dma_start(mask[:, :], inp["mask"]).then_inc(sem("const"), 16)
            if kinds & {FFN0, GATE0}:
                sp.dma_start(scales[:, :, :], inp["scales"].rearrange("(a s) k -> a s k", a=1).broadcast_to((P, F0_STEPS, 12))).then_inc(sem("const"), 16)
                sp.dma_start(lpoint[:, :], inp["local_point"]).then_inc(sem("const"), 16)
                sp.dma_start(coef[:, :], inp["discount"].broadcast_to((P, ORDERS))).then_inc(sem("const"), 16)
            load(0, chunks[0][0], 0)
            sp.dma_start(x[:, HT:TT, :], x_tiles[:, HT:TT, :]).then_inc(sem("x_loaded_1"), 16)
            at_aux = {q.cb + 1: q for q in calls if q.first and aux.get(q.kind)}

            def load_aux(n):
                if n in at_aux:
                    q = at_aux.pop(n)
                    if q.xb:
                        sp.wait_ge(sem("x_ready"), q.xb)
                    for dst, src in aux[q.kind]:
                        sp.dma_start(dst, src).then_inc(sem("aux"), 16)

            n = 1
            grouped = {q.cb: q for q in calls if q.kind in GROUPS}
            while n < len(chunks):
                m = n
                if n in grouped:
                    q = grouped[n]
                    per, first, groups = CHUNKS[q.kind], chunks[n][0], GROUPS[q.kind]
                    load(n, first, n % 2)
                    if q.xb:
                        sp.wait_ge(sem("x_ready"), q.xb)
                    for dst, src in aux[q.kind]:
                        sp.dma_start(dst, src).then_inc(sem("aux"), 16)
                    at_aux.pop(n + 1)
                    with sp.Fori(0, groups - 1) as g:
                        for a in range(1, per + 1):
                            load(g * per + (n + a), bass.ds(g * per + (first + a), 1), (n + a) % 2)
                    for a in range((groups - 1) * per + 1, groups * per):
                        load(n + a, first + a, (n + a) % 2)
                    n += per * groups
                    continue
                load_aux(n)
                while m + 1 < len(chunks) and chunks[m + 1][0] == chunks[m][0] + 1 and m + 1 not in at_aux and m + 1 not in grouped:
                    m += 1
                count = m + 1 - n
                while count and (n < 2 or count % 2):
                    load(n, chunks[n][0], n % 2)
                    n, count = n + 1, count - 1
                if count >= 4:
                    with sp.Fori(0, count // 2) as j:
                        for a in range(2):
                            load(j * 2 + (n + a), bass.ds(j * 2 + (chunks[n][0] + a), 1), (n + a) % 2)
                else:
                    for a in range(count):
                        load(n + a, chunks[n + a][0], (n + a) % 2)
                n += count
            sp.wait_ge(sem("x_ready"), x_total)
            sp.dma_start(out.rearrange("(t p) d -> p t d", p=P), x[:, :, :]).then_inc(sem("stored"), 16)
            sp.wait_ge(sem("stored"), 16)

        @block.gpsimd
        def _(pool):
            nc.gpsimd.memset(minus_half[:, :], -0.5).then_inc(sem("pool_const"), 1)

            def split_lo(c, slot, sign=False, w_hi=w_hi, w_lo=w_lo, to=None):
                to = slot if to is None else to
                for part, lo, hi in (("a", 0, PA), ("b", PA, CHUNK)):
                    pool.wait_ge(sem(f"w_hi_{part}"), c + 1)
                    if sign:
                        pool.wait_ge(sem(f"w_lo_{part}"), c)
                        pool.sem_inc(sem(f"w_lo_{part}"), 1)
                    else:
                        nc.gpsimd.tensor_tensor(w_lo[to][:, lo:hi], raw[:, slot, lo:hi], w_hi[to][:, lo:hi].bitcast(F32),
                                                ALU.subtract).then_inc(sem(f"w_lo_{part}"), 1)

            def pow_of(ln):
                pool.wait_ge(sem("var_ready"), ln + 1)
                nc.gpsimd.tensor_tensor(rstd[:, :], var_eps[:, :], minus_half[:, :], ALU.pow).then_inc(sem("rstd"), 1)

            pool.wait_ge(sem("pool_const"), 1)
            at_chunk = {}
            for before, q in zip([None] + calls, calls):
                if q.kind not in GROUPS:
                    at = q.cb if before and before.prepares else q.cb + 1
                    if before and before.kind in (FFN0, GATE0):
                        at = sum(gated(before)[0:2]) - 1
                    at_chunk.setdefault(at, []).extend(q.lns)

            def one(c):
                for ln in at_chunk.get(c, []):
                    pow_of(ln)
                split_lo(c, c % 2, chunks[c][2])

            def run_chunks(n, stop):
                while n < stop:
                    def plain(c):
                        return c < stop and c not in at_chunk and not chunks[c][2]
                    one(n)
                    n += 1
                    m = n
                    while plain(m):
                        m += 1
                    pairs = (m - n) // 2
                    if pairs < 2:
                        continue
                    with pool.Fori(0, pairs) as j:
                        for a in range(2):
                            c = n + a
                            split_lo(j * 2 + c, c % 2)
                    n += 2 * pairs

            def attention(c):
                m = att[c.kind]
                pow_of(c.lns[0])
                split_lo(c.cb, c.cb % 2)
                pow_of(c.lns[1])
                if c.kind == ATT1:
                    for pads in m.v_pad:
                        for v in pads:
                            nc.gpsimd.memset(v[:, :, :].bitcast(F32), 0.0).then_inc(sem("pool_pad"), 1)
                    nc.gpsimd.memset(m.zero[:, :, :], 0.0).then_inc(sem("pool_pad"), 1)
                    pool.wait_ge(sem("pool_pad"), 5)

                def phase(g, qt):
                    ph = Phase(c, g, qt)

                    def pad(u):
                        if u >= 2:
                            pool.wait_ge(ph.sem("av"), ph.units + (u - 1))
                        old, new = ((u - 2) % m.heads) * HD1, u * HD1
                        for v, src in zip(m.v_pad[u % 2], (m.v_hi, m.v_lo)):
                            nc.gpsimd.tensor_tensor(v[:, :, old:old + HD1], m.zero[:, :, :], m.zero[:, :, :], ALU.add)
                            ins = nc.gpsimd.tensor_copy(v[:, 0:ph.nkb, new:new + HD1], src[:, 0:ph.nkb, new:new + HD1].bitcast(F32))
                        ins.then_inc(ph.sem("pad"), 1)

                    def normalise(u, q):
                        row = u * HT + q
                        pool.wait_ge(ph.sem("rinv"), ph.rows + (row + 1))
                        v, n = ph.row(u, q), (qt * HT + q + 1) * P
                        nc.gpsimd.tensor_tensor(v, v, m.rinv[:, row % 8:row % 8 + 1].broadcast_to((P, n)), ALU.mult)\
                            .then_inc(ph.sem("norm"), 1)

                    def lo(i):
                        split_lo(ph.chunk + i, (c.cb + i) % 2, w_hi=m.w_hi, w_lo=m.w_lo, to=ph.w_slot(i))

                    if qt == 0:
                        lo(1)
                    if c.kind == ATT3:
                        for t in range(HT):
                            pool.wait_ge(ph.sem("by_sin"), ph.tiles + (t + 1))
                            rot = m.rot[t % 2][:, :, :].rearrange("p h d -> p (h d)")
                            nc.gpsimd.tensor_tensor(rot, rot, m.by_sin[:, :, :].rearrange("p h d -> p (h d)"), ALU.add)\
                                .then_inc(ph.sem("rot"), 1)
                        if qt == 0:
                            lo(2)
                            lo(3)
                    else:
                        pool.wait_ge(ph.sem("v_lo"), ph.tiles + HT)
                        pad(0)
                        pad(1)
                    if qt:
                        lo(m.ch)
                    for row in range(HT, AHEAD - 1):
                        normalise(row // HT, row % HT)
                    for u, q, keys, ahead, late in ph.steps():
                        if late:
                            normalise(*late)
                        if c.kind == ATT1 and u and u + 1 < m.heads and late == (u + 1, HT - 1):
                            pad(u + 1)

                with pool.Fori(0, m.groups) as g:
                    phase(g, 0)
                    phase(g, 1)

            skip = 0
            for n, c in enumerate(calls):
                stop = calls[n + 1].cb if n + 1 < len(calls) else len(chunks)
                if c.kind in GROUPS:
                    attention(c)
                    skip = 1
                else:
                    run_chunks(c.cb + skip, stop)
                    skip = 0

        @block.scalar
        def _(act):
            n_scaled = [0]

            def split_hi(c, part, loop=None):
                if c >= len(chunks):
                    return
                slot = c % 2
                _, scaled, sign = chunks[c]
                off = 0 if loop is None else loop
                if scaled:
                    k = sum(1 for q in chunks[:c + 1] if q[1])
                    act.wait_ge(sem("scaled"), off * 2 + k)
                else:
                    act.wait_ge(sem(f"raw{slot}"), off * 16 + 16 * (c // 2 + 1))
                if c >= 2:
                    act.wait_ge(sem(f"w_free_{part}"), off * 2 + (c - 1))
                lo, hi = (0, PA) if part == "a" else (PA, CHUNK)
                nc.scalar.activation(w_hi[slot][:, lo:hi], raw[:, slot, lo:hi], ACT.Sign if sign else ACT.Copy)\
                    .then_inc(sem(f"w_hi_{part}"), 1)

            def turn(n, half):
                for t in range(HT):
                    act.wait_ge(sem("turned"), n * HT + t + 1)
                    nc.scalar.activation(xt_hi[:, :, tok(half, t):tok(half, t) + P],
                                         W[:, t % 2, :].rearrange("p (k q) -> p k q", k=KT), ACT.Copy).then_inc(sem("xt_hi"), 1)

            def gate0_terms(c, ms):
                for m in ms:
                    act.wait_ge(*((sem("term"), ORDERS * c.n + m) if m else (sem("up_copied"), c.n + 1)))
                    kw = {} if m == 0 else dict(scale=coef[:, m - 1:m])
                    nc.scalar.activation(term_hi[m][:, :], term[:, m, :], ACT.Copy if m == 0 else ACT.Identity, **kw)\
                        .then_inc(sem("term_hi"), 1)

            def gated_call(c):
                steps, cb, _ = gated(c)
                if c.kind == GATE0:
                    split_hi(cb, "a")
                    act.wait_ge(sem("w_free_a"), cb)
                    nc.scalar.activation(term[:, 0, :], W[:, 0, :], ACT.Copy).then_inc(sem("up_copied"), 1)
                    gate0_terms(c, [0])
                    split_hi(cb, "b")

                def step(i, j=None):
                    off = 0 if j is None else j
                    split_hi(cb + i + 1, "a", j)
                    p = i % 2
                    act.wait_ge(sem("w_free_a"), off * 2 + (cb + i + 1))
                    nc.scalar.activation(s_buf[:, p, :], W[:, 2 * p, :], ACT.Silu).then_inc(sem("silu"), 1)
                    act.wait_ge(sem("h"), off * 2 + (c.sb + i + 1))
                    nc.scalar.activation(h_hi[p][:, :], h_buf[:, p, :], ACT.Copy).then_inc(sem("h_hi"), 1)
                    split_hi(cb + i + 1, "b", j)

                step(0)
                if c.kind == GATE0:
                    gate0_terms(c, [1, 2])
                step(1)
                if c.kind == GATE0:
                    gate0_terms(c, [3, 4, 5, 6])
                with act.Fori(0, (steps - 4) // 2) as j:
                    step(2, j)
                    step(3, j)
                step(steps - 2)
                step(steps - 1)
                if c.kind == GATE0:
                    for q in (1, 2):
                        for part in "ab":
                            split_hi(cb + steps + q, part)

            def split(c):
                split_hi(c, "a")
                split_hi(c, "b")

            def ffn1_call(c):
                cb = c.cb
                split(cb + 1)
                split(cb + 2)
                act.wait_ge(sem("w_free_a"), cb + 2)
                nc.scalar.activation(q_sb[:, :, :], W[:, :, 0:EXP1 * DK1], ACT.Copy).then_inc(sem("q_copied"), 1)
                nc.scalar.activation(h1[:, :, :], Y[:, 0, :].rearrange("p (e r) -> p e r", r=RANK1), ACT.Copy)\
                    .then_inc(sem("h1_copied"), 1)
                split(cb + 3)
                act.wait_ge(sem("score1"), c.n + 1)
                nc.scalar.activation(soft1[:, :, :], score1[:, :, :], ACT.Exp, scale=DK1 ** -0.5).then_inc(sem("exp1"), 1)
                act.wait_ge(sem("wh_turned"), c.n + 1)
                nc.scalar.activation(wht_hi[:, :], W[:, 0, :], ACT.Copy).then_inc(sem("wht_hi"), 1)
                split(cb + 4)

            def ffn2_call(c):
                if c.first:
                    act.wait_ge(sem("aux"), c.aux)
                    nc.scalar.activation(small2_hi[:, :], small2[:, :], ACT.Copy)
                    nc.scalar.activation(chan_hi[0:E2, :], chan[0:E2, :], ACT.Copy).then_inc(sem("chan_hi"), 1)
                split(c.cb + 1)
                act.wait_ge(sem("logit"), c.n + 1)
                nc.scalar.activation(route[:, :, :], logit[:, :, :], ACT.Exp).then_inc(sem("exp2"), 1)
                act.wait_ge(sem("route_turned"), c.n + 1)
                nc.scalar.activation(rt_hi[0:E2, :], W[0:E2, 1, :], ACT.Copy).then_inc(sem("rt_hi"), 1)
                turn(c.ts[1], c.half)
                act.wait_ge(sem("out_scale"), c.n + 1)
                nc.scalar.activation(out_sc[:, :, :], W[:, :, :], ACT.Copy).then_inc(sem("out_sc"), 1)
                split(c.cb + 2)

            def att2_call(c):
                cb = c.cb
                split(cb + 1)
                split(cb + 2)
                act.wait_ge(sem("spectrum"), 2 * c.n + 1)
                nc.scalar.activation(spec[:, :, :], Y[:, :, :], ACT.Copy).then_inc(sem("spec"), 1)
                nc.scalar.activation(sq[:, :, :], Y[:, :, :], ACT.Square).then_inc(sem("sq"), 1)
                act.wait_ge(sem("power"), c.n + 1)
                nc.scalar.activation(power_hi[:, :, :], power_sum[:, :, :], ACT.Copy)
                nc.scalar.activation(nyq_hi[0:1, :], sq[0:1, 2, :], ACT.Copy).then_inc(sem("power_hi"), 1)
                split(cb + 3)
                act.wait_ge(sem("correlated"), c.n + 1)
                for t in range(HT):
                    nc.scalar.activation(corr[:, t, 0:D], W[:, t, :], ACT.Copy).then_inc(sem("corr"), 1)
                for t in range(HT):
                    act.wait_ge(sem("nmax2"), c.n * HT + t + 1)
                    nc.scalar.activation(ex2[:, t, :], W[:, t, :], ACT.Exp, bias=nmax2[:, t:t + 1]).then_inc(sem("ex2"), 1)
                turn(c.ts[1], c.half)
                split(cb + 4)
                act.wait_ge(sem("mix"), c.n + 1)
                nc.scalar.activation(mix_hi[:, :, :], mix[:, :, :], ACT.Copy).then_inc(sem("mix_hi"), 1)
                split(cb + 5)

            def ffn3_call(c):
                if c.first:
                    split(c.cb + 1)
                    act.wait_ge(sem("gmat"), c.n // 2 + 1)
                    nc.scalar.activation(gmat_hi[:, :], gmat[:, :, :].rearrange("p b r -> p (b r)"), ACT.Copy).then_inc(sem("gmat_hi"), 1)
                    split(c.cb + 2)
                    act.wait_ge(sem("eff"), c.n + 1)
                    nc.scalar.activation(aeff_hi[:, :, :], W[:, :, 0:B3 * R3], ACT.Copy).then_inc(sem("eff_hi"), 1)
                    split(c.cb + 3)
                    act.wait_ge(sem("eff"), c.n + 2)
                    nc.scalar.activation(beff_hi[:, :, :], Y[:, 0:2, :], ACT.Copy).then_inc(sem("eff_hi"), 1)
                split(c.mb + 1)
                act.wait_ge(sem("h3"), c.n + 1)
                nc.scalar.activation(h3_hi[:, :], h3[:, :], ACT.Copy)
                nc.scalar.activation(hs_hi[:, :], W[0:R3, 1, :], ACT.Copy).then_inc(sem("h3_hi"), 1)
                split(c.mb + 2)

            def attention(c):
                m = att[c.kind]

                def phase(g, qt):
                    ph = Phase(c, g, qt)

                    def hi(i):
                        slot = (c.cb + i) % 2
                        for part in "ab":
                            act.wait_ge(sem(f"raw{slot}"), g * (16 * m.ch // 2) + 16 * ((c.cb + i) // 2 + 1))
                            act.wait_ge(sem(f"w_free_{part}"), ph.chunk + (i + 1 - m.ch))
                            lo, hi_ = (0, PA) if part == "a" else (PA, CHUNK)
                            nc.scalar.activation(m.w_hi[ph.w_slot(i)][:, lo:hi_], raw[:, slot, lo:hi_], ACT.Copy)\
                                .then_inc(sem(f"w_hi_{part}"), 1)

                    def project1(t):
                        s, tt = t % 2, qt * HT + t
                        act.wait_ge(ph.sem("qkv"), ph.tiles + (t + 1))
                        for i, dst in ((0, m.q_parts[s][:, :, :, 0, :]), (1, m.k_parts[s][:, :, 0, :, :])):
                            src = m.qkv[:, s, i, :, :].rearrange("p h (one d) -> p h one d", one=1)
                            nc.scalar.activation(dst, src.broadcast_to((P, m.heads, 2, HD1)), ACT.Copy)
                        nc.scalar.activation(m.v_hi[:, tt, :], m.qkv[:, s, 2, :, :].rearrange("p h d -> p (h d)"), ACT.Copy)\
                            .then_inc(ph.sem("parts_hi"), 1)

                    def turned1(t):
                        act.wait_ge(ph.sem("qk_turned"), ph.tiles + (t + 1))
                        nc.scalar.activation(m.q[:, :, t * P:(t + 1) * P], Y[:, 0, :].rearrange("p (h q) -> p h q", q=P), ACT.Copy,
                                             scale=HD1 ** -0.5).then_inc(ph.sem("q_out"), 1)

                    def project3(t):
                        s, tt = t % 2, qt * HT + t
                        act.wait_ge(ph.sem("by_sin"), ph.tiles + (t + 1))
                        nc.scalar.activation(m.v_hi[:, tt, :], W[:, 2 * s + 1, P:2 * P], ACT.Copy).then_inc(ph.sem("v_hi"), 1)

                    def turned3(t):
                        tt = qt * HT + t
                        act.wait_ge(ph.sem("qk_turned"), ph.tiles + (t + 1))
                        nc.scalar.activation(m.q_hi[:, :, t * P:(t + 1) * P], Y[:, 0, :].rearrange("p (h q) -> p h q", q=P), ACT.Copy)
                        nc.scalar.activation(m.k_hi[:, tt * P:(tt + 1) * P], Y[:, 1, 0:P], ACT.Copy, scale=HD3 ** -0.5)\
                            .then_inc(ph.sem("qk_hi"), 1)

                    def exponent(u, q):
                        row = u * HT + q
                        n = (qt * HT + q + 1) * P
                        act.wait_ge(ph.sem("nmax"), ph.rows + (row + 1))
                        s = row % 2
                        sc = W[:, 2 * s:2 * s + 2, :].rearrange("p b c -> p (b c)")
                        nc.scalar.activation(ph.row(u, q), sc[:, 0:n], ACT.Exp, bias=m.nmax[:, row % 8:row % 8 + 1],
                                             accum_out=m.rsum[:, row % 8:row % 8 + 1]).then_inc(ph.sem("exp"), 1)

                    def upper(u, j):
                        b = u * ph.nkb + j
                        act.wait_ge(ph.sem("p_turned"), ph.blocks + (b + 1))
                        s = b % PT_SLOTS
                        nc.scalar.activation(m.pt_hi[s][:, ph.cols(j):HALF], Y[:, s, ph.cols(j):HALF], ACT.Copy).then_inc(ph.sem("pt_hi"), 1)

                    def out_hi(u):
                        act.wait_ge(ph.sem("av"), ph.units + (u + 1))
                        if c.kind == ATT1:
                            nc.scalar.activation(m.o_hi[:, 0, :], Y[:, AV, :], ACT.Copy).then_inc(ph.sem("o_hi"), 1)
                            return
                        if u:
                            act.wait_ge(ph.sem("o_lo"), ph.units + u)
                        nc.scalar.activation(m.o_raw, Y[:, AV, :], ACT.Copy).then_inc(ph.sem("o_out"), 1)
                        act.wait_ge(ph.sem("o_out"), ph.units + (u + 1))
                        nc.scalar.activation(m.o_hi[:, u, :], m.o_raw, ACT.Copy).then_inc(ph.sem("o_hi"), 1)

                    if qt == 0:
                        hi(1)
                    proj, turned = (project1, turned1) if c.kind == ATT1 else (project3, turned3)
                    proj(0)
                    for t in range(HT):
                        if t + 1 < HT:
                            proj(t + 1)
                        turned(t)
                    if c.kind == ATT3 and qt == 0:
                        hi(2)
                        hi(3)
                    if qt:
                        hi(m.ch)
                    for row in range(AHEAD - 1):
                        exponent(row // HT, row % HT)
                    for u, q, keys, ahead, late in ph.steps():
                        for n, key in enumerate(keys):
                            upper(*key)
                            if n == 0 and late:
                                exponent(*late)
                        if c.kind == ATT3 and u and q == 1 - qt:
                            out_hi(u - 1)
                    out_hi(m.heads - 1)

                for part in "ab":
                    act.wait_ge(sem(f"w_free_{part}"), c.cb)
                with act.Fori(0, m.groups) as g:
                    phase(g, 0)
                    phase(g, 1)

            if GATE0 in kinds:
                act.wait_ge(sem("const"), 16 * 5)
                nc.scalar.activation(coef[:, :], coef[:, :], ACT.Exp, scale=-1.0).then_inc(sem("coef"), 1)
                act.wait_ge(sem("coef"), 1)
            split_hi(0, "a")
            split_hi(0, "b")
            act.wait_ge(sem("const"), 32)
            nc.scalar.activation(ident_r[:, :], ident[:, :], ACT.Copy)
            nc.scalar.activation(mask_r[:, :], mask[:, :], ACT.Copy).then_inc(sem("const_r"), 1)
            for c in calls:
                if c.kind in GROUPS:
                    turn(c.ts[0], 0)
                    turn(c.ts[1], 1)
                    attention(c)
                    continue
                turn(c.ts[0], c.half)
                dict(FFN0=gated_call, GATE0=gated_call, FFN1=ffn1_call, FFN2=ffn2_call, ATT2=att2_call, FFN3=ffn3_call)[c.kind](c)

        @block.vector
        def _(dve):
            chain = Chain(dve, sem("dve"))
            xc = [0]

            def measure(half):
                for t in range(HT):
                    ins = nc.vector.bn_stats(stats[:, t, :], x[:, half * HT + t, :])
                chain.link(ins)
                for t in range(HT):
                    ins = nc.vector.bn_aggr(mv[:, t, :], stats[:, t, :])
                chain.link(ins)
                nc.vector.tensor_scalar(var_eps[:, :], mv[:, :, 1], EPS, None, ALU.add).then_inc(sem("var_ready"), 1)

            def turn_in(ln, half):
                dve.wait_ge(sem("rstd"), ln + 1)
                for t in range(HT):
                    nc.vector.tensor_scalar(xn[:, t, :], x[:, half * HT + t, :], mv[:, t, 0:1], rstd[:, t:t + 1],
                                            ALU.subtract, ALU.mult).then_inc(sem("turn_in"), 1)

            def turn(n, half):
                for t in range(HT):
                    dve.wait_ge(sem("xt_hi"), n * HT + t + 1)
                    sl = slice(tok(half, t), tok(half, t) + P)
                    nc.vector.tensor_tensor(xt_lo[:, :, sl], W[:, t % 2, :].rearrange("p (k q) -> p k q", k=KT),
                                            xt_hi[:, :, sl].bitcast(F32), ALU.subtract).then_inc(sem("xt_lo"), 1)

            def prepare(c, measured=False):
                if c.prepares:
                    half = c.next.half or 0
                    if not measured:
                        measure(half)
                    turn_in(c.next.lns[0], half)
                    if c.next.kind == FFN0 and c.kind != FFN0:
                        scale(c.next.cb)
                    turn(c.next.ts[0], half)

            def scale(n, j=None, of=0):
                slot, step = n % 2, chunks[n][0] - DRAM_BASE[FFN0]
                off, at = (0, slice(step, step + 1)) if j is None else (j, bass.ds(j * 2 + step, 1))
                dve.wait_ge(sem(f"raw{slot}"), off * 16 + 16 * (n // 2 + 1))
                v = raw[:, slot, :].rearrange("p (b f) -> p b f", f=P)
                sc = scales[:, at, :].rearrange("p one k -> p k one")
                nc.vector.tensor_tensor(v, v, sc.broadcast_to((P, 3 * KT, P)), ALU.mult).then_inc(sem("scaled"), 1)

            def residual(half, coef_, name, count):
                dve.wait_ge(sem(name), count)
                for t in range(HT):
                    nc.vector.scalar_tensor_tensor(x[:, half * HT + t, :], Y[:, t, :], coef_, x[:, half * HT + t, :],
                                                   ALU.mult, ALU.add).then_inc(sem("x_ready"), 1)
                    xc[0] += 1

            def term_lo_of(c, ms):
                for m in ms:
                    dve.wait_ge(sem("term_hi"), (ORDERS + 1) * c.n + m + 1)
                    if m == 0:
                        ins = nc.vector.tensor_tensor(term_lo[0][:, :], term[:, 0, :], term_hi[0][:, :].bitcast(F32), ALU.subtract)
                    else:
                        ins = nc.vector.scalar_tensor_tensor(term_lo[m][:, :], term[:, m, :], coef[:, m - 1:m],
                                                             term_hi[m][:, :].bitcast(F32), ALU.mult, ALU.subtract)
                    ins.then_inc(sem("term_lo"), 1)

            def gated_call(c):
                steps, cb, after = gated(c)

                def step(i, j=None):
                    off = 0 if j is None else j
                    p = i % 2
                    dve.wait_ge(sem("silu"), off * 2 + (c.sb + i + 1))
                    nc.vector.tensor_tensor(h_buf[:, p, :], W[:, 2 * p + 1, :], s_buf[:, p, :], ALU.mult).then_inc(sem("h"), 1)
                    dve.wait_ge(sem("h_hi"), off * 2 + (c.sb + i + 1))
                    nc.vector.tensor_tensor(h_lo[p][:, :], h_buf[:, p, :], h_hi[p][:, :].bitcast(F32), ALU.subtract)\
                        .then_inc(sem("h_lo"), 1)

                def power(m):
                    ins = nc.vector.tensor_tensor(term[:, m, :], term[:, m - 1, :], delta[:, :], ALU.mult)
                    if m == 5:
                        chain.link(ins)
                        ins = nc.vector.tensor_tensor(term[:, m, :], term[:, m, :], near[:, :], ALU.mult)
                    ins.then_inc(sem("term"), 1)
                    dve.wait_ge(sem("term"), ORDERS * c.n + m)

                if c.kind == GATE0:
                    if c.n == 0:
                        dve.wait_ge(sem("const"), 16 * 5)
                        dve.wait_ge(sem("coef"), 1)
                    dve.wait_ge(sem("w_free_a"), cb)
                    chain.link(nc.vector.tensor_scalar(delta[:, :], W[:, 1, :], lpoint[:, 0:1], None, ALU.subtract))
                    dve.wait_ge(sem("up_copied"), c.n + 1)
                    chain.link(nc.vector.tensor_scalar(near[:, :], delta[:, :], -THD, None, ALU.is_ge))
                    nc.vector.scalar_tensor_tensor(near[:, :], delta[:, :], THD, near[:, :], ALU.is_le, ALU.mult)\
                        .then_inc(sem("gate_read"), 1)
                    dve.wait_ge(sem("gate_read"), c.n + 1)
                    term_lo_of(c, (0,))
                    step(0)
                    for m in (1, 2):
                        power(m)
                    term_lo_of(c, (1, 2))
                    step(1)
                    for m in (3, 4, 5, 6):
                        power(m)
                    term_lo_of(c, (3, 4, 5, 6))
                else:
                    scale(cb + 1)
                    step(0)
                    scale(cb + 2)
                    step(1)
                    scale(cb + 3)
                with dve.Fori(0, (steps - 4) // 2) as j:
                    for a in (2, 3):
                        step(a, j)
                        if c.kind == FFN0:
                            scale(cb + a + 2, j)
                if c.prepares:
                    measure(c.next.half or 0)
                step(steps - 2)
                if c.kind == FFN0 and c.next and c.next.kind == FFN0:
                    scale(c.next.cb)
                step(steps - 1)
                prepare(c, True)
                residual(c.half, 0.5 if c.kind == FFN0 else 1.0, "w_free_b", cb + steps + after)

            def add_bias(c, bias):
                dve.wait_ge(sem("aux"), c.aux)
                xs = x[:, c.half * HT:(c.half + 1) * HT, :]
                b = bias[:, :].rearrange("p (one d) -> p one d", one=1).broadcast_to((P, HT, D))
                dve.wait_ge(sem("turn_in"), (c.ts[0] + 1) * HT)
                chain.link(nc.vector.scalar_tensor_tensor(xs, b, 0.5, xs, ALU.mult, ALU.add))

            def over(ap, n):
                return ap.rearrange("p (m one) -> p m one", one=1).broadcast_to((ap.shape[0], ap.shape[1], n))

            def ffn1_call(c):
                add_bias(c, bias1)
                dve.wait_ge(sem("q_copied"), c.n + 1)
                chain.link(nc.vector.tensor_tensor(prod[:, :, :].rearrange("p (t e) d -> p t (e d)", t=HT), W[:, :, EXP1 * DK1:D],
                                                   q_sb[:, :, :], ALU.mult))
                s2 = score1[:, :, :].rearrange("p t e -> p (t e)")
                chain.link(nc.vector.tensor_reduce(s2, prod[:, :, :], AX, ALU.add))
                chain.link(nc.vector.tensor_reduce(top1[:, :], score1[:, :, :], AX, ALU.max))
                nc.vector.tensor_tensor(score1[:, :, :], score1[:, :, :], over(top1[:, :], EXP1), ALU.subtract).then_inc(sem("score1"), 1)
                dve.wait_ge(sem("exp1"), c.n + 1)
                chain.link(nc.vector.tensor_reduce(top1[:, :], soft1[:, :, :], AX, ALU.add))
                chain.link(nc.vector.reciprocal(top1[:, :], top1[:, :]))
                chain.link(nc.vector.tensor_tensor(soft1[:, :, :], soft1[:, :, :], over(top1[:, :], EXP1), ALU.mult))
                dve.wait_ge(sem("h1_copied"), c.n + 1)
                nc.vector.tensor_tensor(wh[:, :, :], h1[:, :, :], over(soft1[:, :, :].rearrange("p t e -> p (t e)"), RANK1), ALU.mult)\
                    .then_inc(sem("wh"), 1)
                dve.wait_ge(sem("wht_hi"), c.n + 1)
                nc.vector.tensor_tensor(wht_lo[:, :], W[:, 0, :], wht_hi[:, :].bitcast(F32), ALU.subtract).then_inc(sem("wht_lo"), 1)
                prepare(c)
                residual(c.half, 0.5, "w_free_a", c.cb + 4)

            def ffn2_call(c):
                add_bias(c, bias2)
                if c.first:
                    dve.wait_ge(sem("chan_hi"), c.n // 2 + 1)
                    nc.vector.tensor_tensor(small2_lo[:, :], small2[:, :], small2_hi[:, :].bitcast(F32), ALU.subtract)
                    nc.vector.tensor_tensor(chan_lo[0:E2, :], chan[0:E2, :], chan_hi[0:E2, :].bitcast(F32), ALU.subtract)\
                        .then_inc(sem("chan_lo"), 1)
                dve.wait_ge(sem("logits"), c.n + 1)
                lg = W[:, 0, 0:HT * E2].rearrange("p (t e) -> p t e", e=E2)
                chain.link(nc.vector.tensor_reduce(top2[:, :], lg, AX, ALU.max))
                nc.vector.tensor_tensor(logit[:, :, :], lg, over(top2[:, :], E2), ALU.subtract).then_inc(sem("logit"), 1)
                dve.wait_ge(sem("exp2"), c.n + 1)
                chain.link(nc.vector.tensor_reduce(top2[:, :], route[:, :, :], AX, ALU.add))
                chain.link(nc.vector.reciprocal(top2[:, :], top2[:, :]))
                nc.vector.tensor_tensor(route[:, :, :], route[:, :, :], over(top2[:, :], E2), ALU.mult).then_inc(sem("route"), 1)
                dve.wait_ge(sem("rt_hi"), c.n + 1)
                nc.vector.tensor_tensor(rt_lo[0:E2, :], W[0:E2, 1, :], rt_hi[0:E2, :].bitcast(F32), ALU.subtract).then_inc(sem("rt_lo"), 1)
                for t in range(HT):
                    dve.wait_ge(sem("in_scale"), c.n * HT + t + 1)
                    nc.vector.tensor_tensor(xn[:, t, :], W[:, t, :], xn[:, t, :], ALU.mult).then_inc(sem("turn_in"), 1)
                turn(c.ts[1], c.half)
                prepare(c)
                dve.wait_ge(sem("out_sc"), c.n + 1)
                dve.wait_ge(sem("w_free_a"), c.cb + 2)
                for t in range(HT):
                    ins = nc.vector.tensor_tensor(scaled_y[:, t, :], Y[:, t, :], out_sc[:, t, :], ALU.mult)
                chain.link(ins)
                for t in range(HT):
                    xs = x[:, c.half * HT + t, :]
                    nc.vector.scalar_tensor_tensor(xs, scaled_y[:, t, :], 0.5, xs, ALU.mult, ALU.add).then_inc(sem("x_ready"), 1)
                    xc[0] += 1

            def att2_call(c):
                dve.wait_ge(sem("turn_in"), (c.ts[0] + 1) * HT)
                nc.vector.memset(corr[:, :, D:D + 2], NONE)
                dve.wait_ge(sem("sq"), c.n + 1)
                chain.link(nc.vector.tensor_tensor(power_sum[:, :, :], sq[:, 0:2, :], sq[:, 2:4, :], ALU.add))
                nc.vector.tensor_copy(power_sum[0:1, 0, :], sq[0:1, 0, :]).then_inc(sem("power"), 1)
                dve.wait_ge(sem("power_hi"), c.n + 1)
                dve.wait_ge(sem("power"), c.n + 1)
                nc.vector.tensor_tensor(power_lo[:, :, :], power_sum[:, :, :], power_hi[:, :, :].bitcast(F32), ALU.subtract)
                nc.vector.tensor_tensor(nyq_lo[0:1, :], sq[0:1, 2, :], nyq_hi[0:1, :].bitcast(F32), ALU.subtract).then_inc(sem("power_lo"), 1)
                for t in range(HT):
                    dve.wait_ge(sem("corr"), c.n * HT + t + 1)
                    chain.link(nc.vector.max(top8[:, t, :], corr[:, t, 0:D]))
                    nc.vector.tensor_scalar(nmax2[:, t:t + 1], top8[:, t, 0:1], -1.0, None, ALU.mult).then_inc(sem("nmax2"), 1)
                    chain.link(nc.vector.memset(top8[:, t, TOPK:8], NONE))
                    chain.sig(nc.vector.match_replace(marked[:, t, 0:D + 2], top8[:, t, :], corr[:, t, 0:D + 2], BIG))
                chain.wait()
                for t in range(HT):
                    dve.wait_ge(sem("ex2"), c.n * HT + t + 1)
                    ins = nc.vector.scalar_tensor_tensor(ex2[:, t, :], marked[:, t, 0:D], BIG, ex2[:, t, :], ALU.is_equal, ALU.mult,
                                                         accum_out=sum2[:, t:t + 1])
                    chain.sig(ins)
                chain.wait()
                chain.link(nc.vector.reciprocal(sum2[:, :], sum2[:, :]))
                for t in range(HT):
                    nc.vector.tensor_scalar(xn[:, t, :], ex2[:, t, :], sum2[:, t:t + 1], None, ALU.mult).then_inc(sem("turn_in"), 1)
                turn(c.ts[1], c.half)
                dve.wait_ge(sem("spectrum"), 2 * c.n + 2)
                nc.vector.tensor_tensor(sq[:, :, :], Y[:, :, :], spec[:, :, :], ALU.mult)
                nc.vector.tensor_tensor(cross[:, 0:2, :], Y[:, 0:2, :], spec[:, 2:4, :], ALU.mult)
                chain.link(nc.vector.tensor_tensor(cross[:, 2:4, :], Y[:, 2:4, :], spec[:, 0:2, :], ALU.mult))
                nc.vector.tensor_tensor(mix[:, 0:2, :], sq[:, 0:2, :], sq[:, 2:4, :], ALU.add)
                chain.link(nc.vector.tensor_tensor(mix[:, 2:4, :], cross[:, 2:4, :], cross[:, 0:2, :], ALU.subtract))
                nc.vector.tensor_copy(mix[0:1, 0, :], sq[0:1, 0, :])
                nc.vector.tensor_copy(mix[0:1, 2, :], sq[0:1, 2, :]).then_inc(sem("mix"), 1)
                dve.wait_ge(sem("mix_hi"), c.n + 1)
                nc.vector.tensor_tensor(mix_lo[:, :, :], mix[:, :, :], mix_hi[:, :, :].bitcast(F32), ALU.subtract).then_inc(sem("mix_lo"), 1)
                prepare(c)
                residual(c.half, 1.0, "w_free_b", c.cb + 5)

            def ffn3_call(c):
                add_bias(c, bias3)
                if c.first:
                    g = over(gate_rep[:, :], R3)
                    r = same_rank[:, :].rearrange("p (one r) -> p one r", one=1).broadcast_to((P, 4 * B3, R3))
                    nc.vector.tensor_tensor(gmat[:, :, :], g, r, ALU.mult).then_inc(sem("gmat"), 1)
                    dve.wait_ge(sem("gmat_hi"), c.n // 2 + 1)
                    nc.vector.tensor_tensor(gmat_lo[:, :], gmat[:, :, :].rearrange("p b r -> p (b r)"), gmat_hi[:, :].bitcast(F32),
                                            ALU.subtract).then_inc(sem("gmat_lo"), 1)
                    dve.wait_ge(sem("eff_hi"), c.n + 1)
                    nc.vector.tensor_tensor(aeff_lo[:, :, :], W[:, :, 0:B3 * R3], aeff_hi[:, :, :].bitcast(F32), ALU.subtract)\
                        .then_inc(sem("eff_lo"), 1)
                    dve.wait_ge(sem("eff_hi"), c.n + 2)
                    nc.vector.tensor_tensor(beff_lo[:, :, :], Y[:, 0:2, :], beff_hi[:, :, :].bitcast(F32), ALU.subtract)\
                        .then_inc(sem("eff_lo"), 1)
                dve.wait_ge(sem("down3"), c.n + 1)
                nc.vector.tensor_tensor(h3[:, :], W[:, 0, :], own_block[:, :], ALU.mult).then_inc(sem("h3"), 1)
                dve.wait_ge(sem("h3_hi"), c.n + 1)
                nc.vector.tensor_tensor(h3_lo[:, :], h3[:, :], h3_hi[:, :].bitcast(F32), ALU.subtract)
                nc.vector.tensor_tensor(hs_lo[:, :], W[0:R3, 1, :], hs_hi[:, :].bitcast(F32), ALU.subtract).then_inc(sem("h3_lo"), 1)
                prepare(c)
                residual(c.half, 0.5, "w_free_b", c.mb + 2)

            def attention(c):
                m = att[c.kind]
                if c.kind == ATT1:
                    dve.wait_ge(sem("aux"), c.aux)
                    b = m.bias_o[:, :].rearrange("p (one d) -> p one d", one=1).broadcast_to((P, TT, D))
                    dve.wait_ge(sem("turn_in"), (c.ts[1] + 1) * HT)
                    chain.link(nc.vector.tensor_tensor(x[:, :, :], x[:, :, :], b, ALU.add))
                else:
                    dve.wait_ge(sem("aux"), c.aux)

                def phase(g, qt):
                    ph = Phase(c, g, qt)

                    def bank(s):
                        return W[:, 2 * s:2 * s + 2, :].rearrange("p b c -> p (b c)")

                    def project1(t):
                        s, tt = t % 2, qt * HT + t
                        n = 3 * m.heads * HD1
                        dve.wait_ge(ph.sem("proj"), ph.tiles + (t + 1))
                        qkv = m.qkv[:, s, :, :, :].rearrange("p i h d -> p (i h d)")
                        b = m.bias_qkv[:, bass.ds(g, 1), :].rearrange("p one c -> p (one c)")
                        nc.vector.tensor_tensor(qkv, W[:, 2 * s, 0:n], b, ALU.add).then_inc(ph.sem("qkv"), 1)
                        dve.wait_ge(ph.sem("parts_hi"), ph.tiles + (t + 1))
                        for i, hi, dst in ((0, m.q_parts[s][:, :, :, 0, :], m.q_parts[s][:, :, :, 1, :]),
                                           (1, m.k_parts[s][:, :, 0, :, :], m.k_parts[s][:, :, 1, :, :])):
                            src = m.qkv[:, s, i, :, :].rearrange("p h (one d) -> p h one d", one=1)
                            nc.vector.tensor_tensor(dst, src.broadcast_to((P, m.heads, 2, HD1)), hi.bitcast(F32), ALU.subtract)
                        nc.vector.tensor_tensor(m.v_lo[:, tt, :], m.qkv[:, s, 2, :, :].rearrange("p h d -> p (h d)"),
                                                m.v_hi[:, tt, :].bitcast(F32), ALU.subtract).then_inc(ph.sem("v_lo"), 1)

                    def turned1(t):
                        tt = qt * HT + t
                        dve.wait_ge(ph.sem("qk_turned"), ph.tiles + (t + 1))
                        nc.vector.tensor_copy(m.k[:, :, tt * P:(tt + 1) * P], Y[:, 1, :].rearrange("p (h q) -> p h q", q=P))\
                            .then_inc(ph.sem("k_out"), 1)

                    def project3(t):
                        s, tt = t % 2, qt * HT + t
                        H = m.heads + 1
                        dve.wait_ge(ph.sem("proj"), ph.tiles + (t + 1))
                        if t:
                            dve.wait_ge(ph.sem("rot"), ph.tiles + t)
                        cos = m.cos[:, tt, :].rearrange("p (one d) -> p one d", one=1)
                        sin = m.sin[:, tt, :].rearrange("p (one d) -> p one d", one=1).broadcast_to((P, H, HD3 // 2))
                        qk = bank(s)[:, 0:H * HD3]
                        pair = qk.rearrange("p (h two d) -> p h two d", h=H, two=2)
                        out2 = m.by_sin[:, :, :].rearrange("p (h two) d -> p h two d", two=2)
                        nc.vector.tensor_tensor(m.rot[s][:, :, :].rearrange("p h (two d) -> p (h two) d", two=2), qk.rearrange("p (h d) -> p h d", d=HD3 // 2),
                                                cos.broadcast_to((P, 2 * H, HD3 // 2)), ALU.mult)
                        nc.vector.scalar_tensor_tensor(out2[:, :, 0, :], pair[:, :, 1, :], -1.0, sin, ALU.mult, ALU.mult)
                        nc.vector.tensor_tensor(out2[:, :, 1, :], pair[:, :, 0, :], sin, ALU.mult).then_inc(ph.sem("by_sin"), 1)
                        dve.wait_ge(ph.sem("v_hi"), ph.tiles + (t + 1))
                        nc.vector.tensor_tensor(m.v_lo[:, tt, :], W[:, 2 * s + 1, P:2 * P], m.v_hi[:, tt, :].bitcast(F32), ALU.subtract)\
                            .then_inc(ph.sem("v_lo"), 1)

                    def turned3(t):
                        tt = qt * HT + t
                        dve.wait_ge(ph.sem("qk_hi"), ph.tiles + (t + 1))
                        q, kk = slice(t * P, (t + 1) * P), slice(tt * P, (tt + 1) * P)
                        nc.vector.tensor_tensor(m.q_lo[:, :, q], Y[:, 0, :].rearrange("p (h q) -> p h q", q=P),
                                                m.q_hi[:, :, q].bitcast(F32), ALU.subtract)
                        nc.vector.scalar_tensor_tensor(m.k_lo[:, kk], Y[:, 1, 0:P], HD3 ** -0.5, m.k_hi[:, kk].bitcast(F32),
                                                       ALU.mult, ALU.subtract).then_inc(ph.sem("k_out"), 1)

                    def maximum(u, q):
                        row = u * HT + q
                        dve.wait_ge(ph.sem("scores"), ph.rows + (row + 1))
                        nc.vector.tensor_reduce(m.nmax[:, row % 8:row % 8 + 1], bank(row % 2)[:, 0:(qt * HT + q + 1) * P], AX, ALU.max,
                                                negate=True).then_inc(ph.sem("nmax"), 1)

                    def inverse(row):
                        dve.wait_ge(ph.sem("exp"), ph.rows + (row + 1))
                        inv = m.rinv[:, row % 8:row % 8 + 1]
                        nc.vector.reciprocal(inv, m.rsum[:, row % 8:row % 8 + 1]).then_inc(ph.sem("rinv"), 1)
                        if row < HT:
                            dve.wait_ge(ph.sem("rinv"), ph.rows + (row + 1))
                            v = ph.row(0, row)
                            nc.vector.tensor_scalar(v, v, inv, None, ALU.mult).then_inc(ph.sem("norm_0"), 1)

                    def lower(u, j):
                        b = u * ph.nkb + j
                        dve.wait_ge(ph.sem("pt_hi"), ph.blocks + (b + 1))
                        q = slice(ph.cols(j), HALF)
                        s = b % PT_SLOTS
                        nc.vector.tensor_tensor(m.pt_lo[s][:, q], Y[:, s, q], m.pt_hi[s][:, q].bitcast(F32), ALU.subtract)\
                            .then_inc(ph.sem("pt_lo"), 1)

                    def out_lo(u):
                        i, n = (u, ph.units + (u + 1)) if c.kind == ATT3 else (0, ph.no + 1)
                        dve.wait_ge(ph.sem("o_hi"), n)
                        src = m.o_raw if c.kind == ATT3 else Y[:, AV, :]
                        nc.vector.tensor_tensor(m.o_lo[:, i, :], src, m.o_hi[:, i, :].bitcast(F32), ALU.subtract)\
                            .then_inc(ph.sem("o_lo"), 1)

                    proj, turned = (project1, turned1) if c.kind == ATT1 else (project3, turned3)
                    proj(0)
                    for t in range(HT):
                        if t + 1 < HT:
                            proj(t + 1)
                        turned(t)
                    for row in range(AHEAD):
                        maximum(row // HT, row % HT)
                        if row:
                            inverse(row - 1)
                    for u, q, keys, ahead, late in ph.steps():
                        for n, key in enumerate(keys):
                            lower(*key)
                            if n == 0 and ahead:
                                maximum(*ahead)
                        if late:
                            inverse(late[0] * HT + late[1])
                        if c.kind == ATT3 and u and q == 1 - qt:
                            out_lo(u - 1)
                    out_lo(m.heads - 1)
                    for t in range(HT):
                        dve.wait_ge(ph.sem("wo"), ph.no * HT + (t + 1))
                        xs = x[:, qt * HT + t, :]
                        nc.vector.tensor_tensor(xs, Y[:, 2 + t % 2, :], xs, ALU.add).then_inc(sem("x_ready"), 1)

                with dve.Fori(0, m.groups) as g:
                    dve.wait_ge(sem("x_ready"), g * TT + c.xb)
                    phase(g, 0)
                    phase(g, 1)
                xc[0] += TT * m.groups

            for before, c in zip([None] + calls, calls):
                if before is None:
                    dve.wait_ge(sem("x_loaded_0"), 16)
                else:
                    dve.wait_ge(sem("x_ready"), xc[0])
                if not (before and before.prepares):
                    measure(c.half or 0)
                    if chunks[c.cb][1]:
                        dve.wait_ge(sem("const"), 16 * 5)
                        scale(c.cb)
                    turn_in(c.lns[0], c.half or 0)
                    turn(c.ts[0], c.half or 0)
                if before is None:
                    dve.wait_ge(sem("x_loaded_1"), 16)
                if c.kind in GROUPS:
                    measure(1)
                    turn_in(c.lns[1], 1)
                    turn(c.ts[1], 1)
                    attention(c)
                    continue
                dict(FFN0=gated_call, GATE0=gated_call, FFN1=ffn1_call, FFN2=ffn2_call, ATT2=att2_call, FFN3=ffn3_call)[c.kind](c)

        @block.tensor
        def _(pe):
            def turn(n, src=xn):
                for t in range(HT):
                    pe.wait_ge(sem("turn_in"), n * HT + t + 1)
                    if n * HT + t >= 2:
                        pe.wait_ge(sem("xt_lo"), n * HT + t - 1)
                    for k in range(KT):
                        ins = nc.tensor.transpose(W[:, t % 2, k * P:(k + 1) * P], src[:, t, k * P:(k + 1) * P], ident[:, :])
                    ins.then_inc(sem("turned"), 1)
                pe.wait_ge(sem("xt_lo"), (n + 1) * HT)

            def xt(half, k, lo=0, hi=HALF):
                return (xt_hi[:, k, half * HALF + lo:half * HALF + hi], xt_lo[:, k, half * HALF + lo:half * HALF + hi])

            def y_free(c):
                if c.xb:
                    pe.wait_ge(sem("x_ready"), c.xb)

            def gated_call(c):
                steps, cb, after = gated(c)

                def up(i, j=None):
                    off = 0 if j is None else j
                    s, p = (cb + i) % 2, i % 2
                    pe.wait_ge(sem("w_lo_a"), off * 2 + (cb + i + 1))
                    if c.sb + i >= 2:
                        pe.wait_ge(sem("h"), off * 2 + (c.sb + i - 1))
                    if c.kind == GATE0 and i == 0:
                        pe.wait_ge(sem("gate_read"), c.n + 1)
                    for g in range(2):
                        for k in range(KT):
                            w = slice((g * KT + k) * P, (g * KT + k + 1) * P)
                            ins = mm3(W[:, 2 * p + g, :], w_hi[s][:, w], w_lo[s][:, w], *xt(c.half, k), k == 0, k == KT - 1)
                    ins.then_inc(sem("w_free_a"), 1)

                def down(i, j=None):
                    off = 0 if j is None else j
                    s, p = (cb + i) % 2, i % 2
                    pe.wait_ge(sem("w_lo_b"), off * 2 + (cb + i + 1))
                    pe.wait_ge(sem("h_lo"), off * 2 + (c.sb + i + 1))
                    last = i == steps - 1 and not after and j is None
                    for t in range(HT):
                        q = slice(t * P, (t + 1) * P)
                        ins = mm3(Y[:, t, :], h_hi[p][:, q], h_lo[p][:, q], w_hi[s][:, PA:CHUNK], w_lo[s][:, PA:CHUNK],
                                  i == 0 and c.kind == FFN0, last)
                    ins.then_inc(sem("w_free_b"), 1)

                def terms(chunk, lo, m, start, stop, signal):
                    s = chunk % 2
                    pe.wait_ge(sem("term_lo"), (ORDERS + 1) * c.n + m + 1)
                    for t in range(HT):
                        q = slice(t * P, (t + 1) * P)
                        ins = mm3(Y[:, t, :], term_hi[m][:, q], term_lo[m][:, q], w_hi[s][:, lo:lo + D], w_lo[s][:, lo:lo + D],
                                  start, stop)
                    if signal:
                        ins.then_inc(sem(signal), 1)

                if c.kind == GATE0:
                    s = (cb - 1) % 2
                    pe.wait_ge(sem("w_lo_a"), cb)
                    for g in range(2):
                        for k in range(KT):
                            w = slice((g * KT + k) * P, (g * KT + k + 1) * P)
                            ins = mm3(W[:, g, :], w_hi[s][:, w], w_lo[s][:, w], *xt(c.half, k), k == 0, k == KT - 1)
                    ins.then_inc(sem("w_free_a"), 1)
                up(0)
                y_free(c)
                if c.kind == GATE0:
                    pe.wait_ge(sem("w_lo_b"), cb)
                    terms(cb - 1, PA, 0, True, False, "w_free_b")
                up(1)
                down(0)
                with pe.Fori(0, (steps - 2) // 2) as j:
                    for a in range(2):
                        up(2 + a, j)
                        down(1 + a, j)
                down(steps - 1)
                if c.kind == GATE0:
                    for q in range(2):
                        chunk = cb + steps + q
                        pe.wait_ge(sem("w_lo_a"), chunk + 1)
                        terms(chunk, 0, 3 * q + 1, False, False, None)
                        terms(chunk, D, 3 * q + 2, False, False, "w_free_a")
                        pe.wait_ge(sem("w_lo_b"), chunk + 1)
                        terms(chunk, PA, 3 * q + 3, False, q == 1, "w_free_b")

            def parts(chunk, lo, hi, rows=P):
                s = chunk % 2
                return w_hi[s][0:rows, lo:hi], w_lo[s][0:rows, lo:hi]

            def ready(chunk, part):
                pe.wait_ge(sem(f"w_lo_{part}"), chunk + 1)

            def blk(t):
                return t * P, (t + 1) * P

            def ffn1_call(c):
                cb = c.cb
                for chunk, part, ks in ((cb, "a", (0, 1)), (cb, "b", (2,)), (cb + 1, "a", (3,))):
                    ready(chunk, part)
                    for t in range(HT):
                        for k in ks:
                            lo = PA if part == "b" else (k % 3) * D
                            ins = mm3(W[:, t, :], *xt(c.half, k, *blk(t)), *parts(chunk, lo, lo + D), k == 0, k == 3)
                    if chunk == cb:
                        ins.then_inc(sem(f"w_free_{part}"), 1)
                y_free(c)
                for t in range(HT):
                    for k in range(KT):
                        ins = mm3(Y[:, 0, t * P:(t + 1) * P], *xt(c.half, k, *blk(t)), *parts(cb + 1, D + k * P, D + (k + 1) * P),
                                  k == 0, k == KT - 1)
                ins.then_inc(sem("w_free_a"), 1)
                for chunk, part, ks in ((cb + 1, "b", (0,)), (cb + 2, "a", (1, 2)), (cb + 2, "b", (3,))):
                    ready(chunk, part)
                    for t in (1, 2, 3, 0):
                        if chunk == cb + 1 and t == 0:
                            pe.wait_ge(sem("h1_copied"), c.n + 1)
                        for k in ks:
                            lo = PA if part == "b" else (k - 1) * D
                            ins = mm3(Y[:, t, :], *xt(c.half, k, *blk(t)), *parts(chunk, lo, lo + D), k == 0, False)
                    ins.then_inc(sem(f"w_free_{part}"), 1)
                pe.wait_ge(sem("wh"), c.n + 1)
                for t in range(HT):
                    ins = nc.tensor.transpose(W[:, 0, t * P:(t + 1) * P],
                                              wh[:, t * EXP1:(t + 1) * EXP1, :].rearrange("p e r -> p (e r)"), ident[:, :])
                ins.then_inc(sem("wh_turned"), 1)
                ready(cb + 3, "a")
                pe.wait_ge(sem("wht_lo"), c.n + 1)
                for t in range(HT):
                    lo, hi = blk(t)
                    ins = mm3(Y[:, t, :], wht_hi[:, lo:hi], wht_lo[:, lo:hi], *parts(cb + 3, 0, D), False, True)
                ins.then_inc(sem("w_free_a"), 1)
                pe.wait_ge(sem("w_free_b"), cb + 3)
                pe.sem_inc(sem("w_free_b"), 1)

            def ffn2_call(c):
                pe.wait_ge(sem("chan_lo"), c.n // 2 + 1)
                for t in range(HT):
                    for k in range(KT):
                        w = slice(k * E2, (k + 1) * E2)
                        ins = mm3(W[:, 0, t * E2:(t + 1) * E2], *xt(c.half, k, *blk(t)), small2_hi[:, w], small2_lo[:, w],
                                  k == 0, k == KT - 1)
                ins.then_inc(sem("logits"), 1)
                pe.wait_ge(sem("route"), c.n + 1)
                for t in range(HT):
                    ins = nc.tensor.transpose(W[0:E2, 1, t * P:(t + 1) * P], route[:, t, :], ident[:, :])
                ins.then_inc(sem("route_turned"), 1)
                pe.wait_ge(sem("rt_lo"), c.n + 1)
                for t in range(HT):
                    lo, hi = blk(t)
                    mm3(W[:, t, :], rt_hi[0:E2, lo:hi], rt_lo[0:E2, lo:hi], chan_hi[0:E2, 0:D], chan_lo[0:E2, 0:D], True, True)\
                        .then_inc(sem("in_scale"), 1)
                turn(c.ts[1])
                for t in range(HT):
                    lo, hi = blk(t)
                    ins = mm3(W[:, t, :], rt_hi[0:E2, lo:hi], rt_lo[0:E2, lo:hi], chan_hi[0:E2, D:], chan_lo[0:E2, D:], True, True)
                ins.then_inc(sem("out_scale"), 1)
                y_free(c)
                for chunk, part, ks in ((c.cb, "a", (0, 1)), (c.cb, "b", (2,)), (c.cb + 1, "a", (3,))):
                    ready(chunk, part)
                    for t in range(HT):
                        for k in ks:
                            lo = PA if part == "b" else (k % 3) * D
                            x_hi, x_lo = xt(c.half, k, *blk(t))
                            w = w_hi[chunk % 2][:, lo:lo + D]
                            nc.tensor.matmul(Y[:, t, :], x_hi, w, start=k == 0, stop=False)
                            ins = nc.tensor.matmul(Y[:, t, :], x_lo, w, start=False, stop=k == 3)
                    ins.then_inc(sem(f"w_free_{part}"), 1)
                pe.wait_ge(sem("w_free_b"), c.cb + 1)
                pe.sem_inc(sem("w_free_b"), 1)
                pe.wait_ge(sem("out_sc"), c.n + 1)

            def att2_call(c):
                cb = c.cb

                def transform(pieces, last):
                    for k, (chunk, part, lo, signal) in enumerate(pieces):
                        ready(chunk, part)
                        for f in range(4):
                            ins = mm3(Y[:, f, :], *parts(chunk, lo + f * P, lo + (f + 1) * P), *xt(c.half, k), k == 0, k == 3)
                        if signal:
                            ins.then_inc(sem(signal), 1)
                    return ins

                y_free(c)
                transform([(cb, "a", 0, None), (cb, "a", D, "w_free_a"), (cb, "b", PA, "w_free_b"), (cb + 1, "a", 0, "spectrum")], None)
                pe.wait_ge(sem("power_lo"), c.n + 1)
                for part, lo, f in (("a", D, 0), ("b", PA, 1)):
                    ready(cb + 1, part)
                    for t in range(HT):
                        q = slice(*blk(t))
                        ins = mm3(W[:, t, :], power_hi[:, f, q], power_lo[:, f, q], *parts(cb + 1, lo, lo + D), f == 0, False)
                    ins.then_inc(sem(f"w_free_{part}"), 1)
                ready(cb + 2, "a")
                for t in range(HT):
                    q = slice(*blk(t))
                    ins = mm3(W[:, t, :], nyq_hi[0:1, q], nyq_lo[0:1, q], *parts(cb + 2, 0, D, 1), False, True)
                ins.then_inc(sem("correlated"), 1)
                turn(c.ts[1])
                transform([(cb + 2, "a", D, "w_free_a"), (cb + 2, "b", PA, "w_free_b"), (cb + 3, "a", 0, None),
                           (cb + 3, "a", D, "w_free_a")], None)
                pe.wait_ge(sem("w_free_a"), cb + 4)
                pe.sem_inc(sem("spectrum"), 1)
                pe.wait_ge(sem("mix_lo"), c.n + 1)
                for f, (chunk, part, lo, signal) in enumerate([(cb + 3, "b", PA, 1), (cb + 4, "a", 0, 0), (cb + 4, "a", D, 1), (cb + 4, "b", PA, 1)]):
                    ready(chunk, part)
                    for t in range(HT):
                        q = slice(*blk(t))
                        ins = mm3(Y[:, t, :], mix_hi[:, f, q], mix_lo[:, f, q], *parts(chunk, lo, lo + D), f == 0, f == 3)
                    if signal:
                        ins.then_inc(sem(f"w_free_{part}"), 1)

            def ffn3_call(c):
                if c.first:
                    cb = c.cb
                    where = lambda k: ((cb, "a", 0), (cb, "a", D), (cb, "b", PA), (cb + 1, "a", 0), (cb + 1, "a", D), (cb + 1, "b", PA),
                                       (cb + 2, "a", 0), (cb + 2, "a", D))[k]
                    pe.wait_ge(sem("gmat_lo"), c.n // 2 + 1)
                    G = B3 * R3
                    for k in range(4):
                        chunk, part, lo = where(k)
                        ready(chunk, part)
                        for j in range(KT):
                            ins = mm3(W[:, j, 0:G], *parts(chunk, lo + j * P, lo + (j + 1) * P), gmat_hi[:, k * G:(k + 1) * G],
                                      gmat_lo[:, k * G:(k + 1) * G], k == 0, k == 3)
                        if k in (1, 2):
                            ins.then_inc(sem(f"w_free_{part}"), 1)
                    ins.then_inc(sem("eff"), 1)
                    y_free(c)
                    for k in range(4):
                        chunk, part, lo = where(4 + k)
                        ready(chunk, part)
                        for g in range(2):
                            q = slice(k * G + g * P, k * G + (g + 1) * P)
                            ins = mm3(Y[:, g, :], gmat_hi[:, q], gmat_lo[:, q], *parts(chunk, lo, lo + D), k == 0, k == 3)
                        if k < 2:
                            ins.then_inc(sem(f"w_free_{part}"), 1)
                    ins.then_inc(sem("eff"), 1)
                    pe.wait_ge(sem("eff"), c.n + 2)
                    pe.sem_inc(sem("w_free_a"), 1)
                    pe.sem_inc(sem("w_free_b"), 1)
                    pe.wait_ge(sem("eff_lo"), c.n + 2)
                mb = c.mb
                ready(mb + 1, "a")
                hb = slice(c.half * P, (c.half + 1) * P)
                for k in range(KT):
                    mm3(W[:, 0, :], aeff_hi[:, k, hb], aeff_lo[:, k, hb], *xt(c.half, k), k == 0, k == 3)
                for k in range(KT):
                    lo = D + k * R3
                    ins = mm3(W[0:R3, 1, :], *parts(mb + 1, lo, lo + R3), *xt(c.half, k), k == 0, k == 3)
                ins.then_inc(sem("down3"), 1)
                y_free(c)
                for chunk, part, ks in ((mb, "a", (0, 1)), (mb, "b", (2,)), (mb + 1, "a", (3,))):
                    ready(chunk, part)
                    for t in range(HT):
                        for k in ks:
                            lo = PA if part == "b" else (k % 3) * D
                            ins = mm3(Y[:, t, :], *xt(c.half, k, *blk(t)), *parts(chunk, lo, lo + D), k == 0, False)
                    ins.then_inc(sem(f"w_free_{part}"), 1)
                ready(mb + 1, "b")
                pe.wait_ge(sem("h3_lo"), c.n + 1)
                for t in range(HT):
                    q = slice(*blk(t))
                    mm3(Y[:, t, :], h3_hi[:, q], h3_lo[:, q], beff_hi[:, c.half, :], beff_lo[:, c.half, :], False, False)
                    ins = mm3(Y[:, t, :], hs_hi[:, q], hs_lo[:, q], *parts(mb + 1, PA, CHUNK, R3), False, True)
                ins.then_inc(sem("w_free_b"), 1)

            def attention(c):
                m = att[c.kind]

                def phase(g, qt):
                    ph = Phase(c, g, qt)

                    def ready_(i):
                        for part in "ab":
                            pe.wait_ge(sem(f"w_lo_{part}"), ph.chunk + (i + 1))

                    def part_(i, lo, hi):
                        s = ph.w_slot(i)
                        return m.w_hi[s][:, lo:hi], m.w_lo[s][:, lo:hi]

                    def free(i):
                        for part in "ab":
                            pe.sem_inc(sem(f"w_free_{part}"), 1)

                    def project(t):
                        s, tt = t % 2, qt * HT + t
                        if t >= 2:
                            pe.wait_ge(ph.sem("v_lo"), ph.tiles + (t - 1))
                        half, q = tt // HT, blk(tt % HT)
                        for k in range(KT):
                            if c.kind == ATT1:
                                w = part_(0, k * 384, (k + 1) * 384)
                                ins = mm3(W[:, 2 * s, 0:384], *xt(half, k, *q), *w, k == 0, k == KT - 1)
                            else:
                                lo = (k % 2) * 768
                                w = part_(k // 2, lo, lo + D)
                                mm3(W[:, 2 * s, :], *xt(half, k, *q), *w, k == 0, k == KT - 1)
                                w = part_(k // 2, lo + D, lo + 768)
                                ins = mm3(W[:, 2 * s + 1, 0:256], *xt(half, k, *q), *w, k == 0, k == KT - 1)
                        ins.then_inc(ph.sem("proj"), 1)

                    def turned(t):
                        if t:
                            pe.wait_ge(ph.sem("k_out"), ph.tiles + t)
                        if c.kind == ATT1:
                            if t:
                                pe.wait_ge(ph.sem("q_out"), ph.tiles + t)
                            pe.wait_ge(ph.sem("v_lo"), ph.tiles + (t + 1))
                            for b, src in ((0, m.q_parts[t % 2]), (1, m.k_parts[t % 2])):
                                v = src[:, :, :, :, :].rearrange("p h a b d -> p (h a b d)").bitcast(F32)
                                for i in range(4):
                                    ins = nc.tensor.transpose(Y[:, b, i * P:(i + 1) * P], v[:, i * P:(i + 1) * P], ident[:, :])
                        else:
                            pe.wait_ge(ph.sem("rot"), ph.tiles + (t + 1))
                            for h in range(m.heads + 1):
                                ins = nc.tensor.transpose(Y[:, h // 4, (h % 4) * P:(h % 4 + 1) * P], m.rot[t % 2][:, h, :], ident[:, :])
                        ins.then_inc(ph.sem("qk_turned"), 1)

                    def scores(u, q):
                        row, i = u * HT + q, qt * HT + q
                        if row >= 2:
                            pe.wait_ge(ph.sem("exp"), ph.rows + (row - 1))
                        s = row % 2
                        for b in range(i // 4 + 1):
                            lo, hi = b * D, min((i + 1) * P, (b + 1) * D)
                            out_ = W[:, 2 * s + b, 0:hi - lo]
                            diag = hi == (i + 1) * P
                            if c.kind == ATT1:
                                r = slice(64 * (u % 2), 64 * (u % 2) + 64)
                                nc.tensor.matmul(out_, m.q[r, u // 2, q * P:(q + 1) * P], m.k[r, u // 2, lo:hi], start=True, stop=not diag)
                            else:
                                qq = slice(q * P, (q + 1) * P)
                                mm3(out_, m.q_hi[:, u, qq], m.q_lo[:, u, qq], m.k_hi[:, lo:hi], m.k_lo[:, lo:hi], True, not diag)
                        nc.tensor.matmul(W[:, 2 * s + b, i * P - lo:hi - lo], ident_r[:, :], mask_r[:, :], start=False, stop=True)\
                            .then_inc(ph.sem("scores"), 1)

                    def turn_p(u, j):
                        b = u * ph.nkb + j
                        if j == 0 and u == 0:
                            pe.wait_ge(ph.sem("norm_0"), ph.no * HT + HT)
                        elif j == 0:
                            pe.wait_ge(ph.sem("norm"), ph.no * ((m.heads - 1) * HT) + u * HT)
                        if b >= PT_SLOTS:
                            pe.wait_ge(ph.sem("pt_lo"), ph.blocks + (b - PT_SLOTS + 1))
                        for q in range(ph.cols(j) // P, HT):
                            ins = nc.tensor.transpose(Y[:, b % PT_SLOTS, q * P:(q + 1) * P], ph.row(u, q, j * P, (j + 1) * P), ident[:, :])
                        ins.then_inc(ph.sem("p_turned"), 1)

                    def values(u, j):
                        b, lo = u * ph.nkb + j, ph.cols(j)
                        pe.wait_ge(ph.sem("pt_lo"), ph.blocks + (b + 1))
                        if c.kind == ATT1:
                            if j == 0:
                                pe.wait_ge(ph.sem("pad"), ph.units + (u + 1))
                            v_hi, v_lo = m.v_pad[u % 2]
                            start, stop = u == 0 and j == 0, u == m.heads - 1 and j == ph.nkb - 1
                        else:
                            if j == 0 and u:
                                pe.wait_ge(ph.sem("o_out"), ph.units + u)
                            v_hi, v_lo = m.v_hi, m.v_lo
                            start, stop = j == 0, j == ph.nkb - 1
                        s = b % PT_SLOTS
                        ins = mm3(Y[:, AV, lo:HALF], v_hi[:, j, :], v_lo[:, j, :], m.pt_hi[s][:, lo:HALF], m.pt_lo[s][:, lo:HALF], start, stop)
                        if j == ph.nkb - 1:
                            ins.then_inc(ph.sem("av"), 1)

                    if qt == 0:
                        ready_(0)
                        if c.kind == ATT3:
                            ready_(1)
                    project(0)
                    for t in range(HT):
                        if t + 1 < HT:
                            project(t + 1)
                        turned(t)
                    pe.wait_ge(ph.sem("proj"), ph.tiles + HT)
                    if qt:
                        for i in range(2 if c.kind == ATT3 else 1):
                            free(i)
                    pe.wait_ge(ph.sem("k_out"), ph.tiles + HT)
                    if c.kind == ATT1:
                        pe.wait_ge(ph.sem("q_out"), ph.tiles + HT)
                    pe.wait_ge(ph.sem("v_lo"), ph.tiles + HT)
                    pe.wait_ge(sem("x_ready"), ph.x)
                    for row in range(AHEAD):
                        scores(row // HT, row % HT)
                    turned_ = []
                    for u, q, keys, ahead, late in ph.steps():
                        for n, key in enumerate(keys):
                            turn_p(*key)
                            turned_.append(key)
                            if len(turned_) == PT_SLOTS:
                                values(*turned_.pop(0))
                            if n == 0 and ahead:
                                scores(*ahead)
                    for key in turned_:
                        values(*key)
                    pe.wait_ge(ph.sem("o_lo"), ph.units + m.heads if c.kind == ATT3 else ph.no + 1)
                    first = 2 if c.kind == ATT3 else 1
                    if qt == 0:
                        for i in range(first, m.ch):
                            ready_(i)
                    for t in range(HT):
                        if t >= 2:
                            pe.wait_ge(sem("x_ready"), ph.x + (t - 1))
                        n = m.heads if c.kind == ATT3 else 1
                        for h in range(n):
                            w = part_(first + h // 3, (h % 3) * D, (h % 3 + 1) * D)
                            ins = mm3(Y[:, 2 + t % 2, :], m.o_hi[:, h, t * P:(t + 1) * P], m.o_lo[:, h, t * P:(t + 1) * P], *w, h == 0, h == n - 1)
                        ins.then_inc(ph.sem("wo"), 1)
                    if qt:
                        pe.wait_ge(ph.sem("wo"), ph.no * HT + HT)
                        for i in range(first, m.ch):
                            free(i)

                with pe.Fori(0, m.groups) as g:
                    phase(g, 0)
                    phase(g, 1)

            pe.wait_ge(sem("const_r"), 1)
            pe.wait_ge(sem("const"), 16 * 5 if kinds & {FFN0, GATE0} else 32)
            for c in calls:
                if c.kind in GROUPS:
                    turn(c.ts[0])
                    turn(c.ts[1])
                    attention(c)
                    continue
                turn(c.ts[0])
                dict(FFN0=gated_call, GATE0=gated_call, FFN1=ffn1_call, FFN2=ffn2_call, ATT2=att2_call, FFN3=ffn3_call)[c.kind](c)


def _tiles(w):
    n = w.shape[0] // P
    return w.reshape(n, P, KT, P).transpose(0, 3, 2, 1)


def _pad_rows(w, n):
    return np.concatenate([w, np.zeros((n - w.shape[0],) + w.shape[1:], w.dtype)], 0)


def rope_tables():
    inv = 1.0 / 500000.0 ** (np.arange(0, HD3, 2, dtype=np.float32) / HD3)
    wavelen = 2.0 * np.pi / inv
    smooth = (1024 / wavelen - 1.0) / (4.0 - 1.0)
    medium = (wavelen <= 1024) & (wavelen >= 256)
    freq = np.where(medium, (1.0 - smooth) / 8.0 * inv + smooth * inv, np.where(wavelen > 1024, inv / 8.0, inv)).astype(np.float32)
    angle = np.arange(T, dtype=np.float32)[:, None] * freq[None, :]
    return np.cos(angle.astype(np.float64)).astype(np.float32), np.sin(angle.astype(np.float64)).astype(np.float32)


def layout(i):
    f = lambda name: np.asarray(i[name])
    out = []
    w1, w3 = _tiles(f("L0_ffn_w1")), _tiles(f("L0_ffn_w3"))
    w2 = f("L0_ffn_w2").T.reshape(F0_STEPS, P, D)
    out.append(np.concatenate([w1.reshape(F0_STEPS, P, D), w3.reshape(F0_STEPS, P, D), w2], 2))
    up, gate = _tiles(f("L0_attn_up_w"))[0].reshape(P, D), _tiles(f("L0_attn_gate_w"))[0].reshape(P, D)
    out.append(np.concatenate([up, gate, f("L0_attn_local_approx_output").T], 1)[None])
    n = G0_STEPS * P
    fg, fu = (_tiles(_pad_rows(f(f"L0_attn_ffn_{q}_w"), n)).reshape(G0_STEPS, P, D) for q in ("gate", "up"))
    fd = _pad_rows(f("L0_attn_ffn_down_w").T, n).reshape(G0_STEPS, P, D)
    out.append(np.concatenate([fg, fu, fd], 2))
    fuse = f("L0_attn_fuse_weight").transpose(1, 2, 0).reshape(P, 2, CHUNK).transpose(1, 0, 2)
    out.append(fuse)
    zeros = np.zeros((P, D), np.float32)
    kt = lambda w: [w.T[k * P:(k + 1) * P] for k in range(KT)]

    def pack(units):
        units = [np.pad(u, ((0, P - u.shape[0]), (0, D - u.shape[1]))) for u in units]
        units += [zeros] * (-len(units) % 3)
        return np.stack([np.concatenate(units[n:n + 3], 1) for n in range(0, len(units), 3)])

    qk = kt(np.concatenate([f("L1_ffn_Wq"), f("L1_ffn_Wk")], 0))
    down = np.concatenate(kt(f("L1_ffn_A").reshape(EXP1 * RANK1, D)), 1)
    out.append(pack(qk + [down] + kt(f("L1_ffn_W")) + [f("L1_ffn_Bm").transpose(0, 2, 1).reshape(EXP1 * RANK1, D)]))
    for g in range(GROUPS[ATT1]):
        rows_ = slice(g * P, (g + 1) * P)
        out.append(np.concatenate(kt(np.concatenate([f(f"L1_attn_W{q}")[rows_] for q in "qkv"], 0)), 1)[None])
        out.append(pack([f("L1_attn_Wo").T[rows_]]))
    out.append(pack(kt(f("L2_ffn_weight"))))
    lag, freq = np.arange(D), np.arange(D // 2)
    angle = lambda k: 2 * np.pi * (np.outer(lag, k) % D) / D
    fwd = np.concatenate([np.cos(angle(freq)), np.sin(angle(freq))], 1)
    top = np.cos(angle(np.array([D // 2])))[:, 0]
    fwd[:, D // 2] = top
    twice = np.where(freq == 0, 1.0, 2.0)[:, None] / D
    inv_cos, inv_sin = twice * np.cos(angle(freq)).T, -twice * np.sin(angle(freq)).T
    inv_sin[0] = top / D
    rows = lambda m: [m[k * P:(k + 1) * P].astype(np.float32) for k in range(m.shape[0] // P)]
    out.append(pack(rows(fwd) + rows(inv_cos) + [(top / D)[None].astype(np.float32)] + rows(fwd) + rows(inv_cos) + rows(inv_sin)))
    lora_a = f("L3_ffn_lora_A").reshape(NL3 * R3, D)
    lora_b = f("L3_ffn_lora_B").transpose(0, 2, 1).reshape(NL3 * R3, D)
    tiles = lambda w: [w[k * P:(k + 1) * P] for k in range(w.shape[0] // P)]
    out.append(pack(tiles(lora_a) + tiles(lora_b)))
    shared = np.concatenate(kt(f("L3_ffn_lora_A_shared")), 1)
    out.append(pack(tiles(f("L3_ffn_kernel")) + [shared, f("L3_ffn_lora_B_shared").T]))
    for g in range(KV3):
        n = H3 // KV3 * HD3
        qkv = kt(np.concatenate([f("L3_attn_Wq")[g * n:(g + 1) * n]] + [f(f"L3_attn_W{q}")[g * HD3:(g + 1) * HD3] for q in "kv"], 0))
        out += [np.concatenate(qkv[0:2], 1)[None], np.concatenate(qkv[2:4], 1)[None]]
        out.append(pack(tiles(f("L3_attn_Wo").T[g * n:(g + 1) * n])))
    rest = N_DRAM_CHUNKS - sum(o.shape[0] for o in out)
    arrays = {"ident": np.eye(P, dtype=np.float32)}
    s1, s3, s2 = f("L0_ffn_w1_scale"), f("L0_ffn_w3_scale"), f("L0_ffn_w2_scale").T
    arrays["scales"] = np.concatenate([s1, s3, s2], 1)
    arrays["local_point"] = f("L0_attn_local_point").reshape(P, 1)
    arrays["discount"] = f("L0_attn_discount_factor").reshape(1, ORDERS)
    arrays["ffn1_b"], arrays["ffn2_b"], arrays["ffn3_b"] = (f(f"L{n}_ffn_{q}").reshape(1, D) for n, q in ((1, "b"), (2, "bias"), (3, "bias")))
    arrays["router"] = np.concatenate(kt(f("L2_ffn_gate_w")), 1)
    arrays["channel"] = np.concatenate([f("L2_ffn_in_channel_scale"), f("L2_ffn_out_channel_scale")], 1)
    g = f("L3_ffn_gate").T.reshape(4, 4, 1, B3)
    arrays["gate_rep"] = np.broadcast_to(g, (4, 4, R3, B3)).transpose(1, 2, 0, 3).reshape(P, 4 * B3)
    arrays["same_rank"] = np.tile(np.eye(R3, dtype=np.float32), (4, 1))
    arrays["own_block"] = np.kron(np.eye(4, dtype=np.float32), np.ones((R3, P), np.float32))
    arrays["mask"] = np.triu(np.full((P, P), NEG, np.float32), 1)
    qkv_b = np.stack([f(f"L1_attn_b{q}").reshape(GROUPS[ATT1], P) for q in "qkv"], 1)
    arrays["att1_qkv_b"], arrays["att1_o_b"] = qkv_b.reshape(1, 3 * D), f("L1_attn_bo").reshape(1, D)
    cos, sin = rope_tables()
    arrays["rope_cos"], arrays["rope_sin"] = (q.reshape(TT, P, HD3 // 2).transpose(1, 0, 2) for q in (cos, sin))
    if rest:
        out.append(np.zeros((rest, P, CHUNK), np.float32))
    arrays["weights"] = np.concatenate(out, 0)
    assert arrays["weights"].shape[0] == N_DRAM_CHUNKS
    return {k: np.ascontiguousarray(v) for k, v in arrays.items()}


def kernel(**inputs):
    import concourse.bacc as bacc
    from concourse.bass_utils import run_bass_kernel_spmd

    nc = bacc.Bacc("TRN2", target_bir_lowering=False, num_devices=1)
    hidden = np.ascontiguousarray(np.asarray(inputs["L0_attn_hidden_states"]).reshape(T, D))
    arrays = {f"in_{name}": a for name, a in layout(inputs).items()}
    arrays["in_x"] = hidden
    aps = {name: nc.dram_tensor(name, a.shape, mybir.dt.from_np(a.dtype), kind="ExternalInput").ap() for name, a in arrays.items()}
    out = nc.dram_tensor("out", (T, D), F32, kind="ExternalOutput").ap()
    x_in = aps.pop("in_x")
    build(nc, {name[3:]: ap for name, ap in aps.items()}, x_in, out)
    got = run_bass_kernel_spmd(nc, [arrays], core_ids=[0])
    return got.results[0]["out"].reshape(1, T, D)
```

```python
import numpy as np
import concourse.bass as bass
from concourse import mybir

F32 = mybir.dt.float32
F32R = mybir.dt.float32r
ALU = mybir.AluOpType
ACT = mybir.ActivationFunctionType
AX = mybir.AxisListType.X

P = 128
T = 1024
D = 512
TT = T // P
KT = D // P
HT = TT // 2
HALF = T // 2
CHUNK = 3 * D
PA = 2 * D
EPS = 1e-5

FFN0, GATE0, FFN1, ATT1, FFN2, ATT2, FFN3, ATT3 = "FFN0 GATE0 FFN1 ATT1 FFN2 ATT2 FFN3 ATT3".split()
ORDER = [FFN0, GATE0, FFN0, FFN1, ATT1, FFN1, FFN2, ATT2, FFN2, FFN3, ATT3, FFN3]

F0_STEPS = 1792 // P
G0_STEPS = -(-1248 // P)
ORDERS = 6
THD = 2.5
EXP1, DK1, RANK1 = 8, 32, 16
H1, HD1 = 32, 16
E2 = 8
TOPK = int(np.log(D))
H3, KV3, HD3 = 32, 8, 128
NL3, R3, B3 = 16, 32, 8
GROUPS = {ATT1: 4, ATT3: 8}
AHEAD = (HT + 3, HT + 2)
PT_SLOTS = 3
AV = 3
NEG = -1e30
BIG, NONE = 1e30, -3e38

EARLY = {ATT3: 2}

CHUNKS = {FFN0: F0_STEPS, GATE0: G0_STEPS + 3, FFN1: 4, ATT1: 2, FFN2: 2, ATT2: 5, FFN3: 2, ATT3: 4}
EFF_CHUNKS = 3


def chunk_bases():
    base, at = {}, 0
    for kind in (FFN0, GATE0, FFN1, ATT1, FFN2, ATT2, FFN3, ATT3):
        base[kind] = at
        at += CHUNKS[kind] * (GROUPS.get(kind, 1)) + (EFF_CHUNKS if kind == FFN3 else 0)
    return base, at


DRAM_BASE, N_DRAM_CHUNKS = chunk_bases()


class Call:
    pass


def plan(layers):
    calls, chunks = [], []
    xb = steps = t_runs = lns = 0
    for n, kind in enumerate(layers):
        halves = [None] if kind in GROUPS else [0, 1]
        for half in halves:
            c = Call()
            c.kind, c.half, c.first = kind, half, half in (0, None)
            c.xb = xb
            c.sb = steps
            c.cb = len(chunks)
            c.n = sum(1 for q in calls if q.kind == kind)
            base = DRAM_BASE[kind]
            if kind in GROUPS:
                c.lns = [lns, lns + 1]
                lns += 2
                c.ts = [t_runs, t_runs + 1]
                t_runs += 2
                chunks += [(base + g * CHUNKS[kind] + i, False, False) for g in range(GROUPS[kind])
                           for i in range(CHUNKS[kind])]
                xb += TT * GROUPS[kind]
            else:
                c.lns = [lns]
                lns += 1
                if kind == FFN3:
                    if half == 0:
                        chunks += [(base + i, False, False) for i in range(EFF_CHUNKS)]
                    base += EFF_CHUNKS
                c.mb = len(chunks)
                chunks += [(base + i, kind == FFN0, kind == FFN2) for i in range(CHUNKS[kind])]
                c.ts = [t_runs + i for i in range(2 if kind in (FFN2, ATT2) else 1)]
                t_runs += len(c.ts)
                xb += HT
                steps += {FFN0: F0_STEPS, GATE0: G0_STEPS}.get(kind, 0)
            calls.append(c)
    for before, c, after in zip([None] + calls, calls, calls[1:] + [None]):
        c.next = after
        c.early = EARLY.get(before.kind, 1) if before else 0
        c.prepares = after is not None and c.kind not in GROUPS
    return calls, chunks, xb


class Chain:

    def __init__(self, eng, sem):
        self.eng, self.sem, self.value = eng, sem, 0

    def sig(self, ins):
        ins.then_inc(self.sem, 1)
        self.value = self.value + 1

    def wait(self):
        self.eng.wait_ge(self.sem, self.value)

    def link(self, ins):
        self.sig(ins)
        self.wait()


def build(nc, inp, x_in, out, layers=ORDER):
    calls, chunks, x_total = plan(layers)
    kinds = set(layers)
    sems = {}

    def sem(name):
        if name not in sems:
            sems[name] = nc.alloc_semaphore(name)
        return sems[name]

    top = [16512]

    def keep(name, shape, dtype=F32):
        size = int(np.prod(shape[1:])) * 4
        t = nc.alloc_sbuf_tensor_at(name, shape, dtype, offset=top[0])
        top[0] += -(-size // 32) * 32
        return t

    x = keep("x", [P, TT, D])
    xt_hi = keep("xt_hi", [P, KT, T], F32R)
    xt_lo = keep("xt_lo", [P, KT, T], F32R)
    XN_AT = top[0]
    xn = keep("xn", [P, HT, D])
    raw = keep("raw", [P, 2, CHUNK])
    w_hi = [keep(f"w_hi{s}", [P, CHUNK], F32R) for s in range(2)]
    w_lo = [keep(f"w_lo{s}", [P, CHUNK], F32R) for s in range(2)]
    ident = keep("ident", [P, P])
    stats = keep("stats", [P, HT, 6])
    mv = keep("mv", [P, HT, 2])
    var_eps = keep("var_eps", [P, HT])
    rstd = keep("rstd", [P, HT])
    ident_r = keep("ident_r", [P, P], F32R)
    mask = keep("mask", [P, P])
    mask_r = keep("mask_r", [P, P], F32R)
    minus_half = keep("minus_half", [P, HT])
    ARENA = top[0]
    SBUF_END = 229344

    class Arena:

        def __init__(self, tag):
            self.tag, self.at = tag, ARENA

        def __call__(self, name, shape, dtype=F32):
            size = int(np.prod(shape[1:])) * 4
            t = nc.alloc_sbuf_tensor_at(f"{self.tag}_{name}", shape, dtype, offset=self.at)
            self.at += -(-size // 32) * 32
            assert self.at <= SBUF_END, (self.tag, name, self.at - SBUF_END)
            return t

    a = Arena("g")
    s_buf = a("s_buf", [P, 2, D])
    h_buf = a("h_buf", [P, 2, D])
    h_hi = [a(f"h_hi{p}", [P, D], F32R) for p in range(2)]
    h_lo = [a(f"h_lo{p}", [P, D], F32R) for p in range(2)]
    scales = a("scales", [P, F0_STEPS, 3 * KT])
    lpoint = a("lpoint", [P, 1])
    coef = a("coef", [P, ORDERS])
    delta = a("delta", [P, D])
    near = a("near", [P, D])
    term = a("term", [P, ORDERS + 1, D])
    term_hi = [a(f"term_hi{m}", [P, D], F32R) for m in range(ORDERS + 1)]
    term_lo = [a(f"term_lo{m}", [P, D], F32R) for m in range(ORDERS + 1)]

    a = Arena("f1")
    bias1 = a("bias", [P, D])
    q_sb = a("q_sb", [P, HT, EXP1 * DK1])
    h1 = a("h1", [P, HT * EXP1, RANK1])
    prod = a("prod", [P, HT * EXP1, DK1])
    score1 = a("score1", [P, HT, EXP1])
    top1 = a("top1", [P, HT])
    soft1 = a("soft1", [P, HT, EXP1])
    wh = a("wh", [P, HT * EXP1, RANK1])
    wht_hi = a("wht_hi", [P, HALF], F32R)
    wht_lo = a("wht_lo", [P, HALF], F32R)

    a = Arena("f2")
    bias2 = a("bias", [P, D])
    small2 = a("small", [P, KT * E2])
    small2_hi = a("small_hi", [P, KT * E2], F32R)
    small2_lo = a("small_lo", [P, KT * E2], F32R)
    chan = a("chan", [P, 2 * D])
    chan_hi = a("chan_hi", [P, 2 * D], F32R)
    chan_lo = a("chan_lo", [P, 2 * D], F32R)
    logit_t = a("logit_t", [P, HALF])
    logit = a("logit", [P, HT, E2])
    top2 = a("top2", [P, HT])
    route = a("route", [P, HT, E2])
    rt_hi = a("rt_hi", [P, HALF], F32R)
    rt_lo = a("rt_lo", [P, HALF], F32R)
    out_sc = a("out_sc", [P, HT, D])
    scaled_y = a("scaled_y", [P, HT, D])

    a = Arena("a2")
    spec = a("spec", [P, 4, HALF])
    sq = a("sq", [P, 4, HALF])
    power_hi = a("power_hi", [P, 2, HALF], F32R)
    power_lo = a("power_lo", [P, 2, HALF], F32R)
    power_sum = a("power_sum", [P, 2, HALF])
    nyq_hi = a("nyq_hi", [P, HALF], F32R)
    nyq_lo = a("nyq_lo", [P, HALF], F32R)
    corr = a("corr", [P, HT, D + 8])
    marked = a("marked", [P, HT, D + 8])
    ex2 = a("ex2", [P, HT, D])
    top8 = a("top8", [P, HT, 8])
    nmax2 = a("nmax2", [P, HT])
    sum2 = a("sum2", [P, HT])
    cross = a("cross", [P, 4, HALF])
    mix = a("mix", [P, 4, HALF])
    mix_hi = a("mix_hi", [P, 4, HALF], F32R)
    mix_lo = a("mix_lo", [P, 4, HALF], F32R)

    a = Arena("f3")
    bias3 = a("bias", [P, D])
    gate_rep = a("gate_rep", [P, 4 * B3])
    same_rank = a("same_rank", [P, R3])
    own_block = a("own_block", [P, HALF])
    gmat = a("gmat", [P, 4 * B3, R3])
    gmat_hi = a("gmat_hi", [P, 4 * B3 * R3], F32R)
    gmat_lo = a("gmat_lo", [P, 4 * B3 * R3], F32R)
    aeff_hi = a("aeff_hi", [P, KT, B3 * R3], F32R)
    aeff_lo = a("aeff_lo", [P, KT, B3 * R3], F32R)
    beff_hi = a("beff_hi", [P, 2, D], F32R)
    beff_lo = a("beff_lo", [P, 2, D], F32R)
    h3 = a("h3", [P, HALF])
    h3_hi = a("h3_hi", [P, HALF], F32R)
    h3_lo = a("h3_lo", [P, HALF], F32R)
    hs_hi = a("hs_hi", [R3, HALF], F32R)
    hs_lo = a("hs_lo", [R3, HALF], F32R)

    att = {}
    for kind, tag in ((ATT1, "a1"), (ATT3, "a3")):
        a, m = Arena(tag), Call()
        att[kind] = m
        m.tag, m.kind, m.ch = tag, kind, CHUNKS[kind]
        m.heads = {ATT1: H1, ATT3: H3}[kind] // GROUPS[kind]
        m.groups = GROUPS[kind]
        m.prob_at = [sum(HT + i + 1 for i in range(q)) * P for q in range(HT)]
        m.prob = [a(f"prob{i}", [P, m.prob_at[-1] + T]) for i in range(2)]
        if kind == ATT1:
            m.w_hi, m.w_lo = w_hi, w_lo
        else:
            m.w_hi = w_hi + [a(f"w_hi{s}", [P, CHUNK], F32R) for s in (2, 3)]
            m.w_lo = w_lo + [a(f"w_lo{s}", [P, CHUNK], F32R) for s in (2, 3)]
        m.pt_hi = [a(f"pt_hi{i}", [P, HALF], F32R) for i in range(PT_SLOTS)]
        m.pt_lo = [a(f"pt_lo{i}", [P, HALF], F32R) for i in range(PT_SLOTS)]
        m.nmax = a("nmax", [P, 8])
        m.sums = 8 if kind == ATT3 else HT * m.heads
        m.rsum = a("rsum", [P, m.sums])
        m.rinv = a("rinv", [P, m.sums])
        m.v_hi = a("v_hi", [P, TT, P], F32R)
        m.v_lo = a("v_lo", [P, TT, P], F32R)
        if kind == ATT1:
            m.qkv = a("qkv", [P, 2, 3, m.heads, HD1])
            m.bias_qkv = a("bias_qkv", [P, m.groups, 3 * m.heads * HD1])
            m.bias_o = a("bias_o", [P, D])
            m.q_parts = [a(f"q_parts{i}", [P, m.heads, 2, 2, HD1], F32R) for i in range(2)]
            m.k_parts = [a(f"k_parts{i}", [P, m.heads, 2, 2, HD1], F32R) for i in range(2)]
            m.q = a("q", [P, m.heads // 2, HALF], F32R)
            m.k = a("k", [P, m.heads // 2, T], F32R)
            m.v_pad = [[a(f"v_pad_{q}{i}", [P, TT, P], F32R) for q in ("hi", "lo")] for i in range(2)]
            m.zero = a("zero", [P, TT, HD1])
            m.out = a("out", [P, HALF])
            m.o_hi = a("o_hi", [P, 1, HALF], F32R)
            m.o_lo = a("o_lo", [P, 1, HALF], F32R)
        else:
            m.cos = a("cos", [P, TT, HD3 // 2])
            m.sin = a("sin", [P, TT, HD3 // 2])
            m.by_sin = a("by_sin", [P, 2 * (m.heads + 1), HD3 // 2])
            m.o_raw = m.by_sin[:, :, :].rearrange("p h d -> p (h d)")[:, 0:HALF]
            m.rot = [a(f"rot{i}", [P, m.heads + 1, HD3]) for i in range(2)]
            m.q_hi = a("q_hi", [P, m.heads, HALF], F32R)
            m.q_lo = a("q_lo", [P, m.heads, HALF], F32R)
            m.k_hi = a("k_hi", [P, T], F32R)
            m.k_lo = a("k_lo", [P, T], F32R)
            m.o_hi = nc.alloc_sbuf_tensor_at("a3_o_hi", [P, m.heads, HALF], F32R, offset=XN_AT)
            m.o_lo = a("o_lo", [P, m.heads, HALF], F32R)

    Y = nc.alloc_psum_tensor("Y", [P, 4, D], F32)
    W = nc.alloc_psum_tensor("W", [P, 4, D], F32)

    def mm3(o, a_hi, a_lo, b_hi, b_lo, start, stop):
        nc.tensor.matmul(o, a_hi, b_hi, start=start, stop=False)
        nc.tensor.matmul(o, a_lo, b_hi, start=False, stop=False)
        return nc.tensor.matmul(o, a_hi, b_lo, start=False, stop=stop)

    def gated(c):
        if c.kind == FFN0:
            return F0_STEPS, c.cb, 0
        return G0_STEPS, c.cb + 1, 2

    aux = {
        FFN1: [(bias1[:, :], inp["ffn1_b"].broadcast_to((P, D)))],
        FFN2: [(bias2[:, :], inp["ffn2_b"].broadcast_to((P, D))), (small2[:, :], inp["router"]),
               (chan[0:E2, :], inp["channel"])],
        FFN3: [(bias3[:, :], inp["ffn3_b"].broadcast_to((P, D))), (gate_rep[:, :], inp["gate_rep"]),
               (same_rank[:, :], inp["same_rank"]), (own_block[:, :], inp["own_block"])],
    }
    aux[ATT1] = [(att[ATT1].bias_qkv[:, :, :].rearrange("p g c -> p (g c)"), inp["att1_qkv_b"].broadcast_to((P, 3 * D))),
                 (att[ATT1].bias_o[:, :], inp["att1_o_b"].broadcast_to((P, D)))]
    aux[ATT3] = [(att[ATT3].cos[:, :, :], inp["rope_cos"]), (att[ATT3].sin[:, :, :], inp["rope_sin"])]
    aux_total = 0
    for q in calls:
        if q.first:
            aux_total += 16 * len(aux.get(q.kind, []))
        q.aux = aux_total

    class Phase:

        def __init__(self, c, g, qt, later=0):
            m = self.m = att[c.kind]
            self.c, self.g, self.qt = c, g, qt
            self.nkb = (qt + 1) * HT
            self.row_slots = 2 if qt else 4
            per = 2 * m.heads * HT
            at = lambda a_group, more: g * a_group + (later * a_group + more)
            self.tiles = at(TT, qt * HT)
            self.rows = at(per, qt * m.heads * HT)
            self.blocks = at(3 * m.heads * HT, qt * m.heads * HT)
            self.units = at(2 * m.heads, qt * m.heads)
            self.chunk = at(m.ch, c.cb)
            self.no = at(2, qt)
            self.x = at(TT, c.xb + qt * HT)

        def sem(self, name):
            return sem(f"{self.m.tag}_{name}")

        def steps(self):
            for u in range(self.m.heads):
                for q in range(HT):
                    row = lambda n: divmod(n, HT) if n < self.m.heads * HT else None
                    keys = [(u, j) for j in range(q * self.nkb // HT, (q + 1) * self.nkb // HT)]
                    yield u, q, keys, row(u * HT + q + AHEAD[self.qt]), row(u * HT + q + AHEAD[self.qt] - 1)

        def chunks_after(self, u, q):
            early = EARLY.get(self.m.kind, 1)
            return [self.m.ch + u - 1] if self.qt and q == 0 and 1 <= u <= early else []

        def on_dve(self, row):
            return self.qt == 0 or row < HT or row % HT == HT - 1

        def normalised(self, u):
            rows, whole = (u + 1) * HT, self.m.heads * HT
            phases = [Phase(self.c, 0, qt) for qt in range(2)]
            first, second = (sum(ph.on_dve(row) for row in range(whole)) for ph in phases)
            here = sum(self.on_dve(row) for row in range(rows))
            return (self.g * (first + second) + (self.qt * first + here),
                    self.g * (2 * whole - first - second) + (self.qt * (whole - first) + rows - here))

        def w_slot(self, i):
            return (self.c.cb + i) % 2 + (2 if 2 <= i < self.m.ch else 0)

        def row(self, u, q, lo=0, hi=None):
            hi = (self.qt * HT + q + 1) * P if hi is None else hi
            return self.m.prob[u % 2][:, self.m.prob_at[q] + lo:self.m.prob_at[q] + hi]

        def row_bank(self, row):
            return row % self.row_slots * (4 // self.row_slots)

        def scored(self, row, q):
            first, n = self.row_bank(row), (self.qt * HT + q + 1) * P
            return W[:, first:first + 4 // self.row_slots, :].rearrange("p b c -> p (b c)")[:, 0:n]

        def sum_at(self, row):
            m = self.m
            n = row % m.sums if m.kind == ATT3 else row % HT * m.heads + row // HT
            return slice(n, n + 1)

        def cols(self, j):
            return max(0, j - self.qt * HT) * P

    def tok(half, t):
        return half * HALF + t * P

    with nc.Block() as block:

        @block.sync
        def _(sp):
            def load(c, dram, slot):
                if not isinstance(c, int) or c >= 2:
                    sp.wait_ge(sem("w_lo_b"), c - 1)
                sp.dma_start(raw[:, slot, :], inp["weights"][dram]).then_inc(sem(f"raw{slot}"), 16)

            x_tiles = x_in.rearrange("(t p) d -> p t d", p=P)
            sp.dma_start(x[:, 0:HT, :], x_tiles[:, 0:HT, :]).then_inc(sem("x_loaded_0"), 16)
            sp.dma_start(ident[:, :], inp["ident"]).then_inc(sem("const"), 16)
            sp.dma_start(mask[:, :], inp["mask"]).then_inc(sem("const"), 16)
            if kinds & {FFN0, GATE0}:
                every_row = inp["scales"].rearrange("(a s) k -> a s k", a=1).broadcast_to((P, F0_STEPS, 3 * KT))
                sp.dma_start(scales[:, :, :], every_row).then_inc(sem("const"), 16)
                sp.dma_start(lpoint[:, :], inp["local_point"]).then_inc(sem("const"), 16)
                sp.dma_start(coef[:, :], inp["discount"].broadcast_to((P, ORDERS))).then_inc(sem("const"), 16)
            load(0, chunks[0][0], 0)
            sp.dma_start(x[:, HT:TT, :], x_tiles[:, HT:TT, :]).then_inc(sem("x_loaded_1"), 16)
            at_aux = {q.cb + max(1, q.early): q for q in calls if q.first and aux.get(q.kind)}

            def load_aux(n):
                if n in at_aux:
                    q = at_aux.pop(n)
                    if q.xb:
                        sp.wait_ge(sem("x_ready"), q.xb)
                    for dst, src in aux[q.kind]:
                        sp.dma_start(dst, src).then_inc(sem("aux"), 16)

            n = 1
            grouped = {q.cb: q for q in calls if q.kind in GROUPS}
            while n < len(chunks):
                m = n
                if n in grouped:
                    q = grouped[n]
                    per, first, groups = CHUNKS[q.kind], chunks[n][0], GROUPS[q.kind]
                    load(n, first, n % 2)
                    if q.xb:
                        sp.wait_ge(sem("x_ready"), q.xb)
                    for dst, src in aux[q.kind]:
                        sp.dma_start(dst, src).then_inc(sem("aux"), 16)
                    at_aux.pop(n + 1)
                    with sp.Fori(0, groups - 1) as g:
                        for a in range(1, per + 1):
                            load(g * per + (n + a), bass.ds(g * per + (first + a), 1), (n + a) % 2)
                    for a in range((groups - 1) * per + 1, groups * per):
                        load(n + a, first + a, (n + a) % 2)
                    n += per * groups
                    continue
                load_aux(n)
                while m + 1 < len(chunks) and chunks[m + 1][0] == chunks[m][0] + 1 and m + 1 not in at_aux and m + 1 not in grouped:
                    m += 1
                count = m + 1 - n
                while count and (n < 2 or count % 2):
                    load(n, chunks[n][0], n % 2)
                    n, count = n + 1, count - 1
                if count >= 4:
                    with sp.Fori(0, count // 2) as j:
                        for a in range(2):
                            load(j * 2 + (n + a), bass.ds(j * 2 + (chunks[n][0] + a), 1), (n + a) % 2)
                else:
                    for a in range(count):
                        load(n + a, chunks[n + a][0], (n + a) % 2)
                n += count
            sp.wait_ge(sem("x_ready"), x_total)
            sp.dma_start(out.rearrange("(t p) d -> p t d", p=P), x[:, :, :]).then_inc(sem("stored"), 16)
            sp.wait_ge(sem("stored"), 16)

        @block.gpsimd
        def _(pool):
            nc.gpsimd.memset(minus_half[:, :], -0.5).then_inc(sem("pool_const"), 1)

            def split_lo(c, slot, sign=False, w_hi=w_hi, w_lo=w_lo, to=None):
                to = slot if to is None else to
                for part, lo, hi in (("a", 0, PA), ("b", PA, CHUNK)):
                    pool.wait_ge(sem(f"w_hi_{part}"), c + 1)
                    if sign:
                        pool.wait_ge(sem(f"w_lo_{part}"), c)
                        pool.sem_inc(sem(f"w_lo_{part}"), 1)
                    else:
                        nc.gpsimd.tensor_tensor(w_lo[to][:, lo:hi], raw[:, slot, lo:hi], w_hi[to][:, lo:hi].bitcast(F32),
                                                ALU.subtract).then_inc(sem(f"w_lo_{part}"), 1)

            def pow_of(ln):
                pool.wait_ge(sem("var_ready"), ln + 1)
                nc.gpsimd.tensor_tensor(rstd[:, :], var_eps[:, :], minus_half[:, :], ALU.pow).then_inc(sem("rstd"), 1)

            pool.wait_ge(sem("pool_const"), 1)
            at_chunk = {}
            for before, q in zip([None] + calls, calls):
                if q.kind not in GROUPS or before:
                    at = q.cb if before and before.prepares else q.cb + max(1, q.early)
                    if before and before.kind in (FFN0, GATE0):
                        at = sum(gated(before)[0:2]) - 1
                    elif before and before.kind == FFN1:
                        at = before.cb + 2
                    at_chunk.setdefault(at, []).append(q.lns[0])

            def one(c):
                for ln in at_chunk.get(c, []):
                    pow_of(ln)
                split_lo(c, c % 2, chunks[c][2])

            def run_chunks(n, stop):
                while n < stop:
                    def plain(c):
                        return c < stop and c not in at_chunk and not chunks[c][2]
                    one(n)
                    n += 1
                    m = n
                    while plain(m):
                        m += 1
                    pairs = (m - n) // 2
                    if pairs < 2:
                        continue
                    with pool.Fori(0, pairs) as j:
                        for a in range(2):
                            c = n + a
                            split_lo(j * 2 + c, c % 2)
                    n += 2 * pairs

            def attention(c):
                m = att[c.kind]
                one(c.cb)
                pow_of(c.lns[1])
                if c.kind == ATT1:
                    for pads in m.v_pad:
                        for v in pads:
                            nc.gpsimd.memset(v[:, :, :].bitcast(F32), 0.0).then_inc(sem("pool_pad"), 1)
                    nc.gpsimd.memset(m.zero[:, :, :], 0.0).then_inc(sem("pool_pad"), 1)
                    pool.wait_ge(sem("pool_pad"), 5)

                def phase(g, qt):
                    ph = Phase(c, g, qt)

                    def pad(u):
                        if u >= 2:
                            pool.wait_ge(ph.sem("av"), ph.units + (u - 1))
                        old, new = ((u - 2) % m.heads) * HD1, u * HD1
                        for v, src in zip(m.v_pad[u % 2], (m.v_hi, m.v_lo)):
                            nc.gpsimd.tensor_tensor(v[:, :, old:old + HD1], m.zero[:, :, :], m.zero[:, :, :], ALU.add)
                            ins = nc.gpsimd.tensor_copy(v[:, 0:ph.nkb, new:new + HD1], src[:, 0:ph.nkb, new:new + HD1].bitcast(F32))
                        ins.then_inc(ph.sem("pad"), 1)

                    def normalise(u, q):
                        row = u * HT + q
                        pool.wait_ge(ph.sem("rinv"), ph.rows + (row + 1))
                        v, n = ph.row(u, q), (qt * HT + q + 1) * P
                        nc.gpsimd.tensor_tensor(v, v, m.rinv[:, ph.sum_at(row)].broadcast_to((P, n)), ALU.mult)\
                            .then_inc(ph.sem("norm_pool"), 1)

                    def lo(i):
                        split_lo(ph.chunk + i, (c.cb + i) % 2, w_hi=m.w_hi, w_lo=m.w_lo, to=ph.w_slot(i))

                    if qt == 0 and c.kind == ATT1:
                        lo(1)
                    if c.kind == ATT3:
                        for t in range(HT):
                            pool.wait_ge(ph.sem("by_sin"), ph.tiles + (t + 1))
                            rot = m.rot[t % 2][:, :, :].rearrange("p h d -> p (h d)")
                            nc.gpsimd.tensor_tensor(rot, rot, m.by_sin[:, :, :].rearrange("p h d -> p (h d)"), ALU.add)\
                                .then_inc(ph.sem("rot"), 1)
                        if qt == 0:
                            lo(2)
                            lo(3)
                    else:
                        pool.wait_ge(ph.sem("v_lo"), ph.tiles + HT)
                        pad(0)
                        pad(1)
                    if c.kind == ATT3 and qt:
                        for row in range(HT, AHEAD[qt] - 1):
                            if not ph.on_dve(row):
                                normalise(row // HT, row % HT)
                    for u, q, keys, ahead, late in ph.steps():
                        if late and c.kind == ATT3 and not ph.on_dve(late[0] * HT + late[1]):
                            normalise(*late)
                        if c.kind == ATT1 and u and u + 1 < m.heads and late == (u + 1, HT - 1):
                            pad(u + 1)
                        for i in ph.chunks_after(u, q):
                            lo(i)

                if c.kind == ATT3:
                    split_lo(c.cb + 1, (c.cb + 1) % 2)
                with pool.Fori(0, m.groups) as g:
                    phase(g, 0)
                    phase(g, 1)

            skip = 0
            for n, c in enumerate(calls):
                stop = calls[n + 1].cb if n + 1 < len(calls) else len(chunks)
                if c.kind in GROUPS:
                    attention(c)
                    skip = 1
                else:
                    run_chunks(c.cb + (c.early if skip else 0), stop)
                    skip = 0

        @block.scalar
        def _(act):
            def split_hi(c, part, loop=None):
                if c >= len(chunks):
                    return
                slot = c % 2
                _, scaled, sign = chunks[c]
                off = 0 if loop is None else loop
                if scaled:
                    k = sum(1 for q in chunks[:c + 1] if q[1])
                    act.wait_ge(sem("scaled"), off * 2 + k)
                else:
                    act.wait_ge(sem(f"raw{slot}"), off * 16 + 16 * (c // 2 + 1))
                if c >= 2:
                    act.wait_ge(sem(f"w_free_{part}"), off * 2 + (c - 1))
                lo, hi = (0, PA) if part == "a" else (PA, CHUNK)
                nc.scalar.activation(w_hi[slot][:, lo:hi], raw[:, slot, lo:hi], ACT.Sign if sign else ACT.Copy)\
                    .then_inc(sem(f"w_hi_{part}"), 1)

            def turn(n, half):
                for t in range(HT):
                    act.wait_ge(sem("turned"), n * HT + t + 1)
                    nc.scalar.activation(xt_hi[:, :, tok(half, t):tok(half, t) + P],
                                         W[:, t, :].rearrange("p (k q) -> p k q", k=KT), ACT.Copy).then_inc(sem("xt_hi"), 1)

            def gate0_terms(c, ms):
                for m in ms:
                    act.wait_ge(*((sem("term"), ORDERS * c.n + m) if m else (sem("up_copied"), c.n + 1)))
                    kw = {} if m == 0 else dict(scale=coef[:, m - 1:m])
                    nc.scalar.activation(term_hi[m][:, :], term[:, m, :], ACT.Copy if m == 0 else ACT.Identity, **kw)\
                        .then_inc(sem("term_hi"), 1)

            def gated_call(c):
                steps, cb, _ = gated(c)
                if c.kind == GATE0:
                    split_hi(cb, "a")
                    act.wait_ge(sem("w_free_a"), cb)
                    nc.scalar.activation(term[:, 0, :], W[:, 0, :], ACT.Copy).then_inc(sem("up_copied"), 1)
                    gate0_terms(c, [0])
                    split_hi(cb, "b")

                def step(i, j=None):
                    off = 0 if j is None else j
                    split_hi(cb + i + 1, "a", j)
                    p = i % 2
                    act.wait_ge(sem("w_free_a"), off * 2 + (cb + i + 1))
                    nc.scalar.activation(s_buf[:, p, :], W[:, 2 * p, :], ACT.Silu).then_inc(sem("silu"), 1)
                    act.wait_ge(sem("h"), off * 2 + (c.sb + i + 1))
                    nc.scalar.activation(h_hi[p][:, :], h_buf[:, p, :], ACT.Copy).then_inc(sem("h_hi"), 1)
                    split_hi(cb + i + 1, "b", j)

                step(0)
                if c.kind == GATE0:
                    gate0_terms(c, [1, 2])
                step(1)
                if c.kind == GATE0:
                    gate0_terms(c, [3, 4, 5, 6])
                with act.Fori(0, (steps - 4) // 2) as j:
                    step(2, j)
                    step(3, j)
                step(steps - 2)
                step(steps - 1)
                if c.kind == GATE0:
                    for q in (1, 2):
                        for part in "ab":
                            split_hi(cb + steps + q, part)

            def split(c):
                split_hi(c, "a")
                split_hi(c, "b")

            def ffn1_call(c):
                cb = c.cb
                split(cb + 1)
                split(cb + 2)
                act.wait_ge(sem("w_free_a"), cb + 2)
                nc.scalar.activation(q_sb[:, :, :], W[:, :, 0:EXP1 * DK1], ACT.Copy).then_inc(sem("q_copied"), 1)
                nc.scalar.activation(h1[:, :, :], Y[:, 0, :].rearrange("p (e r) -> p e r", r=RANK1), ACT.Copy)\
                    .then_inc(sem("h1_copied"), 1)
                split(cb + 3)
                act.wait_ge(sem("score1"), c.n + 1)
                nc.scalar.activation(soft1[:, :, :], score1[:, :, :], ACT.Exp, scale=DK1 ** -0.5).then_inc(sem("exp1"), 1)
                act.wait_ge(sem("wh_turned"), c.n + 1)
                nc.scalar.activation(wht_hi[:, :], W[:, 0, :], ACT.Copy).then_inc(sem("wht_hi"), 1)
                split(cb + 4)

            def ffn2_call(c):
                if c.first:
                    act.wait_ge(sem("aux"), c.aux)
                    nc.scalar.activation(small2_hi[:, :], small2[:, :], ACT.Copy)
                    nc.scalar.activation(chan_hi[0:E2, :], chan[0:E2, :], ACT.Copy).then_inc(sem("chan_hi"), 1)
                act.wait_ge(sem("logits_t"), c.n + 1)
                nc.scalar.activation(logit_t[0:E2, :], W[0:E2, 1, :], ACT.Copy).then_inc(sem("logits_copied"), 1)
                split(c.cb + 1)
                act.wait_ge(sem("logit"), c.n + 1)
                nc.scalar.activation(route[:, :, :], logit[:, :, :], ACT.Exp).then_inc(sem("exp2"), 1)
                act.wait_ge(sem("route_turned"), c.n + 1)
                nc.scalar.activation(rt_hi[0:E2, :], W[0:E2, 1, :], ACT.Copy).then_inc(sem("rt_hi"), 1)
                turn(c.ts[1], c.half)
                act.wait_ge(sem("out_scale"), c.n + 1)
                nc.scalar.activation(out_sc[:, :, :], W[:, :, :], ACT.Copy).then_inc(sem("out_sc"), 1)
                split(c.cb + 2)

            def att2_call(c):
                cb = c.cb
                split(cb + 1)
                split(cb + 2)
                act.wait_ge(sem("spectrum"), 2 * c.n + 1)
                for f in range(2):
                    nc.scalar.activation(sq[:, f:4:2, :], Y[:, f:4:2, :], ACT.Square).then_inc(sem("sq"), 1)
                act.wait_ge(sem("sq"), 2 * c.n + 1)
                nc.scalar.activation(nyq_hi[0:1, :], sq[0:1, 2, :], ACT.Copy)
                for f in range(2):
                    act.wait_ge(sem("power"), 2 * c.n + f + 1)
                    nc.scalar.activation(power_hi[:, f, :], power_sum[:, f, :], ACT.Copy).then_inc(sem("power_hi"), 1)
                nc.scalar.activation(spec[:, :, :], Y[:, :, :], ACT.Copy).then_inc(sem("spec"), 1)
                split(cb + 3)
                act.wait_ge(sem("correlated"), c.n + 1)
                for t in range(HT):
                    nc.scalar.activation(corr[:, t, 0:D], W[:, t, :], ACT.Copy).then_inc(sem("corr"), 1)
                for t in range(HT):
                    act.wait_ge(sem("nmax2"), c.n * HT + t + 1)
                    nc.scalar.activation(ex2[:, t, :], W[:, t, :], ACT.Exp, bias=nmax2[:, t:t + 1]).then_inc(sem("ex2"), 1)
                turn(c.ts[1], c.half)
                split(cb + 4)
                for f in range(4):
                    act.wait_ge(sem("mix"), 4 * c.n + f + 1)
                    nc.scalar.activation(mix_hi[:, f, :], mix[:, f, :], ACT.Copy).then_inc(sem("mix_hi"), 1)
                split(cb + 5)

            def ffn3_call(c):
                if c.first:
                    if c.early < 2:
                        split(c.cb + 1)
                    act.wait_ge(sem("gmat"), c.n // 2 + 1)
                    nc.scalar.activation(gmat_hi[:, :], gmat[:, :, :].rearrange("p b r -> p (b r)"), ACT.Copy).then_inc(sem("gmat_hi"), 1)
                    split(c.cb + 2)
                    act.wait_ge(sem("eff"), c.n + 1)
                    nc.scalar.activation(aeff_hi[:, :, :], W[:, :, 0:B3 * R3], ACT.Copy).then_inc(sem("eff_hi"), 1)
                    split(c.cb + 3)
                    act.wait_ge(sem("eff"), c.n + 2)
                    nc.scalar.activation(beff_hi[:, :, :], Y[:, 0:2, :], ACT.Copy).then_inc(sem("eff_hi"), 1)
                split(c.mb + 1)
                act.wait_ge(sem("h3"), c.n + 1)
                nc.scalar.activation(h3_hi[:, :], h3[:, :], ACT.Copy)
                nc.scalar.activation(hs_hi[:, :], W[0:R3, 1, :], ACT.Copy).then_inc(sem("h3_hi"), 1)
                split(c.mb + 2)

            def attention(c):
                m = att[c.kind]

                def phase(g, qt):
                    ph = Phase(c, g, qt)

                    def hi(i):
                        slot = (c.cb + i) % 2
                        for part in "ab":
                            act.wait_ge(sem(f"raw{slot}"), g * (16 * m.ch // 2) + 16 * ((c.cb + i) // 2 + 1))
                            act.wait_ge(sem(f"w_free_{part}"), ph.chunk + (i + 1 - m.ch))
                            lo, hi_ = (0, PA) if part == "a" else (PA, CHUNK)
                            nc.scalar.activation(m.w_hi[ph.w_slot(i)][:, lo:hi_], raw[:, slot, lo:hi_], ACT.Copy)\
                                .then_inc(sem(f"w_hi_{part}"), 1)

                    def project1(t):
                        s, tt = t % 2, qt * HT + t
                        act.wait_ge(ph.sem("qkv"), ph.tiles + (t + 1))
                        for i, dst in ((0, m.q_parts[s][:, :, :, 0, :]), (1, m.k_parts[s][:, :, 0, :, :])):
                            src = m.qkv[:, s, i, :, :].rearrange("p h (one d) -> p h one d", one=1)
                            nc.scalar.activation(dst, src.broadcast_to((P, m.heads, 2, HD1)), ACT.Copy)
                        nc.scalar.activation(m.v_hi[:, tt, :], m.qkv[:, s, 2, :, :].rearrange("p h d -> p (h d)"), ACT.Copy)\
                            .then_inc(ph.sem("parts_hi"), 1)

                    def turned1(t):
                        act.wait_ge(ph.sem("qk_turned"), ph.tiles + (t + 1))
                        nc.scalar.activation(m.q[:, :, t * P:(t + 1) * P], Y[:, 0, :].rearrange("p (h q) -> p h q", q=P), ACT.Copy,
                                             scale=HD1 ** -0.5).then_inc(ph.sem("q_out"), 1)

                    def project3(t):
                        s, tt = t % 2, qt * HT + t
                        act.wait_ge(ph.sem("by_sin"), ph.tiles + (t + 1))
                        nc.scalar.activation(m.v_hi[:, tt, :], W[:, 2 * s + 1, P:2 * P], ACT.Copy).then_inc(ph.sem("v_hi"), 1)

                    def turned3(t):
                        tt = qt * HT + t
                        act.wait_ge(ph.sem("qk_turned"), ph.tiles + (t + 1))
                        nc.scalar.activation(m.q_hi[:, :, t * P:(t + 1) * P], Y[:, 0, :].rearrange("p (h q) -> p h q", q=P), ACT.Copy)
                        nc.scalar.activation(m.k_hi[:, tt * P:(tt + 1) * P], Y[:, 1, 0:P], ACT.Copy, scale=HD3 ** -0.5)\
                            .then_inc(ph.sem("qk_hi"), 1)

                    def exponent(u, q):
                        row = u * HT + q
                        act.wait_ge(ph.sem("nmax"), ph.rows + (row + 1))
                        nc.scalar.activation(ph.row(u, q), ph.scored(row, q), ACT.Exp, bias=m.nmax[:, row % 8:row % 8 + 1],
                                             accum_out=m.rsum[:, ph.sum_at(row)]).then_inc(ph.sem("exp"), 1)

                    def upper(u, j):
                        b = u * ph.nkb + j
                        act.wait_ge(ph.sem("p_turned"), ph.blocks + (b + 1))
                        s = b % PT_SLOTS
                        nc.scalar.activation(m.pt_hi[s][:, ph.cols(j):HALF], Y[:, s, ph.cols(j):HALF], ACT.Copy).then_inc(ph.sem("pt_hi"), 1)

                    def out(u):
                        act.wait_ge(ph.sem("av"), ph.units + (u + 1))
                        if u:
                            act.wait_ge(ph.sem("o_lo"), ph.units + u)
                        nc.scalar.activation(m.o_raw, Y[:, AV, :], ACT.Copy).then_inc(ph.sem("o_out"), 1)

                    def out_hi(u):
                        act.wait_ge(ph.sem("o_out"), ph.units + (u + 1))
                        nc.scalar.activation(m.o_hi[:, u, :], m.o_raw, ACT.Copy).then_inc(ph.sem("o_hi"), 1)

                    if qt == 0 and c.kind == ATT1:
                        hi(1)
                    proj, turned = (project1, turned1) if c.kind == ATT1 else (project3, turned3)
                    proj(0)
                    for t in range(HT - 1):
                        proj(t + 1)
                        turned(t)
                        if c.kind == ATT3 and qt == 0 and t < 2:
                            hi(2 + t)
                    exponent(0, 0)
                    turned(HT - 1)
                    for row in range(1, AHEAD[qt] - 1):
                        exponent(row // HT, row % HT)
                    for u, q, keys, ahead, late in ph.steps():
                        for n, key in enumerate(keys):
                            upper(*key)
                            if n == 0 and late:
                                exponent(*late)
                        if c.kind == ATT3 and u and q == 1 - qt:
                            out(u - 1)
                        if c.kind == ATT3 and u and q == 2 - qt:
                            out_hi(u - 1)
                        for i in ph.chunks_after(u, q):
                            hi(i)
                    if c.kind == ATT3:
                        out(m.heads - 1)
                        out_hi(m.heads - 1)
                    else:
                        act.wait_ge(ph.sem("out"), ph.no + 1)
                        nc.scalar.activation(m.o_hi[:, 0, :], m.out[:, :], ACT.Copy).then_inc(ph.sem("o_hi"), 1)

                for part in "ab":
                    act.wait_ge(sem(f"w_free_{part}"), c.cb)
                if c.kind == ATT3:
                    split(c.cb + 1)
                with act.Fori(0, m.groups) as g:
                    phase(g, 0)
                    phase(g, 1)

            if GATE0 in kinds:
                act.wait_ge(sem("const"), 16 * 5)
                nc.scalar.activation(coef[:, :], coef[:, :], ACT.Exp, scale=-1.0).then_inc(sem("coef"), 1)
                act.wait_ge(sem("coef"), 1)
            split_hi(0, "a")
            split_hi(0, "b")
            act.wait_ge(sem("const"), 32)
            nc.scalar.activation(ident_r[:, :], ident[:, :], ACT.Copy)
            nc.scalar.activation(mask_r[:, :], mask[:, :], ACT.Copy).then_inc(sem("const_r"), 1)
            for c in calls:
                if c.kind in GROUPS:
                    turn(c.ts[0], 0)
                    turn(c.ts[1], 1)
                    attention(c)
                    continue
                turn(c.ts[0], c.half)
                dict(FFN0=gated_call, GATE0=gated_call, FFN1=ffn1_call, FFN2=ffn2_call, ATT2=att2_call, FFN3=ffn3_call)[c.kind](c)

        @block.vector
        def _(dve):
            chain = Chain(dve, sem("dve"))
            xc = [0]

            def measure(half):
                for t in range(HT):
                    ins = nc.vector.bn_stats(stats[:, t, :], x[:, half * HT + t, :])
                chain.link(ins)
                for t in range(HT):
                    ins = nc.vector.bn_aggr(mv[:, t, :], stats[:, t, :])
                chain.link(ins)
                nc.vector.tensor_scalar(var_eps[:, :], mv[:, :, 1], EPS, None, ALU.add).then_inc(sem("var_ready"), 1)

            def turn_in(ln, half):
                dve.wait_ge(sem("rstd"), ln + 1)
                for t in range(HT):
                    nc.vector.tensor_scalar(xn[:, t, :], x[:, half * HT + t, :], mv[:, t, 0:1], rstd[:, t:t + 1],
                                            ALU.subtract, ALU.mult).then_inc(sem("turn_in"), 1)

            def turn(n, half):
                for t in range(HT):
                    dve.wait_ge(sem("xt_hi"), n * HT + t + 1)
                    sl = slice(tok(half, t), tok(half, t) + P)
                    nc.vector.tensor_tensor(xt_lo[:, :, sl], W[:, t, :].rearrange("p (k q) -> p k q", k=KT),
                                            xt_hi[:, :, sl].bitcast(F32), ALU.subtract).then_inc(sem("xt_lo"), 1)

            def normalise_next(c):
                if c.prepares:
                    measure(c.next.half or 0)
                    turn_in(c.next.lns[0], c.next.half or 0)

            def prepare(c, normalised=False):
                if c.prepares:
                    half = c.next.half or 0
                    if not normalised:
                        normalise_next(c)
                    if c.next.kind == FFN0 and c.kind != FFN0:
                        scale(c.next.cb)
                    turn(c.next.ts[0], half)

            def scale(n, j=None):
                slot, step = n % 2, chunks[n][0] - DRAM_BASE[FFN0]
                off, at = (0, slice(step, step + 1)) if j is None else (j, bass.ds(j * 2 + step, 1))
                dve.wait_ge(sem(f"raw{slot}"), off * 16 + 16 * (n // 2 + 1))
                v = raw[:, slot, :].rearrange("p (b f) -> p b f", f=P)
                sc = scales[:, at, :].rearrange("p one k -> p k one")
                nc.vector.tensor_tensor(v, v, sc.broadcast_to((P, 3 * KT, P)), ALU.mult).then_inc(sem("scaled"), 1)

            def residual(half, coef_, name, count):
                dve.wait_ge(sem(name), count)
                for t in range(HT):
                    nc.vector.scalar_tensor_tensor(x[:, half * HT + t, :], Y[:, t, :], coef_, x[:, half * HT + t, :],
                                                   ALU.mult, ALU.add).then_inc(sem("x_ready"), 1)
                    xc[0] += 1

            def term_lo_of(c, ms):
                for m in ms:
                    dve.wait_ge(sem("term_hi"), (ORDERS + 1) * c.n + m + 1)
                    if m == 0:
                        ins = nc.vector.tensor_tensor(term_lo[0][:, :], term[:, 0, :], term_hi[0][:, :].bitcast(F32), ALU.subtract)
                    else:
                        ins = nc.vector.scalar_tensor_tensor(term_lo[m][:, :], term[:, m, :], coef[:, m - 1:m],
                                                             term_hi[m][:, :].bitcast(F32), ALU.mult, ALU.subtract)
                    ins.then_inc(sem("term_lo"), 1)

            def gated_call(c):
                steps, cb, after = gated(c)

                def step(i, j=None):
                    off = 0 if j is None else j
                    p = i % 2
                    dve.wait_ge(sem("silu"), off * 2 + (c.sb + i + 1))
                    nc.vector.tensor_tensor(h_buf[:, p, :], W[:, 2 * p + 1, :], s_buf[:, p, :], ALU.mult).then_inc(sem("h"), 1)
                    dve.wait_ge(sem("h_hi"), off * 2 + (c.sb + i + 1))
                    nc.vector.tensor_tensor(h_lo[p][:, :], h_buf[:, p, :], h_hi[p][:, :].bitcast(F32), ALU.subtract)\
                        .then_inc(sem("h_lo"), 1)

                def power(m):
                    ins = nc.vector.tensor_tensor(term[:, m, :], term[:, m - 1, :], delta[:, :], ALU.mult)
                    if m == 5:
                        chain.link(ins)
                        ins = nc.vector.tensor_tensor(term[:, m, :], term[:, m, :], near[:, :], ALU.mult)
                    ins.then_inc(sem("term"), 1)
                    dve.wait_ge(sem("term"), ORDERS * c.n + m)

                if c.kind == GATE0:
                    if c.n == 0:
                        dve.wait_ge(sem("const"), 16 * 5)
                        dve.wait_ge(sem("coef"), 1)
                    dve.wait_ge(sem("w_free_a"), cb)
                    chain.link(nc.vector.tensor_scalar(delta[:, :], W[:, 1, :], lpoint[:, 0:1], None, ALU.subtract))
                    dve.wait_ge(sem("up_copied"), c.n + 1)
                    chain.link(nc.vector.tensor_scalar(near[:, :], delta[:, :], -THD, None, ALU.is_ge))
                    nc.vector.scalar_tensor_tensor(near[:, :], delta[:, :], THD, near[:, :], ALU.is_le, ALU.mult)\
                        .then_inc(sem("gate_read"), 1)
                    dve.wait_ge(sem("gate_read"), c.n + 1)
                    term_lo_of(c, (0,))
                    step(0)
                    for m in (1, 2):
                        power(m)
                    term_lo_of(c, (1, 2))
                    step(1)
                    for m in (3, 4, 5, 6):
                        power(m)
                    term_lo_of(c, (3, 4, 5, 6))
                else:
                    scale(cb + 1)
                    step(0)
                    scale(cb + 2)
                    step(1)
                    scale(cb + 3)
                with dve.Fori(0, (steps - 4) // 2) as j:
                    for a in (2, 3):
                        step(a, j)
                        if c.kind == FFN0:
                            scale(cb + a + 2, j)
                if c.prepares:
                    measure(c.next.half or 0)
                step(steps - 2)
                if c.kind == FFN0 and c.next and c.next.kind == FFN0:
                    scale(c.next.cb)
                if c.prepares:
                    turn_in(c.next.lns[0], c.next.half or 0)
                step(steps - 1)
                prepare(c, True)
                residual(c.half, 0.5 if c.kind == FFN0 else 1.0, "w_free_b", cb + steps + after)

            def add_bias(c, bias):
                dve.wait_ge(sem("aux"), c.aux)
                xs = x[:, c.half * HT:(c.half + 1) * HT, :]
                b = bias[:, :].rearrange("p (one d) -> p one d", one=1).broadcast_to((P, HT, D))
                dve.wait_ge(sem("turn_in"), (c.ts[0] + 1) * HT)
                chain.link(nc.vector.scalar_tensor_tensor(xs, b, 0.5, xs, ALU.mult, ALU.add))

            def over(ap, n):
                return ap.rearrange("p (m one) -> p m one", one=1).broadcast_to((ap.shape[0], ap.shape[1], n))

            def ffn1_call(c):
                add_bias(c, bias1)
                normalise_next(c)
                dve.wait_ge(sem("q_copied"), c.n + 1)
                chain.link(nc.vector.tensor_tensor(prod[:, :, :].rearrange("p (t e) d -> p t (e d)", t=HT), W[:, :, EXP1 * DK1:D],
                                                   q_sb[:, :, :], ALU.mult))
                s2 = score1[:, :, :].rearrange("p t e -> p (t e)")
                chain.link(nc.vector.tensor_reduce(s2, prod[:, :, :], AX, ALU.add))
                chain.link(nc.vector.tensor_reduce(top1[:, :], score1[:, :, :], AX, ALU.max))
                nc.vector.tensor_tensor(score1[:, :, :], score1[:, :, :], over(top1[:, :], EXP1), ALU.subtract).then_inc(sem("score1"), 1)
                dve.wait_ge(sem("exp1"), c.n + 1)
                chain.link(nc.vector.tensor_reduce(top1[:, :], soft1[:, :, :], AX, ALU.add))
                chain.link(nc.vector.reciprocal(top1[:, :], top1[:, :]))
                chain.link(nc.vector.tensor_tensor(soft1[:, :, :], soft1[:, :, :], over(top1[:, :], EXP1), ALU.mult))
                dve.wait_ge(sem("h1_copied"), c.n + 1)
                nc.vector.tensor_tensor(wh[:, :, :], h1[:, :, :], over(soft1[:, :, :].rearrange("p t e -> p (t e)"), RANK1), ALU.mult)\
                    .then_inc(sem("wh"), 1)
                dve.wait_ge(sem("wht_hi"), c.n + 1)
                nc.vector.tensor_tensor(wht_lo[:, :], W[:, 0, :], wht_hi[:, :].bitcast(F32), ALU.subtract).then_inc(sem("wht_lo"), 1)
                prepare(c, True)
                residual(c.half, 0.5, "w_free_a", c.cb + 4)

            def ffn2_call(c):
                add_bias(c, bias2)
                if c.first:
                    dve.wait_ge(sem("chan_hi"), c.n // 2 + 1)
                    nc.vector.tensor_tensor(small2_lo[:, :], small2[:, :], small2_hi[:, :].bitcast(F32), ALU.subtract)
                    nc.vector.tensor_tensor(chan_lo[0:E2, :], chan[0:E2, :], chan_hi[0:E2, :].bitcast(F32), ALU.subtract)\
                        .then_inc(sem("chan_lo"), 1)
                dve.wait_ge(sem("logits"), c.n + 1)
                lg = W[:, 0, 0:HT * E2].rearrange("p (t e) -> p t e", e=E2)
                chain.link(nc.vector.tensor_reduce(top2[:, :], lg, AX, ALU.max))
                nc.vector.tensor_tensor(logit[:, :, :], lg, over(top2[:, :], E2), ALU.subtract).then_inc(sem("logit"), 1)
                dve.wait_ge(sem("exp2"), c.n + 1)
                chain.link(nc.vector.tensor_reduce(top2[:, :], route[:, :, :], AX, ALU.add))
                chain.link(nc.vector.reciprocal(top2[:, :], top2[:, :]))
                nc.vector.tensor_tensor(route[:, :, :], route[:, :, :], over(top2[:, :], E2), ALU.mult).then_inc(sem("route"), 1)
                dve.wait_ge(sem("rt_hi"), c.n + 1)
                nc.vector.tensor_tensor(rt_lo[0:E2, :], W[0:E2, 1, :], rt_hi[0:E2, :].bitcast(F32), ALU.subtract).then_inc(sem("rt_lo"), 1)
                for t in range(HT):
                    dve.wait_ge(sem("in_scale"), c.n * HT + t + 1)
                    nc.vector.tensor_tensor(xn[:, t, :], W[:, t, :], xn[:, t, :], ALU.mult).then_inc(sem("turn_in"), 1)
                turn(c.ts[1], c.half)
                prepare(c)
                dve.wait_ge(sem("out_sc"), c.n + 1)
                dve.wait_ge(sem("w_free_a"), c.cb + 2)
                for t in range(HT):
                    ins = nc.vector.tensor_tensor(scaled_y[:, t, :], Y[:, t, :], out_sc[:, t, :], ALU.mult)
                chain.link(ins)
                for t in range(HT):
                    xs = x[:, c.half * HT + t, :]
                    nc.vector.scalar_tensor_tensor(xs, scaled_y[:, t, :], 0.5, xs, ALU.mult, ALU.add).then_inc(sem("x_ready"), 1)
                    xc[0] += 1

            def att2_call(c):
                dve.wait_ge(sem("turn_in"), (c.ts[0] + 1) * HT)
                nc.vector.memset(corr[:, :, D:D + 2], NONE)
                for f in range(2):
                    dve.wait_ge(sem("sq"), 2 * c.n + f + 1)
                    ins = nc.vector.tensor_tensor(power_sum[:, f, :], sq[:, f, :], sq[:, f + 2, :], ALU.add)
                    if f == 0:
                        chain.link(ins)
                        ins = nc.vector.tensor_copy(power_sum[0:1, 0, :], sq[0:1, 0, :])
                    ins.then_inc(sem("power"), 1)
                for f in range(2):
                    dve.wait_ge(sem("power_hi"), 2 * c.n + f + 1)
                    if f == 0:
                        nc.vector.tensor_tensor(nyq_lo[0:1, :], sq[0:1, 2, :], nyq_hi[0:1, :].bitcast(F32), ALU.subtract)
                    nc.vector.tensor_tensor(power_lo[:, f, :], power_sum[:, f, :], power_hi[:, f, :].bitcast(F32), ALU.subtract)\
                        .then_inc(sem("power_lo"), 1)
                for t in range(HT):
                    dve.wait_ge(sem("corr"), c.n * HT + t + 1)
                    chain.link(nc.vector.max(top8[:, t, :], corr[:, t, 0:D]))
                    nc.vector.tensor_scalar(nmax2[:, t:t + 1], top8[:, t, 0:1], -1.0, None, ALU.mult).then_inc(sem("nmax2"), 1)
                    chain.link(nc.vector.memset(top8[:, t, TOPK:8], NONE))
                    chain.sig(nc.vector.match_replace(marked[:, t, 0:D + 2], top8[:, t, :], corr[:, t, 0:D + 2], BIG))
                chain.wait()
                for t in range(HT):
                    dve.wait_ge(sem("ex2"), c.n * HT + t + 1)
                    ins = nc.vector.scalar_tensor_tensor(ex2[:, t, :], marked[:, t, 0:D], BIG, ex2[:, t, :], ALU.is_equal, ALU.mult,
                                                         accum_out=sum2[:, t:t + 1])
                    chain.sig(ins)
                chain.wait()
                chain.link(nc.vector.reciprocal(sum2[:, :], sum2[:, :]))
                for t in range(HT):
                    nc.vector.tensor_scalar(xn[:, t, :], ex2[:, t, :], sum2[:, t:t + 1], None, ALU.mult).then_inc(sem("turn_in"), 1)
                turn(c.ts[1], c.half)
                dve.wait_ge(sem("spectrum"), 2 * c.n + 2)
                def mix_lo_of(f):
                    dve.wait_ge(sem("mix_hi"), 4 * c.n + f + 1)
                    nc.vector.tensor_tensor(mix_lo[:, f, :], mix[:, f, :], mix_hi[:, f, :].bitcast(F32), ALU.subtract)\
                        .then_inc(sem("mix_lo"), 1)

                for f in range(4):
                    if f < 2:
                        chain.link(nc.vector.tensor_tensor(sq[:, f:4:2, :], W[:, f:4:2, :], spec[:, f:4:2, :], ALU.mult))
                        ins = nc.vector.tensor_tensor(mix[:, f, :], sq[:, f, :], sq[:, f + 2, :], ALU.add)
                    else:
                        nc.vector.tensor_tensor(cross[:, f - 2, :], W[:, f - 2, :], spec[:, f, :], ALU.mult)
                        chain.link(nc.vector.tensor_tensor(cross[:, f, :], W[:, f, :], spec[:, f - 2, :], ALU.mult))
                        ins = nc.vector.tensor_tensor(mix[:, f, :], cross[:, f, :], cross[:, f - 2, :], ALU.subtract)
                    if f in (0, 2):
                        chain.link(ins)
                        ins = nc.vector.tensor_copy(mix[0:1, f, :], sq[0:1, f, :])
                    ins.then_inc(sem("mix"), 1)
                    if f:
                        mix_lo_of(f - 1)
                mix_lo_of(3)
                prepare(c)
                residual(c.half, 1.0, "w_free_b", c.cb + 5)

            def ffn3_call(c):
                add_bias(c, bias3)
                if c.first:
                    g = over(gate_rep[:, :], R3)
                    r = same_rank[:, :].rearrange("p (one r) -> p one r", one=1).broadcast_to((P, 4 * B3, R3))
                    nc.vector.tensor_tensor(gmat[:, :, :], g, r, ALU.mult).then_inc(sem("gmat"), 1)
                    dve.wait_ge(sem("gmat_hi"), c.n // 2 + 1)
                    nc.vector.tensor_tensor(gmat_lo[:, :], gmat[:, :, :].rearrange("p b r -> p (b r)"), gmat_hi[:, :].bitcast(F32),
                                            ALU.subtract).then_inc(sem("gmat_lo"), 1)
                    dve.wait_ge(sem("eff_hi"), c.n + 1)
                    nc.vector.tensor_tensor(aeff_lo[:, :, :], W[:, :, 0:B3 * R3], aeff_hi[:, :, :].bitcast(F32), ALU.subtract)\
                        .then_inc(sem("eff_lo"), 1)
                    dve.wait_ge(sem("eff_hi"), c.n + 2)
                    nc.vector.tensor_tensor(beff_lo[:, :, :], Y[:, 0:2, :], beff_hi[:, :, :].bitcast(F32), ALU.subtract)\
                        .then_inc(sem("eff_lo"), 1)
                dve.wait_ge(sem("down3"), c.n + 1)
                nc.vector.tensor_tensor(h3[:, :], W[:, 0, :], own_block[:, :], ALU.mult).then_inc(sem("h3"), 1)
                dve.wait_ge(sem("h3_hi"), c.n + 1)
                nc.vector.tensor_tensor(h3_lo[:, :], h3[:, :], h3_hi[:, :].bitcast(F32), ALU.subtract)
                nc.vector.tensor_tensor(hs_lo[:, :], W[0:R3, 1, :], hs_hi[:, :].bitcast(F32), ALU.subtract).then_inc(sem("h3_lo"), 1)
                prepare(c)
                residual(c.half, 0.5, "w_free_b", c.mb + 2)

            def attention(c):
                m = att[c.kind]
                if c.kind == ATT1:
                    dve.wait_ge(sem("aux"), c.aux)
                    b = m.bias_o[:, :].rearrange("p (one d) -> p one d", one=1).broadcast_to((P, TT, D))
                    dve.wait_ge(sem("turn_in"), (c.ts[1] + 1) * HT)
                    chain.link(nc.vector.tensor_tensor(x[:, :, :], x[:, :, :], b, ALU.add))
                else:
                    dve.wait_ge(sem("aux"), c.aux)

                def phase(g, qt):
                    ph = Phase(c, g, qt)

                    def bank(s):
                        return W[:, 2 * s:2 * s + 2, :].rearrange("p b c -> p (b c)")

                    def project1(t):
                        s, tt = t % 2, qt * HT + t
                        n = 3 * m.heads * HD1
                        dve.wait_ge(ph.sem("proj"), ph.tiles + (t + 1))
                        qkv = m.qkv[:, s, :, :, :].rearrange("p i h d -> p (i h d)")
                        b = m.bias_qkv[:, bass.ds(g, 1), :].rearrange("p one c -> p (one c)")
                        nc.vector.tensor_tensor(qkv, W[:, 2 * s, 0:n], b, ALU.add).then_inc(ph.sem("qkv"), 1)
                        dve.wait_ge(ph.sem("parts_hi"), ph.tiles + (t + 1))
                        for i, hi, dst in ((0, m.q_parts[s][:, :, :, 0, :], m.q_parts[s][:, :, :, 1, :]),
                                           (1, m.k_parts[s][:, :, 0, :, :], m.k_parts[s][:, :, 1, :, :])):
                            src = m.qkv[:, s, i, :, :].rearrange("p h (one d) -> p h one d", one=1)
                            nc.vector.tensor_tensor(dst, src.broadcast_to((P, m.heads, 2, HD1)), hi.bitcast(F32), ALU.subtract)
                        nc.vector.tensor_tensor(m.v_lo[:, tt, :], m.qkv[:, s, 2, :, :].rearrange("p h d -> p (h d)"),
                                                m.v_hi[:, tt, :].bitcast(F32), ALU.subtract).then_inc(ph.sem("v_lo"), 1)

                    def turned1(t):
                        tt = qt * HT + t
                        dve.wait_ge(ph.sem("qk_turned"), ph.tiles + (t + 1))
                        nc.vector.tensor_copy(m.k[:, :, tt * P:(tt + 1) * P], Y[:, 1, :].rearrange("p (h q) -> p h q", q=P))\
                            .then_inc(ph.sem("k_out"), 1)

                    def project3(t):
                        s, tt = t % 2, qt * HT + t
                        H = m.heads + 1
                        dve.wait_ge(ph.sem("proj"), ph.tiles + (t + 1))
                        if t:
                            dve.wait_ge(ph.sem("rot"), ph.tiles + t)
                        cos = m.cos[:, tt, :].rearrange("p (one d) -> p one d", one=1)
                        sin = m.sin[:, tt, :].rearrange("p (one d) -> p one d", one=1).broadcast_to((P, H, HD3 // 2))
                        qk = bank(s)[:, 0:H * HD3]
                        pair = qk.rearrange("p (h two d) -> p h two d", h=H, two=2)
                        out2 = m.by_sin[:, :, :].rearrange("p (h two) d -> p h two d", two=2)
                        nc.vector.tensor_tensor(m.rot[s][:, :, :].rearrange("p h (two d) -> p (h two) d", two=2), qk.rearrange("p (h d) -> p h d", d=HD3 // 2),
                                                cos.broadcast_to((P, 2 * H, HD3 // 2)), ALU.mult)
                        nc.vector.scalar_tensor_tensor(out2[:, :, 0, :], pair[:, :, 1, :], -1.0, sin, ALU.mult, ALU.mult)
                        nc.vector.tensor_tensor(out2[:, :, 1, :], pair[:, :, 0, :], sin, ALU.mult).then_inc(ph.sem("by_sin"), 1)
                        dve.wait_ge(ph.sem("v_hi"), ph.tiles + (t + 1))
                        nc.vector.tensor_tensor(m.v_lo[:, tt, :], W[:, 2 * s + 1, P:2 * P], m.v_hi[:, tt, :].bitcast(F32), ALU.subtract)\
                            .then_inc(ph.sem("v_lo"), 1)

                    def turned3(t):
                        tt = qt * HT + t
                        dve.wait_ge(ph.sem("qk_hi"), ph.tiles + (t + 1))
                        q, kk = slice(t * P, (t + 1) * P), slice(tt * P, (tt + 1) * P)
                        nc.vector.tensor_tensor(m.q_lo[:, :, q], Y[:, 0, :].rearrange("p (h q) -> p h q", q=P),
                                                m.q_hi[:, :, q].bitcast(F32), ALU.subtract)
                        nc.vector.scalar_tensor_tensor(m.k_lo[:, kk], Y[:, 1, 0:P], HD3 ** -0.5, m.k_hi[:, kk].bitcast(F32),
                                                       ALU.mult, ALU.subtract).then_inc(ph.sem("k_out"), 1)

                    def maximum(u, q):
                        row = u * HT + q
                        dve.wait_ge(ph.sem("scores"), ph.rows + (row + 1))
                        nc.vector.tensor_reduce(m.nmax[:, row % 8:row % 8 + 1], ph.scored(row, q), AX, ALU.max,
                                                negate=True).then_inc(ph.sem("nmax"), 1)

                    def inverse(row):
                        dve.wait_ge(ph.sem("exp"), ph.rows + (row + 1))
                        inv = m.rinv[:, ph.sum_at(row)]
                        nc.vector.reciprocal(inv, m.rsum[:, ph.sum_at(row)]).then_inc(ph.sem("rinv"), 1)
                        if ph.on_dve(row):
                            dve.wait_ge(ph.sem("rinv"), ph.rows + (row + 1))
                            v = ph.row(row // HT, row % HT)
                            nc.vector.tensor_scalar(v, v, inv, None, ALU.mult).then_inc(ph.sem("norm_dve"), 1)

                    def lower(u, j):
                        b = u * ph.nkb + j
                        dve.wait_ge(ph.sem("pt_hi"), ph.blocks + (b + 1))
                        q = slice(ph.cols(j), HALF)
                        s = b % PT_SLOTS
                        nc.vector.tensor_tensor(m.pt_lo[s][:, q], Y[:, s, q], m.pt_hi[s][:, q].bitcast(F32), ALU.subtract)\
                            .then_inc(ph.sem("pt_lo"), 1)

                    def out_lo(u):
                        i, n = (u, ph.units + (u + 1)) if c.kind == ATT3 else (0, ph.no + 1)
                        dve.wait_ge(ph.sem("o_hi"), n)
                        src = m.o_raw if c.kind == ATT3 else m.out[:, :]
                        nc.vector.tensor_tensor(m.o_lo[:, i, :], src, m.o_hi[:, i, :].bitcast(F32), ALU.subtract)\
                            .then_inc(ph.sem("o_lo"), 1)

                    proj, turned = (project1, turned1) if c.kind == ATT1 else (project3, turned3)
                    proj(0)
                    for t in range(HT - 1):
                        proj(t + 1)
                        turned(t)
                    maximum(0, 0)
                    maximum(0, 1)
                    turned(HT - 1)
                    for row in range(1, AHEAD[qt]):
                        if row > 1:
                            maximum(row // HT, row % HT)
                        if row and c.kind == ATT3:
                            inverse(row - 1)
                    for u, q, keys, ahead, late in ph.steps():
                        for n, key in enumerate(keys):
                            lower(*key)
                            if n == 0 and ahead:
                                maximum(*ahead)
                        if late and c.kind == ATT3:
                            inverse(late[0] * HT + late[1])
                        if c.kind == ATT1 and (u, q) == (m.heads - 1, 0):
                            dve.wait_ge(ph.sem("exp"), ph.rows + m.heads * HT)
                            nc.vector.reciprocal(m.rinv[:, :], m.rsum[:, :]).then_inc(ph.sem("inverse"), 1)
                            dve.wait_ge(ph.sem("inverse"), ph.no + 1)
                            nc.vector.tensor_copy(m.out[:, :].rearrange("p (n d) -> p n d", d=HD1), over(m.rinv[:, :], HD1))\
                                .then_inc(ph.sem("rinv"), 1)
                        if c.kind == ATT1 and (u, q) == (m.heads - 1, HT - 1):
                            dve.wait_ge(ph.sem("spread"), ph.no + 1)
                            nc.vector.tensor_copy(m.out[:, :], W[:, 3, :]).then_inc(ph.sem("copied"), 1)
                            dve.wait_ge(ph.sem("copied"), ph.no + 1)
                        if c.kind == ATT3 and u and q == 2 - qt:
                            out_lo(u - 1)
                    if c.kind == ATT1:
                        dve.wait_ge(ph.sem("av"), ph.units + m.heads)
                        nc.vector.tensor_tensor(m.out[:, :], Y[:, AV, :], m.out[:, :], ALU.mult).then_inc(ph.sem("out"), 1)
                        dve.wait_ge(ph.sem("out"), ph.no + 1)
                    out_lo(m.heads - 1)
                    for t in range(HT):
                        dve.wait_ge(ph.sem("wo"), ph.no * HT + (t + 1))
                        xs = x[:, qt * HT + t, :]
                        nc.vector.tensor_tensor(xs, Y[:, 2 + t % 2, :], xs, ALU.add).then_inc(sem("x_ready"), 1)

                with dve.Fori(0, m.groups) as g:
                    dve.wait_ge(sem("x_ready"), g * TT + c.xb)
                    phase(g, 0)
                    phase(g, 1)
                xc[0] += TT * m.groups

            for before, c in zip([None] + calls, calls):
                if before is None:
                    dve.wait_ge(sem("x_loaded_0"), 16)
                else:
                    dve.wait_ge(sem("x_ready"), xc[0])
                if not (before and before.prepares):
                    measure(c.half or 0)
                    if chunks[c.cb][1]:
                        dve.wait_ge(sem("const"), 16 * 5)
                        scale(c.cb)
                    turn_in(c.lns[0], c.half or 0)
                    turn(c.ts[0], c.half or 0)
                if before is None:
                    dve.wait_ge(sem("x_loaded_1"), 16)
                if c.kind in GROUPS:
                    measure(1)
                    turn_in(c.lns[1], 1)
                    turn(c.ts[1], 1)
                    attention(c)
                    continue
                dict(FFN0=gated_call, GATE0=gated_call, FFN1=ffn1_call, FFN2=ffn2_call, ATT2=att2_call, FFN3=ffn3_call)[c.kind](c)

        @block.tensor
        def _(pe):
            def turn(n):
                for t in range(HT):
                    pe.wait_ge(sem("turn_in"), n * HT + t + 1)
                    for k in range(KT):
                        ins = nc.tensor.transpose(W[:, t, k * P:(k + 1) * P], xn[:, t, k * P:(k + 1) * P], ident[:, :])
                    ins.then_inc(sem("turned"), 1)

            def turned_out(n):
                pe.wait_ge(sem("xt_lo"), (n + 1) * HT)

            def xt(half, k, lo=0, hi=HALF):
                return (xt_hi[:, k, half * HALF + lo:half * HALF + hi], xt_lo[:, k, half * HALF + lo:half * HALF + hi])

            def y_free(c):
                if c.xb:
                    pe.wait_ge(sem("x_ready"), c.xb)

            def gated_call(c):
                steps, cb, after = gated(c)

                def up(i, j=None):
                    off = 0 if j is None else j
                    s, p = (cb + i) % 2, i % 2
                    pe.wait_ge(sem("w_lo_a"), off * 2 + (cb + i + 1))
                    if c.sb + i >= 2:
                        pe.wait_ge(sem("h"), off * 2 + (c.sb + i - 1))
                    if c.kind == GATE0 and i == 0:
                        pe.wait_ge(sem("gate_read"), c.n + 1)
                    for g in range(2):
                        for k in range(KT):
                            w = slice((g * KT + k) * P, (g * KT + k + 1) * P)
                            ins = mm3(W[:, 2 * p + g, :], w_hi[s][:, w], w_lo[s][:, w], *xt(c.half, k), k == 0, k == KT - 1)
                    ins.then_inc(sem("w_free_a"), 1)

                def down(i, j=None):
                    off = 0 if j is None else j
                    s, p = (cb + i) % 2, i % 2
                    pe.wait_ge(sem("w_lo_b"), off * 2 + (cb + i + 1))
                    pe.wait_ge(sem("h_lo"), off * 2 + (c.sb + i + 1))
                    last = i == steps - 1 and not after and j is None
                    for t in range(HT):
                        q = slice(t * P, (t + 1) * P)
                        ins = mm3(Y[:, t, :], h_hi[p][:, q], h_lo[p][:, q], w_hi[s][:, PA:CHUNK], w_lo[s][:, PA:CHUNK],
                                  i == 0 and c.kind == FFN0, last)
                    ins.then_inc(sem("w_free_b"), 1)

                def terms(chunk, lo, m, start, stop, signal):
                    s = chunk % 2
                    pe.wait_ge(sem("term_lo"), (ORDERS + 1) * c.n + m + 1)
                    for t in range(HT):
                        q = slice(t * P, (t + 1) * P)
                        ins = mm3(Y[:, t, :], term_hi[m][:, q], term_lo[m][:, q], w_hi[s][:, lo:lo + D], w_lo[s][:, lo:lo + D],
                                  start, stop)
                    if signal:
                        ins.then_inc(sem(signal), 1)

                if c.kind == GATE0:
                    s = (cb - 1) % 2
                    pe.wait_ge(sem("w_lo_a"), cb)
                    for g in range(2):
                        for k in range(KT):
                            w = slice((g * KT + k) * P, (g * KT + k + 1) * P)
                            ins = mm3(W[:, g, :], w_hi[s][:, w], w_lo[s][:, w], *xt(c.half, k), k == 0, k == KT - 1)
                    ins.then_inc(sem("w_free_a"), 1)
                up(0)
                y_free(c)
                if c.kind == GATE0:
                    pe.wait_ge(sem("w_lo_b"), cb)
                    terms(cb - 1, PA, 0, True, False, "w_free_b")
                up(1)
                down(0)
                with pe.Fori(0, (steps - 2) // 2) as j:
                    for a in range(2):
                        up(2 + a, j)
                        down(1 + a, j)
                if c.next:
                    pe.wait_ge(sem("h_lo"), c.sb + steps)
                    turn(c.next.ts[0])
                down(steps - 1)
                if c.kind == GATE0:
                    for q in range(2):
                        chunk = cb + steps + q
                        pe.wait_ge(sem("w_lo_a"), chunk + 1)
                        terms(chunk, 0, 3 * q + 1, False, False, None)
                        terms(chunk, D, 3 * q + 2, False, False, "w_free_a")
                        pe.wait_ge(sem("w_lo_b"), chunk + 1)
                        terms(chunk, PA, 3 * q + 3, False, q == 1, "w_free_b")

            def parts(chunk, lo, hi, rows=P):
                s = chunk % 2
                return w_hi[s][0:rows, lo:hi], w_lo[s][0:rows, lo:hi]

            def ready(chunk, part):
                pe.wait_ge(sem(f"w_lo_{part}"), chunk + 1)

            def blk(t):
                return t * P, (t + 1) * P

            def ffn1_call(c):
                cb = c.cb
                for chunk, part, ks in ((cb, "a", (0, 1)), (cb, "b", (2,)), (cb + 1, "a", (3,))):
                    ready(chunk, part)
                    for t in range(HT):
                        for k in ks:
                            lo = PA if part == "b" else (k % 3) * D
                            ins = mm3(W[:, t, :], *xt(c.half, k, *blk(t)), *parts(chunk, lo, lo + D), k == 0, k == 3)
                    if chunk == cb:
                        ins.then_inc(sem(f"w_free_{part}"), 1)
                y_free(c)
                for t in range(HT):
                    for k in range(KT):
                        ins = mm3(Y[:, 0, t * P:(t + 1) * P], *xt(c.half, k, *blk(t)), *parts(cb + 1, D + k * P, D + (k + 1) * P),
                                  k == 0, k == KT - 1)
                ins.then_inc(sem("w_free_a"), 1)
                for chunk, part, ks in ((cb + 1, "b", (0,)), (cb + 2, "a", (1, 2)), (cb + 2, "b", (3,))):
                    ready(chunk, part)
                    for t in (1, 2, 3, 0):
                        if chunk == cb + 1 and t == 0:
                            pe.wait_ge(sem("h1_copied"), c.n + 1)
                        for k in ks:
                            lo = PA if part == "b" else (k - 1) * D
                            ins = mm3(Y[:, t, :], *xt(c.half, k, *blk(t)), *parts(chunk, lo, lo + D), k == 0, False)
                    ins.then_inc(sem(f"w_free_{part}"), 1)
                pe.wait_ge(sem("wh"), c.n + 1)
                for t in range(HT):
                    ins = nc.tensor.transpose(W[:, 0, t * P:(t + 1) * P],
                                              wh[:, t * EXP1:(t + 1) * EXP1, :].rearrange("p e r -> p (e r)"), ident[:, :])
                ins.then_inc(sem("wh_turned"), 1)
                ready(cb + 3, "a")
                pe.wait_ge(sem("wht_lo"), c.n + 1)
                for t in range(HT):
                    lo, hi = blk(t)
                    ins = mm3(Y[:, t, :], wht_hi[:, lo:hi], wht_lo[:, lo:hi], *parts(cb + 3, 0, D), False, True)
                ins.then_inc(sem("w_free_a"), 1)
                pe.wait_ge(sem("w_free_b"), cb + 3)
                pe.sem_inc(sem("w_free_b"), 1)

            def ffn2_call(c):
                pe.wait_ge(sem("chan_lo"), c.n // 2 + 1)
                for k in range(KT):
                    w = slice(k * E2, (k + 1) * E2)
                    ins = mm3(W[0:E2, 1, :], small2_hi[:, w], small2_lo[:, w], *xt(c.half, k), k == 0, k == KT - 1)
                ins.then_inc(sem("logits_t"), 1)
                pe.wait_ge(sem("logits_copied"), c.n + 1)
                for t in range(HT):
                    ins = nc.tensor.transpose(W[:, 0, t * E2:(t + 1) * E2], logit_t[0:E2, t * P:(t + 1) * P], ident[0:E2, 0:E2])
                ins.then_inc(sem("logits"), 1)
                pe.wait_ge(sem("route"), c.n + 1)
                for t in range(HT):
                    ins = nc.tensor.transpose(W[0:E2, 1, t * P:(t + 1) * P], route[:, t, :], ident[:, :])
                ins.then_inc(sem("route_turned"), 1)
                pe.wait_ge(sem("rt_lo"), c.n + 1)
                for t in range(HT):
                    lo, hi = blk(t)
                    mm3(W[:, t, :], rt_hi[0:E2, lo:hi], rt_lo[0:E2, lo:hi], chan_hi[0:E2, 0:D], chan_lo[0:E2, 0:D], True, True)\
                        .then_inc(sem("in_scale"), 1)
                turn(c.ts[1])
                turned_out(c.ts[1])
                for t in range(HT):
                    lo, hi = blk(t)
                    ins = mm3(W[:, t, :], rt_hi[0:E2, lo:hi], rt_lo[0:E2, lo:hi], chan_hi[0:E2, D:], chan_lo[0:E2, D:], True, True)
                ins.then_inc(sem("out_scale"), 1)
                y_free(c)
                for chunk, part, ks in ((c.cb, "a", (0, 1)), (c.cb, "b", (2,)), (c.cb + 1, "a", (3,))):
                    ready(chunk, part)
                    for t in range(HT):
                        for k in ks:
                            lo = PA if part == "b" else (k % 3) * D
                            x_hi, x_lo = xt(c.half, k, *blk(t))
                            w = w_hi[chunk % 2][:, lo:lo + D]
                            nc.tensor.matmul(Y[:, t, :], x_hi, w, start=k == 0, stop=False)
                            ins = nc.tensor.matmul(Y[:, t, :], x_lo, w, start=False, stop=k == 3)
                    ins.then_inc(sem(f"w_free_{part}"), 1)
                pe.wait_ge(sem("w_free_b"), c.cb + 1)
                pe.sem_inc(sem("w_free_b"), 1)
                pe.wait_ge(sem("out_sc"), c.n + 1)

            def att2_call(c):
                cb = c.cb

                def transform(to, pieces):
                    for k, (chunk, part, lo, signal) in enumerate(pieces):
                        ready(chunk, part)
                        for f in range(4):
                            ins = mm3(to[:, f, :], *parts(chunk, lo + f * P, lo + (f + 1) * P), *xt(c.half, k), k == 0, k == 3)
                        if signal:
                            ins.then_inc(sem(signal), 1)
                    return ins

                y_free(c)
                transform(Y, [(cb, "a", 0, None), (cb, "a", D, "w_free_a"), (cb, "b", PA, "w_free_b"), (cb + 1, "a", 0, "spectrum")])
                for part, lo, f in (("a", D, 0), ("b", PA, 1)):
                    ready(cb + 1, part)
                    pe.wait_ge(sem("power_lo"), 2 * c.n + f + 1)
                    for t in range(HT):
                        q = slice(*blk(t))
                        ins = mm3(W[:, t, :], power_hi[:, f, q], power_lo[:, f, q], *parts(cb + 1, lo, lo + D), f == 0, False)
                    ins.then_inc(sem(f"w_free_{part}"), 1)
                ready(cb + 2, "a")
                for t in range(HT):
                    q = slice(*blk(t))
                    ins = mm3(W[:, t, :], nyq_hi[0:1, q], nyq_lo[0:1, q], *parts(cb + 2, 0, D, 1), False, True)
                ins.then_inc(sem("correlated"), 1)
                turn(c.ts[1])
                turned_out(c.ts[1])
                transform(W, [(cb + 2, "a", D, "w_free_a"), (cb + 2, "b", PA, "w_free_b"), (cb + 3, "a", 0, None),
                              (cb + 3, "a", D, "w_free_a")])
                pe.wait_ge(sem("w_free_a"), cb + 4)
                pe.sem_inc(sem("spectrum"), 1)
                pe.wait_ge(sem("spec"), c.n + 1)
                for f, (chunk, part, lo, signal) in enumerate([(cb + 3, "b", PA, 1), (cb + 4, "a", 0, 0), (cb + 4, "a", D, 1), (cb + 4, "b", PA, 1)]):
                    ready(chunk, part)
                    pe.wait_ge(sem("mix_lo"), 4 * c.n + f + 1)
                    for t in range(HT):
                        q = slice(*blk(t))
                        ins = mm3(Y[:, t, :], mix_hi[:, f, q], mix_lo[:, f, q], *parts(chunk, lo, lo + D), f == 0, f == 3)
                    if signal:
                        ins.then_inc(sem(f"w_free_{part}"), 1)

            def ffn3_call(c):
                if c.first:
                    cb = c.cb
                    where = lambda k: ((cb, "a", 0), (cb, "a", D), (cb, "b", PA), (cb + 1, "a", 0), (cb + 1, "a", D), (cb + 1, "b", PA),
                                       (cb + 2, "a", 0), (cb + 2, "a", D))[k]
                    pe.wait_ge(sem("gmat_lo"), c.n // 2 + 1)
                    G = B3 * R3
                    for k in range(4):
                        chunk, part, lo = where(k)
                        ready(chunk, part)
                        for j in range(KT):
                            ins = mm3(W[:, j, 0:G], *parts(chunk, lo + j * P, lo + (j + 1) * P), gmat_hi[:, k * G:(k + 1) * G],
                                      gmat_lo[:, k * G:(k + 1) * G], k == 0, k == 3)
                        if k in (1, 2):
                            ins.then_inc(sem(f"w_free_{part}"), 1)
                    ins.then_inc(sem("eff"), 1)
                    y_free(c)
                    for k in range(4):
                        chunk, part, lo = where(4 + k)
                        ready(chunk, part)
                        for g in range(2):
                            q = slice(k * G + g * P, k * G + (g + 1) * P)
                            ins = mm3(Y[:, g, :], gmat_hi[:, q], gmat_lo[:, q], *parts(chunk, lo, lo + D), k == 0, k == 3)
                        if k < 2:
                            ins.then_inc(sem(f"w_free_{part}"), 1)
                    ins.then_inc(sem("eff"), 1)
                    pe.wait_ge(sem("eff"), c.n + 2)
                    pe.sem_inc(sem("w_free_a"), 1)
                    pe.sem_inc(sem("w_free_b"), 1)
                    pe.wait_ge(sem("eff_lo"), c.n + 2)
                mb = c.mb
                ready(mb + 1, "a")
                hb = slice(c.half * P, (c.half + 1) * P)
                for k in range(KT):
                    mm3(W[:, 0, :], aeff_hi[:, k, hb], aeff_lo[:, k, hb], *xt(c.half, k), k == 0, k == 3)
                for k in range(KT):
                    lo = D + k * R3
                    ins = mm3(W[0:R3, 1, :], *parts(mb + 1, lo, lo + R3), *xt(c.half, k), k == 0, k == 3)
                ins.then_inc(sem("down3"), 1)
                y_free(c)
                for chunk, part, ks in ((mb, "a", (0, 1)), (mb, "b", (2,)), (mb + 1, "a", (3,))):
                    ready(chunk, part)
                    for t in range(HT):
                        for k in ks:
                            lo = PA if part == "b" else (k % 3) * D
                            ins = mm3(Y[:, t, :], *xt(c.half, k, *blk(t)), *parts(chunk, lo, lo + D), k == 0, False)
                    ins.then_inc(sem(f"w_free_{part}"), 1)
                ready(mb + 1, "b")
                pe.wait_ge(sem("h3_lo"), c.n + 1)
                for t in range(HT):
                    q = slice(*blk(t))
                    mm3(Y[:, t, :], h3_hi[:, q], h3_lo[:, q], beff_hi[:, c.half, :], beff_lo[:, c.half, :], False, False)
                    ins = mm3(Y[:, t, :], hs_hi[:, q], hs_lo[:, q], *parts(mb + 1, PA, CHUNK, R3), False, True)
                ins.then_inc(sem("w_free_b"), 1)

            def attention(c):
                m = att[c.kind]

                def ready_(ph, i):
                    for part in "ab":
                        pe.wait_ge(sem(f"w_lo_{part}"), ph.chunk + (i + 1))

                def part_(ph, i, lo, hi):
                    s = ph.w_slot(i)
                    return m.w_hi[s][:, lo:hi], m.w_lo[s][:, lo:hi]

                def project(ph, t):
                    s, tt = t % 2, ph.qt * HT + t
                    if t >= 2:
                        pe.wait_ge(ph.sem("v_lo"), ph.tiles + (t - 1))
                    half, q = tt // HT, blk(tt % HT)
                    for k in range(KT):
                        if c.kind == ATT1:
                            w = part_(ph, 0, k * 384, (k + 1) * 384)
                            ins = mm3(W[:, 2 * s, 0:384], *xt(half, k, *q), *w, k == 0, k == KT - 1)
                        else:
                            lo = (k % 2) * 768
                            w = part_(ph, k // 2, lo, lo + D)
                            mm3(W[:, 2 * s, :], *xt(half, k, *q), *w, k == 0, k == KT - 1)
                            w = part_(ph, k // 2, lo + D, lo + 768)
                            ins = mm3(W[:, 2 * s + 1, 0:256], *xt(half, k, *q), *w, k == 0, k == KT - 1)
                    ins.then_inc(ph.sem("proj"), 1)

                def begin(ph):
                    for i in range(2 if c.kind == ATT3 else 1):
                        ready_(ph, i)
                    project(ph, 0)

                def phase(g, qt, last=False):
                    ph = Phase(c, g, qt)

                    def free(count):
                        for _ in range(count):
                            for part in "ab":
                                pe.sem_inc(sem(f"w_free_{part}"), 1)

                    def turned(t):
                        if t:
                            pe.wait_ge(ph.sem("k_out"), ph.tiles + t)
                        if c.kind == ATT1:
                            if t:
                                pe.wait_ge(ph.sem("q_out"), ph.tiles + t)
                            pe.wait_ge(ph.sem("v_lo"), ph.tiles + (t + 1))
                            for b, src in ((0, m.q_parts[t % 2]), (1, m.k_parts[t % 2])):
                                v = src[:, :, :, :, :].rearrange("p h a b d -> p (h a b d)").bitcast(F32)
                                for i in range(4):
                                    ins = nc.tensor.transpose(Y[:, b, i * P:(i + 1) * P], v[:, i * P:(i + 1) * P], ident[:, :])
                        else:
                            pe.wait_ge(ph.sem("rot"), ph.tiles + (t + 1))
                            for h in range(m.heads + 1):
                                ins = nc.tensor.transpose(Y[:, h // 4, (h % 4) * P:(h % 4 + 1) * P], m.rot[t % 2][:, h, :], ident[:, :])
                        ins.then_inc(ph.sem("qk_turned"), 1)

                    def scores(u, q):
                        row, i = u * HT + q, qt * HT + q
                        if row >= ph.row_slots:
                            pe.wait_ge(ph.sem("exp"), ph.rows + (row - ph.row_slots + 1))
                        first = ph.row_bank(row)
                        for b in range(i // 4 + 1):
                            lo, hi = b * D, min((i + 1) * P, (b + 1) * D)
                            out_ = W[:, first + b, 0:hi - lo]
                            diag = hi == (i + 1) * P
                            if c.kind == ATT1:
                                r = slice(64 * (u % 2), 64 * (u % 2) + 64)
                                nc.tensor.matmul(out_, m.q[r, u // 2, q * P:(q + 1) * P], m.k[r, u // 2, lo:hi], start=True, stop=not diag)
                            else:
                                qq = slice(q * P, (q + 1) * P)
                                mm3(out_, m.q_hi[:, u, qq], m.q_lo[:, u, qq], m.k_hi[:, lo:hi], m.k_lo[:, lo:hi], True, not diag)
                        nc.tensor.matmul(W[:, first + b, i * P - lo:hi - lo], ident_r[:, :], mask_r[:, :], start=False, stop=True)\
                            .then_inc(ph.sem("scores"), 1)

                    def turn_p(u, j):
                        b = u * ph.nkb + j
                        if j == 0 and c.kind == ATT1:
                            pe.wait_ge(ph.sem("exp"), ph.rows + (u + 1) * HT)
                        elif j == 0:
                            by_dve, by_pool = ph.normalised(u)
                            pe.wait_ge(ph.sem("norm_dve"), by_dve)
                            if qt and u:
                                pe.wait_ge(ph.sem("norm_pool"), by_pool)
                        if b >= PT_SLOTS:
                            pe.wait_ge(ph.sem("pt_lo"), ph.blocks + (b - PT_SLOTS + 1))
                        for q in range(ph.cols(j) // P, HT):
                            ins = nc.tensor.transpose(Y[:, b % PT_SLOTS, q * P:(q + 1) * P], ph.row(u, q, j * P, (j + 1) * P), ident[:, :])
                        ins.then_inc(ph.sem("p_turned"), 1)

                    def values(u, j):
                        b, lo = u * ph.nkb + j, ph.cols(j)
                        pe.wait_ge(ph.sem("pt_lo"), ph.blocks + (b + 1))
                        if c.kind == ATT1:
                            if j == 0:
                                pe.wait_ge(ph.sem("pad"), ph.units + (u + 1))
                            v_hi, v_lo = m.v_pad[u % 2]
                            start, stop = u == 0 and j == 0, u == m.heads - 1 and j == ph.nkb - 1
                        else:
                            if j == 0 and u:
                                pe.wait_ge(ph.sem("o_out"), ph.units + u)
                            v_hi, v_lo = m.v_hi, m.v_lo
                            start, stop = j == 0, j == ph.nkb - 1
                        s = b % PT_SLOTS
                        ins = mm3(Y[:, AV, lo:HALF], v_hi[:, j, :], v_lo[:, j, :], m.pt_hi[s][:, lo:HALF], m.pt_lo[s][:, lo:HALF], start, stop)
                        if j == ph.nkb - 1:
                            ins.then_inc(ph.sem("av"), 1)

                    for t in range(HT - 1):
                        project(ph, t + 1)
                        turned(t)
                    for row in range(2):
                        pe.wait_ge(ph.sem("k_out"), ph.tiles + row + 1)
                        if c.kind == ATT1:
                            pe.wait_ge(ph.sem("q_out"), ph.tiles + row + 1)
                        pe.wait_ge(ph.sem("v_lo"), ph.tiles + HT - 1 + ph.row_bank(row) // 2)
                        scores(0, row)
                    turned(HT - 1)
                    pe.wait_ge(ph.sem("proj"), ph.tiles + HT)
                    if qt:
                        free(2 if c.kind == ATT3 else 1)
                    pe.wait_ge(ph.sem("v_lo"), ph.tiles + HT)
                    for row in range(2, AHEAD[qt]):
                        if row == HT - 1:
                            pe.wait_ge(ph.sem("k_out"), ph.tiles + HT)
                            if c.kind == ATT1:
                                pe.wait_ge(ph.sem("q_out"), ph.tiles + HT)
                        scores(row // HT, row % HT)
                    pe.wait_ge(sem("x_ready"), ph.x)
                    turned_ = []
                    for u, q, keys, ahead, late in ph.steps():
                        for n, key in enumerate(keys):
                            turn_p(*key)
                            turned_.append(key)
                            if len(turned_) == PT_SLOTS:
                                values(*turned_.pop(0))
                            if n == 0 and ahead:
                                scores(*ahead)
                        if c.kind == ATT1 and (u, q) == (m.heads - 1, 1):
                            pe.wait_ge(ph.sem("rinv"), ph.no + 1)
                            for t in range(HT):
                                ins = nc.tensor.transpose(W[:, 3, t * P:(t + 1) * P], m.out[:, t * P:(t + 1) * P], ident[:, :])
                            ins.then_inc(ph.sem("spread"), 1)
                    for key in turned_:
                        values(*key)
                    if qt == 0:
                        project(Phase(c, g, 1), 0)
                    elif not last:
                        begin(Phase(c, g, 0, later=1))
                    pe.wait_ge(ph.sem("o_lo"), ph.units + m.heads if c.kind == ATT3 else ph.no + 1)
                    first = 2 if c.kind == ATT3 else 1
                    if qt == 0:
                        for i in range(first, m.ch):
                            ready_(ph, i)
                    for t in range(HT):
                        if t >= 2:
                            pe.wait_ge(sem("x_ready"), ph.x + (t - 1))
                        n = m.heads if c.kind == ATT3 else 1
                        for h in range(n):
                            w = part_(ph, first + h // 3, (h % 3) * D, (h % 3 + 1) * D)
                            ins = mm3(Y[:, 2 + t % 2, :], m.o_hi[:, h, t * P:(t + 1) * P], m.o_lo[:, h, t * P:(t + 1) * P], *w, h == 0, h == n - 1)
                        ins.then_inc(ph.sem("wo"), 1)
                    if qt:
                        pe.wait_ge(ph.sem("wo"), ph.no * HT + HT)
                        free(m.ch - first)

                begin(Phase(c, 0, 0))
                with pe.Fori(0, m.groups - 1) as g:
                    phase(g, 0)
                    phase(g, 1)
                phase(m.groups - 1, 0)
                phase(m.groups - 1, 1, last=True)

            pe.wait_ge(sem("const_r"), 1)
            pe.wait_ge(sem("const"), 16 * 5 if kinds & {FFN0, GATE0} else 32)
            for before, c in zip([None] + calls, calls):
                if c.kind in GROUPS:
                    turn(c.ts[0])
                    turned_out(c.ts[0])
                    turn(c.ts[1])
                    turned_out(c.ts[1])
                    attention(c)
                    continue
                if not (before and before.kind in (FFN0, GATE0)):
                    turn(c.ts[0])
                turned_out(c.ts[0])
                dict(FFN0=gated_call, GATE0=gated_call, FFN1=ffn1_call, FFN2=ffn2_call, ATT2=att2_call, FFN3=ffn3_call)[c.kind](c)


def _tiles(w):
    n = w.shape[0] // P
    return w.reshape(n, P, KT, P).transpose(0, 3, 2, 1)


def _pad_rows(w, n):
    return np.concatenate([w, np.zeros((n - w.shape[0],) + w.shape[1:], w.dtype)], 0)


def rope_tables():
    inv = 1.0 / 500000.0 ** (np.arange(0, HD3, 2, dtype=np.float32) / HD3)
    wavelen = 2.0 * np.pi / inv
    smooth = (1024 / wavelen - 1.0) / (4.0 - 1.0)
    medium = (wavelen <= 1024) & (wavelen >= 256)
    freq = np.where(medium, (1.0 - smooth) / 8.0 * inv + smooth * inv, np.where(wavelen > 1024, inv / 8.0, inv)).astype(np.float32)
    angle = np.arange(T, dtype=np.float32)[:, None] * freq[None, :]
    return np.cos(angle.astype(np.float64)).astype(np.float32), np.sin(angle.astype(np.float64)).astype(np.float32)


def layout(i):
    f = lambda name: np.asarray(i[name])
    out = []
    w1, w3 = _tiles(f("L0_ffn_w1")), _tiles(f("L0_ffn_w3"))
    w2 = f("L0_ffn_w2").T.reshape(F0_STEPS, P, D)
    out.append(np.concatenate([w1.reshape(F0_STEPS, P, D), w3.reshape(F0_STEPS, P, D), w2], 2))
    up, gate = _tiles(f("L0_attn_up_w"))[0].reshape(P, D), _tiles(f("L0_attn_gate_w"))[0].reshape(P, D)
    out.append(np.concatenate([up, gate, f("L0_attn_local_approx_output").T], 1)[None])
    n = G0_STEPS * P
    fg, fu = (_tiles(_pad_rows(f(f"L0_attn_ffn_{q}_w"), n)).reshape(G0_STEPS, P, D) for q in ("gate", "up"))
    fd = _pad_rows(f("L0_attn_ffn_down_w").T, n).reshape(G0_STEPS, P, D)
    out.append(np.concatenate([fg, fu, fd], 2))
    fuse = f("L0_attn_fuse_weight").transpose(1, 2, 0).reshape(P, 2, CHUNK).transpose(1, 0, 2)
    out.append(fuse)
    zeros = np.zeros((P, D), np.float32)
    kt = lambda w: [w.T[k * P:(k + 1) * P] for k in range(KT)]

    def pack(units):
        units = [np.pad(u, ((0, P - u.shape[0]), (0, D - u.shape[1]))) for u in units]
        units += [zeros] * (-len(units) % 3)
        return np.stack([np.concatenate(units[n:n + 3], 1) for n in range(0, len(units), 3)])

    qk = kt(np.concatenate([f("L1_ffn_Wq"), f("L1_ffn_Wk")], 0))
    down = np.concatenate(kt(f("L1_ffn_A").reshape(EXP1 * RANK1, D)), 1)
    out.append(pack(qk + [down] + kt(f("L1_ffn_W")) + [f("L1_ffn_Bm").transpose(0, 2, 1).reshape(EXP1 * RANK1, D)]))
    for g in range(GROUPS[ATT1]):
        rows_ = slice(g * P, (g + 1) * P)
        out.append(np.concatenate(kt(np.concatenate([f(f"L1_attn_W{q}")[rows_] for q in "qkv"], 0)), 1)[None])
        out.append(pack([f("L1_attn_Wo").T[rows_]]))
    out.append(pack(kt(f("L2_ffn_weight"))))
    lag, freq = np.arange(D), np.arange(D // 2)
    angle = lambda k: 2 * np.pi * (np.outer(lag, k) % D) / D
    fwd = np.concatenate([np.cos(angle(freq)), np.sin(angle(freq))], 1)
    top = np.cos(angle(np.array([D // 2])))[:, 0]
    fwd[:, D // 2] = top
    twice = np.where(freq == 0, 1.0, 2.0)[:, None] / D
    inv_cos, inv_sin = twice * np.cos(angle(freq)).T, -twice * np.sin(angle(freq)).T
    inv_sin[0] = top / D
    rows = lambda m: [m[k * P:(k + 1) * P].astype(np.float32) for k in range(m.shape[0] // P)]
    out.append(pack(rows(fwd) + rows(inv_cos) + [(top / D)[None].astype(np.float32)] + rows(fwd) + rows(inv_cos) + rows(inv_sin)))
    lora_a = f("L3_ffn_lora_A").reshape(NL3 * R3, D)
    lora_b = f("L3_ffn_lora_B").transpose(0, 2, 1).reshape(NL3 * R3, D)
    tiles = lambda w: [w[k * P:(k + 1) * P] for k in range(w.shape[0] // P)]
    out.append(pack(tiles(lora_a) + tiles(lora_b)))
    shared = np.concatenate(kt(f("L3_ffn_lora_A_shared")), 1)
    out.append(pack(tiles(f("L3_ffn_kernel")) + [shared, f("L3_ffn_lora_B_shared").T]))
    for g in range(KV3):
        n = H3 // KV3 * HD3
        qkv = kt(np.concatenate([f("L3_attn_Wq")[g * n:(g + 1) * n]] + [f(f"L3_attn_W{q}")[g * HD3:(g + 1) * HD3] for q in "kv"], 0))
        out += [np.concatenate(qkv[0:2], 1)[None], np.concatenate(qkv[2:4], 1)[None]]
        out.append(pack(tiles(f("L3_attn_Wo").T[g * n:(g + 1) * n])))
    arrays = {"ident": np.eye(P, dtype=np.float32)}
    s1, s3, s2 = f("L0_ffn_w1_scale"), f("L0_ffn_w3_scale"), f("L0_ffn_w2_scale").T
    arrays["scales"] = np.concatenate([s1, s3, s2], 1)
    arrays["local_point"] = f("L0_attn_local_point").reshape(P, 1)
    arrays["discount"] = f("L0_attn_discount_factor").reshape(1, ORDERS)
    arrays["ffn1_b"], arrays["ffn2_b"], arrays["ffn3_b"] = (f(f"L{n}_ffn_{q}").reshape(1, D) for n, q in ((1, "b"), (2, "bias"), (3, "bias")))
    arrays["router"] = np.concatenate(kt(f("L2_ffn_gate_w")), 1)
    arrays["channel"] = np.concatenate([f("L2_ffn_in_channel_scale"), f("L2_ffn_out_channel_scale")], 1)
    g = f("L3_ffn_gate").T.reshape(4, 4, 1, B3)
    arrays["gate_rep"] = np.broadcast_to(g, (4, 4, R3, B3)).transpose(1, 2, 0, 3).reshape(P, 4 * B3)
    arrays["same_rank"] = np.tile(np.eye(R3, dtype=np.float32), (4, 1))
    arrays["own_block"] = np.kron(np.eye(4, dtype=np.float32), np.ones((R3, P), np.float32))
    arrays["mask"] = np.triu(np.full((P, P), NEG, np.float32), 1)
    qkv_b = np.stack([f(f"L1_attn_b{q}").reshape(GROUPS[ATT1], P) for q in "qkv"], 1)
    arrays["att1_qkv_b"], arrays["att1_o_b"] = qkv_b.reshape(1, 3 * D), f("L1_attn_bo").reshape(1, D)
    cos, sin = rope_tables()
    arrays["rope_cos"], arrays["rope_sin"] = (q.reshape(TT, P, HD3 // 2).transpose(1, 0, 2) for q in (cos, sin))
    arrays["weights"] = np.concatenate(out, 0)
    assert arrays["weights"].shape[0] == N_DRAM_CHUNKS
    return {k: np.ascontiguousarray(v) for k, v in arrays.items()}


def kernel(**inputs):
    import concourse.bacc as bacc
    from concourse.bass_utils import run_bass_kernel_spmd

    nc = bacc.Bacc("TRN2", target_bir_lowering=False, num_devices=1)
    hidden = np.ascontiguousarray(np.asarray(inputs["L0_attn_hidden_states"]).reshape(T, D))
    arrays = {f"in_{name}": a for name, a in layout(inputs).items()}
    arrays["in_x"] = hidden
    aps = {name: nc.dram_tensor(name, a.shape, mybir.dt.from_np(a.dtype), kind="ExternalInput").ap() for name, a in arrays.items()}
    out = nc.dram_tensor("out", (T, D), F32, kind="ExternalOutput").ap()
    x_in = aps.pop("in_x")
    build(nc, {name[3:]: ap for name, ap in aps.items()}, x_in, out)
    got = run_bass_kernel_spmd(nc, [arrays], core_ids=[0])
    return got.results[0]["out"].reshape(1, T, D)
```
